# Optimizing a Trainium2 kernel written in Bass

```python
import numpy as np
import jax
import jax.numpy as jnp

def _softmax(x, axis=-1):
    return jax.nn.softmax(x, axis=axis)

def _gelu(x):
    return jax.nn.gelu(x, approximate=True)

def _silu(x):
    return jax.nn.silu(x)

def _sigmoid(x):
    return jax.nn.sigmoid(x)

def _layernorm(x, axis=-1, eps=1e-05):
    m = jnp.mean(x, axis=axis, keepdims=True)
    v = jnp.var(x, axis=axis, keepdims=True)
    return (x - m) / jnp.sqrt(v + eps)

def _scatter_add(tgt, idx, src, axis=0):
    return tgt.at[idx].add(src)

def _segment_sum(src, seg, n):
    return jax.ops.segment_sum(src, seg, n)
kernel_name = 'mk_cond_seq_d4_seqx_r2_80322d'

def setup_inputs(seed: int=0):
    np.random.seed(seed)
    _w = jnp.asarray

    def _rec_inputs():
        import jax
        import jax.numpy as jnp
        _rk = jax.random.key(seed)
        x = -7.109e-05 + 0.9999 * jax.random.normal(jax.random.fold_in(_rk, 1), (8, 512, 512), jnp.float32)
        _lenS = 512 - jax.random.randint(jax.random.fold_in(_rk, 7), (8,), 0, max(1, 512 // 4) + 1, jnp.int32)
        _lenS2 = 512 - jax.random.randint(jax.random.fold_in(_rk, 8), (8,), 0, max(1, 512 // 4) + 1, jnp.int32)
        condB_theta = jax.random.uniform(jax.random.fold_in(_rk, 11), (8,), jnp.float32, 0.0, 0.983423)
        condB_phi = jax.random.uniform(jax.random.fold_in(_rk, 12), (8,), jnp.float32, 0.0, 0.961312)
        condB_t = jax.random.uniform(jax.random.fold_in(_rk, 13), (8,), jnp.float32, 0.0, 0.983423)
        condB_safetyscore = -0.927215 + 0.920279 * jax.random.normal(jax.random.fold_in(_rk, 14), (8,), jnp.float32)
        condB_gatescore = jax.random.uniform(jax.random.fold_in(_rk, 15), (8,), jnp.float32, 0.0, 0.581427)
        return (x, condB_theta, condB_phi, condB_t, condB_safetyscore, condB_gatescore)
    x, condB_theta, condB_phi, condB_t, condB_safetyscore, condB_gatescore = _rec_inputs()

    def _L0_cond_setup():
        import jax, jax.numpy as jnp
        import numpy as np
        key = jax.random.key(seed)
        k1, k2, k3 = jax.random.split(key, 3)
        B, N, D = (16, 2048, 512)
        embeddings = jax.random.normal(k1, (B, N, D), dtype=jnp.float32)
        theta = jax.random.uniform(k2, (B,), dtype=jnp.float32)
        phi = jax.random.uniform(k3, (B,), dtype=jnp.float32)
        return {'embeddings': embeddings, 'theta': theta, 'phi': phi}
    _L0_cond_all = _L0_cond_setup()
    _L0_cond_in = {k: v for k, v in _L0_cond_all.items() if k in ()}
    del _L0_cond_all

    def _L1_cond_setup():
        import jax, jax.numpy as jnp
        import numpy as np
        import math
        B, S, D, E = (32, 512, 512, 128)

        def _layer_norm(x, gamma, beta, eps=1e-05):
            mean = jnp.mean(x, axis=(-2, -1), keepdims=True)
            var = jnp.mean(jnp.square(x - mean), axis=(-2, -1), keepdims=True)
            return (x - mean) * jax.lax.rsqrt(var + eps) * gamma + beta

        def _noise_encoding(t, channels):
            half = channels // 2
            freqs = jnp.exp(jnp.arange(half, dtype=jnp.float32) * (-math.log(10000.0) / (half - 1)))
            emb = 5000.0 * t[:, None] * freqs[None, :]
            return jnp.concatenate([jnp.sin(emb), jnp.cos(emb)], axis=1)
        key = jax.random.key(seed)
        ks = jax.random.split(key, 20)

        def lin(k, fan_in, shape):
            return jax.random.normal(k, shape, jnp.float32) / np.sqrt(fan_in)
        inp = {'x': jax.random.normal(ks[0], (B, S, D), jnp.float32), 't': jax.random.uniform(ks[1], (B,), jnp.float32), 'W1': lin(ks[2], E, (E, 4 * E)), 'b1': jnp.zeros((4 * E,), jnp.float32), 'W2': lin(ks[3], 4 * E, (4 * E, 4 * E)), 'b2': jnp.zeros((4 * E,), jnp.float32), 'Wsc': lin(ks[4], 4 * E, (4 * E, D)), 'bsc': jnp.zeros((D,), jnp.float32), 'Wsh': lin(ks[5], 4 * E, (4 * E, D)), 'bsh': jnp.zeros((D,), jnp.float32), 'gamma': jnp.ones((S, D), jnp.float32), 'beta': jnp.zeros((S, D), jnp.float32), 'W_in': lin(ks[6], D, (D, D)), 'b_in': jnp.zeros((D,), jnp.float32), 'W_out': lin(ks[7], D, (D, D)), 'b_out': jnp.zeros((D,), jnp.float32)}
        return inp
    _L1_cond_all = _L1_cond_setup()
    _L1_cond_in = {k: v for k, v in _L1_cond_all.items() if k in ('W1', 'b1', 'W2', 'b2', 'Wsc', 'bsc', 'Wsh', 'bsh', 'gamma', 'beta', 'W_in', 'b_in', 'W_out', 'b_out')}
    del _L1_cond_all

    def _L2_cond_setup():
        import jax, jax.numpy as jnp
        import numpy as np
        TEMPERATURE = 1.0
        ACT_THRESHOLD = 0.1
        MAX_ACT = 1.0
        SAFETY_KNOB = 1.0
        EPS = 1e-08

        def gram_schmidt(X):
            r = X.shape[1]
            Q = X
            for i in range(r):
                q = Q[:, i]
                q = q / (jnp.linalg.norm(q) + EPS)
                Q = Q.at[:, i].set(q)
                coeffs = q @ Q[:, i + 1:]
                Q = Q.at[:, i + 1:].add(-jnp.outer(q, coeffs))
            return Q
        key = jax.random.key(seed)
        ks = jax.random.split(key, 8)
        B, S, D, R = (8, 2048, 512, 32)
        init_std = 0.02
        return {'hidden_states': jax.random.normal(ks[0], (B, S, D), jnp.float32), 'safety_score': jax.random.normal(ks[1], (B,), jnp.float32), 'U': jax.random.normal(ks[2], (D, R), jnp.float32) * init_std, 'V': jax.random.normal(ks[3], (D, R), jnp.float32) * init_std, 'safety_bias': jnp.zeros((D,), jnp.float32), 'gate_w1': jax.random.normal(ks[4], (D // 4, D), jnp.float32) * (1.0 / np.sqrt(D)), 'gate_b1': jnp.zeros((D // 4,), jnp.float32), 'gate_w2': jax.random.normal(ks[5], (1, D // 4), jnp.float32) * (1.0 / np.sqrt(D // 4)), 'gate_b2': jnp.zeros((1,), jnp.float32), 'resp_w': jax.random.normal(ks[6], (D, R), jnp.float32) * (1.0 / np.sqrt(R)), 'resp_b': jnp.zeros((D,), jnp.float32)}
    _L2_cond_all = _L2_cond_setup()
    _L2_cond_in = {k: v for k, v in _L2_cond_all.items() if k in ('U', 'V', 'safety_bias', 'gate_w1', 'gate_b1', 'gate_w2', 'gate_b2', 'resp_w', 'resp_b')}
    del _L2_cond_all

    def _L3_cond_setup():
        import jax, jax.numpy as jnp
        import numpy as np
        D_MODEL = 512
        N_HEADS = 16
        D_HEAD = D_MODEL // N_HEADS
        D_FF = 2048
        EPS = 1e-05

        def layernorm(x, gamma, beta):
            mu = jnp.mean(x, axis=-1, keepdims=True)
            var = jnp.var(x, axis=-1, keepdims=True)
            return (x - mu) * jax.lax.rsqrt(var + EPS) * gamma + beta
        key = jax.random.key(seed)
        ks = jax.random.split(key, 16)
        B, T = (4, 1024)
        s = 1.0 / np.sqrt(D_MODEL)
        sf = 1.0 / np.sqrt(D_FF)
        return {'x': jax.random.normal(ks[0], (B, T, D_MODEL), jnp.float32), 'gate_score': jax.random.uniform(ks[1], (B,), jnp.float32), 'Wq': jax.random.normal(ks[2], (D_MODEL, D_MODEL), jnp.float32) * s, 'bq': jnp.zeros((D_MODEL,), jnp.float32), 'Wk': jax.random.normal(ks[3], (D_MODEL, D_MODEL), jnp.float32) * s, 'bk': jnp.zeros((D_MODEL,), jnp.float32), 'Wv': jax.random.normal(ks[4], (D_MODEL, D_MODEL), jnp.float32) * s, 'bv': jnp.zeros((D_MODEL,), jnp.float32), 'Wo': jax.random.normal(ks[5], (D_MODEL, D_MODEL), jnp.float32) * s, 'bo': jnp.zeros((D_MODEL,), jnp.float32), 'W1': jax.random.normal(ks[6], (D_MODEL, D_FF), jnp.float32) * s, 'b1': jnp.zeros((D_FF,), jnp.float32), 'W2': jax.random.normal(ks[7], (D_FF, D_MODEL), jnp.float32) * sf, 'b2': jnp.zeros((D_MODEL,), jnp.float32), 'gamma1': jnp.ones((D_MODEL,), jnp.float32), 'beta1': jnp.zeros((D_MODEL,), jnp.float32), 'gamma2': jnp.ones((D_MODEL,), jnp.float32), 'beta2': jnp.zeros((D_MODEL,), jnp.float32)}
    _L3_cond_all = _L3_cond_setup()
    _L3_cond_in = {k: v for k, v in _L3_cond_all.items() if k in ('Wq', 'bq', 'Wk', 'bk', 'Wv', 'bv', 'Wo', 'bo', 'W1', 'b1', 'W2', 'b2', 'gamma1', 'beta1', 'gamma2', 'beta2')}
    del _L3_cond_all
    return {'x': x, 'condB_theta': condB_theta, 'condB_phi': condB_phi, 'condB_t': condB_t, 'condB_safetyscore': condB_safetyscore, 'condB_gatescore': condB_gatescore, 'L1_cond_W1': _L1_cond_in['W1'], 'L1_cond_b1': _L1_cond_in['b1'], 'L1_cond_W2': _L1_cond_in['W2'], 'L1_cond_b2': _L1_cond_in['b2'], 'L1_cond_Wsc': _L1_cond_in['Wsc'], 'L1_cond_bsc': _L1_cond_in['bsc'], 'L1_cond_Wsh': _L1_cond_in['Wsh'], 'L1_cond_bsh': _L1_cond_in['bsh'], 'L1_cond_gamma': _L1_cond_in['gamma'], 'L1_cond_beta': _L1_cond_in['beta'], 'L1_cond_W_in': _L1_cond_in['W_in'], 'L1_cond_b_in': _L1_cond_in['b_in'], 'L1_cond_W_out': _L1_cond_in['W_out'], 'L1_cond_b_out': _L1_cond_in['b_out'], 'L2_cond_U': _L2_cond_in['U'], 'L2_cond_V': _L2_cond_in['V'], 'L2_cond_safety_bias': _L2_cond_in['safety_bias'], 'L2_cond_gate_w1': _L2_cond_in['gate_w1'], 'L2_cond_gate_b1': _L2_cond_in['gate_b1'], 'L2_cond_gate_w2': _L2_cond_in['gate_w2'], 'L2_cond_gate_b2': _L2_cond_in['gate_b2'], 'L2_cond_resp_w': _L2_cond_in['resp_w'], 'L2_cond_resp_b': _L2_cond_in['resp_b'], 'L3_cond_Wq': _L3_cond_in['Wq'], 'L3_cond_bq': _L3_cond_in['bq'], 'L3_cond_Wk': _L3_cond_in['Wk'], 'L3_cond_bk': _L3_cond_in['bk'], 'L3_cond_Wv': _L3_cond_in['Wv'], 'L3_cond_bv': _L3_cond_in['bv'], 'L3_cond_Wo': _L3_cond_in['Wo'], 'L3_cond_bo': _L3_cond_in['bo'], 'L3_cond_W1': _L3_cond_in['W1'], 'L3_cond_b1': _L3_cond_in['b1'], 'L3_cond_W2': _L3_cond_in['W2'], 'L3_cond_b2': _L3_cond_in['b2'], 'L3_cond_gamma1': _L3_cond_in['gamma1'], 'L3_cond_beta1': _L3_cond_in['beta1'], 'L3_cond_gamma2': _L3_cond_in['gamma2'], 'L3_cond_beta2': _L3_cond_in['beta2']}

def reference(x, condB_theta, condB_phi, condB_t, condB_safetyscore, condB_gatescore, L1_cond_W1, L1_cond_b1, L1_cond_W2, L1_cond_b2, L1_cond_Wsc, L1_cond_bsc, L1_cond_Wsh, L1_cond_bsh, L1_cond_gamma, L1_cond_beta, L1_cond_W_in, L1_cond_b_in, L1_cond_W_out, L1_cond_b_out, L2_cond_U, L2_cond_V, L2_cond_safety_bias, L2_cond_gate_w1, L2_cond_gate_b1, L2_cond_gate_w2, L2_cond_gate_b2, L2_cond_resp_w, L2_cond_resp_b, L3_cond_Wq, L3_cond_bq, L3_cond_Wk, L3_cond_bk, L3_cond_Wv, L3_cond_bv, L3_cond_Wo, L3_cond_bo, L3_cond_W1, L3_cond_b1, L3_cond_W2, L3_cond_b2, L3_cond_gamma1, L3_cond_beta1, L3_cond_gamma2, L3_cond_beta2):
    import jax
    import jax.numpy as jnp

    def _L0_cond_ref(embeddings, theta, phi):
        import jax, jax.numpy as jnp
        import numpy as np
        B, N, D = embeddings.shape
        e = embeddings.reshape(B, N, D // 4, 4)
        ct = jnp.cos(theta)[:, None, None]
        st = jnp.sin(theta)[:, None, None]
        cp = jnp.cos(phi)[:, None, None]
        sp = jnp.sin(phi)[:, None, None]
        x0, x1, x2, x3 = (e[..., 0], e[..., 1], e[..., 2], e[..., 3])
        out = jnp.stack([x0 * ct + x1 * st, -x0 * st + x1 * ct, x2 * cp + x3 * sp, -x2 * sp + x3 * cp], axis=-1)
        return out.reshape(B, N, D)

    def _L1_cond_ref(x, t, W1, b1, W2, b2, Wsc, bsc, Wsh, bsh, gamma, beta, W_in, b_in, W_out, b_out):
        import jax, jax.numpy as jnp
        import numpy as np
        import math
        B, S, D, E = (32, 512, 512, 128)

        def _layer_norm(x, gamma, beta, eps=1e-05):
            mean = jnp.mean(x, axis=(-2, -1), keepdims=True)
            var = jnp.mean(jnp.square(x - mean), axis=(-2, -1), keepdims=True)
            return (x - mean) * jax.lax.rsqrt(var + eps) * gamma + beta

        def _noise_encoding(t, channels):
            half = channels // 2
            freqs = jnp.exp(jnp.arange(half, dtype=jnp.float32) * (-math.log(10000.0) / (half - 1)))
            emb = 5000.0 * t[:, None] * freqs[None, :]
            return jnp.concatenate([jnp.sin(emb), jnp.cos(emb)], axis=1)
        h = _noise_encoding(t, E)
        h = jax.nn.silu(h @ W1 + b1)
        h = h @ W2 + b2
        scale = (h @ Wsc + bsc)[:, None, :]
        shift = (h @ Wsh + bsh)[:, None, :]
        out = jax.nn.silu(scale * _layer_norm(x, gamma, beta) + shift)
        out = out @ W_in + b_in
        out = jax.nn.silu(scale * _layer_norm(out, gamma, beta) + shift)
        out = out @ W_out + b_out
        return out + x

    def _L2_cond_ref(hidden_states, safety_score, U, V, safety_bias, gate_w1, gate_b1, gate_w2, gate_b2, resp_w, resp_b):
        import jax, jax.numpy as jnp
        import numpy as np
        TEMPERATURE = 1.0
        ACT_THRESHOLD = 0.1
        MAX_ACT = 1.0
        SAFETY_KNOB = 1.0
        EPS = 1e-08

        def gram_schmidt(X):
            r = X.shape[1]
            Q = X
            for i in range(r):
                q = Q[:, i]
                q = q / (jnp.linalg.norm(q) + EPS)
                Q = Q.at[:, i].set(q)
                coeffs = q @ Q[:, i + 1:]
                Q = Q.at[:, i + 1:].add(-jnp.outer(q, coeffs))
            return Q
        R = resp_w.shape[1]
        U_o = gram_schmidt(U)
        V_o = gram_schmidt(V)
        basis = U_o @ V_o.T
        pooled = hidden_states.mean(axis=1)
        h1 = jax.nn.relu(pooled @ gate_w1.T + gate_b1)
        base_act = jax.nn.sigmoid(h1 @ gate_w2.T + gate_b2)
        mod = jax.nn.sigmoid(safety_score[:, None] / TEMPERATURE)
        knob = jnp.clip(jnp.asarray(SAFETY_KNOB, hidden_states.dtype), ACT_THRESHOLD, MAX_ACT)
        strength = (base_act * mod * knob)[:, None, :]
        proj = hidden_states @ basis
        feats = proj @ basis.T[:, :R]
        response = feats @ resp_w.T + resp_b + safety_bias
        return hidden_states + strength * response

    def _L3_cond_ref(x, gate_score, Wq, bq, Wk, bk, Wv, bv, Wo, bo, W1, b1, W2, b2, gamma1, beta1, gamma2, beta2):
        import jax, jax.numpy as jnp
        import numpy as np
        D_MODEL = 512
        N_HEADS = 16
        D_HEAD = D_MODEL // N_HEADS
        D_FF = 2048
        EPS = 1e-05

        def layernorm(x, gamma, beta):
            mu = jnp.mean(x, axis=-1, keepdims=True)
            var = jnp.var(x, axis=-1, keepdims=True)
            return (x - mu) * jax.lax.rsqrt(var + EPS) * gamma + beta
        B, T, C = x.shape
        h = layernorm(x, gamma1, beta1)
        Q = (h @ Wq + bq).reshape(B, T, N_HEADS, D_HEAD).transpose(0, 2, 1, 3)
        K = (h @ Wk + bk).reshape(B, T, N_HEADS, D_HEAD).transpose(0, 2, 1, 3)
        V = (h @ Wv + bv).reshape(B, T, N_HEADS, D_HEAD).transpose(0, 2, 1, 3)
        scores = jnp.einsum('bhqd,bhkd->bhqk', Q, K) / np.sqrt(D_HEAD)
        causal = jnp.tril(jnp.ones((T, T), dtype=bool))
        scores = jnp.where(causal, scores, -jnp.inf)
        attn = jax.nn.softmax(scores, axis=-1)
        ctx = jnp.einsum('bhqk,bhkd->bhqd', attn, V)
        ctx = ctx.transpose(0, 2, 1, 3).reshape(B, T, C)
        attn_out = ctx @ Wo + bo
        x1 = x + attn_out
        h2 = layernorm(x1, gamma2, beta2)
        ff = jax.nn.gelu(h2 @ W1 + b1, approximate=False) @ W2 + b2
        x2 = x1 + ff
        g = gate_score[:, None, None]
        return x + g * (x2 - x)
    x = _L0_cond_ref(x, condB_theta, condB_phi)
    x = _L1_cond_ref(x, condB_t, L1_cond_W1, L1_cond_b1, L1_cond_W2, L1_cond_b2, L1_cond_Wsc, L1_cond_bsc, L1_cond_Wsh, L1_cond_bsh, L1_cond_gamma, L1_cond_beta, L1_cond_W_in, L1_cond_b_in, L1_cond_W_out, L1_cond_b_out)
    x = _L2_cond_ref(x, condB_safetyscore, L2_cond_U, L2_cond_V, L2_cond_safety_bias, L2_cond_gate_w1, L2_cond_gate_b1, L2_cond_gate_w2, L2_cond_gate_b2, L2_cond_resp_w, L2_cond_resp_b)
    x = _L3_cond_ref(x, condB_gatescore, L3_cond_Wq, L3_cond_bq, L3_cond_Wk, L3_cond_bk, L3_cond_Wv, L3_cond_bv, L3_cond_Wo, L3_cond_bo, L3_cond_W1, L3_cond_b1, L3_cond_W2, L3_cond_b2, L3_cond_gamma1, L3_cond_beta1, L3_cond_gamma2, L3_cond_beta2)
    return x

_drawn_inputs = setup_inputs


def setup_inputs(seed=0):
    import zlib

    import numpy as np

    out = dict(_drawn_inputs(seed))
    spreads = {'L1_cond_b1': (0.0, 0.1),
     'L1_cond_b2': (0.0, 0.1),
     'L1_cond_bsc': (0.0, 0.1),
     'L1_cond_bsh': (0.0, 0.1),
     'L1_cond_gamma': (1.0, 0.2),
     'L1_cond_beta': (0.0, 0.273),
     'L1_cond_b_in': (0.0, 0.1),
     'L1_cond_b_out': (0.0, 0.1),
     'L2_cond_safety_bias': (0.0, 0.473),
     'L2_cond_gate_b1': (0.0, 0.8),
     'L2_cond_resp_b': (0.0, 0.43),
     'L3_cond_bq': (0.0, 0.8),
     'L3_cond_bk': (0.0, 0.8),
     'L3_cond_bv': (0.0, 0.1),
     'L3_cond_bo': (0.0, 0.1),
     'L3_cond_b1': (0.0, 0.395),
     'L3_cond_b2': (0.0, 0.1),
     'L3_cond_gamma1': (1.0, 0.2),
     'L3_cond_beta1': (0.0, 0.1),
     'L3_cond_gamma2': (1.0, 0.2),
     'L3_cond_beta2': (0.0, 0.382)}
    factors = {'L2_cond_V': 8.0, 'L2_cond_gate_w1': 8.0, 'L2_cond_gate_w2': 8.0}
    for name, (base, spread) in spreads.items():
        noise = np.random.default_rng([zlib.crc32(name.encode()), seed]).standard_normal(out[name].shape)
        drawn = base * np.exp(spread * noise) if base else spread * noise
        out[name] = jnp.asarray(drawn.astype(out[name].dtype))
    for name, factor in factors.items():
        out[name] = (out[name] * factor).astype(out[name].dtype)
    return out
```

```python
from contextlib import ExitStack

import numpy as np

import concourse.bass as bass
import concourse.mybir as mybir
from concourse.alu_op_type import AluOpType as ALU

F32 = mybir.dt.float32
F32R = mybir.dt.float32r
ACT = mybir.ActivationFunctionType
RADD = bass.bass_isa.ReduceOp.add

P = 128
B, S, D = 8, 512, 512
J = D // P
T = S // P
H, DH = 16, 32
HG = P // DH
G = H // HG
R = 32
FF = 2048
M = FF // P
PAIRS = B // 2

LN_EPS = 1e-5
GS_EPS = 1e-8
MASKED = -1e30
INV_SQRT_DH = float(1.0 / np.sqrt(DH))

TWO_PI = 2.0 * np.pi
TWO_PI_1 = 6.28125
TWO_PI_2 = float(np.float32(np.round((TWO_PI - TWO_PI_1) * 2.0**21) / 2.0**21))
TWO_PI_3 = float(TWO_PI - TWO_PI_1 - TWO_PI_2)
ROUND = 12582912.0
SIN_MAX = 3.1415925

SMALLS = [
    ("t", B), ("theta", B), ("phi", B), ("safety", B), ("gate", B), ("freq", 1),
    ("quarter", 5 * B), ("half_pi", 5 * B), ("t_b1", J), ("t_b2", J), ("b_sc", J), ("b_sh", J),
    ("b_in", J), ("b_out", J), ("gate_b1", 1), ("gate_w2", 1), ("gate_b2", 1), ("safety_bias", J),
    ("resp_b", J), ("bq", G), ("bk", G), ("bv", G), ("bo", J), ("b1", M), ("b2", J),
    ("gamma1", J), ("beta1", J), ("gamma2", J), ("beta2", J), ("row", 1),
]
SMALL_AT, _n = {}, 0
for _name, _width in SMALLS:
    SMALL_AT[_name] = (_n, _width)
    _n += _width
N_SMALLS = _n

CT, ST_, NST, CP, SP_, NSP, SCALE, SHIFT = 0, 1, 2, 3, 4, 5, 6, 6 + J
N_PA = 6 + 2 * J
STRENGTH, RBIAS, GATE, GB2 = 0, 1, 1 + J, 2 + J
N_PB = 2 + 2 * J


def small(smalls, name, col=None):
    at, width = SMALL_AT[name]
    return smalls[:, at:at + width] if col is None else smalls[:, at + col:at + col + 1]


def sample_at(ap, b):
    return ap[bass.ds(b, 1), :, :, :].rearrange("b p j t -> (b p) j t")


def three_pass(pe, out, hi_lo_pairs, start=True, stop=True):
    n = len(hi_lo_pairs)
    for k, (w_hi, w_lo, x_hi, x_lo) in enumerate(hi_lo_pairs):
        pe.matmul(out, w_hi, x_hi, start=start and k == 0, stop=False)
        pe.matmul(out, w_hi, x_lo, start=False, stop=False)
        last = pe.matmul(out, w_lo, x_hi, start=False, stop=stop and k == n - 1)
    return last


def wait_apart(eng, sem, value, waited):
    eng.wait_ge(sem, value)
    eng.sem_inc(waited, 1)


def clear_semaphores(nc, sems):
    with nc.Block() as block:
        @block.gpsimd
        def _(pool):
            for sem in sems:
                pool.sem_clear(sem)
    for sem in sems:
        nc.release_semaphore(sem)


def setup_phase(nc, io, keep, psum):
    smalls, ident, pa = keep["smalls"], keep["ident"], keep["pa"]
    with ExitStack() as ctx:
        def sb(name, shape, dt=F32):
            return ctx.enter_context(nc.sbuf_tensor(name, shape, dt))

        sems = []

        def sem(name):
            sems.append(nc.alloc_semaphore(name))
            return sems[-1]

        ctx.callback(clear_semaphores, nc, sems)
        angle = sb("angle", [P, 5 * B])
        turns = sb("turns", [P, 5 * B])
        sines = sb("sines", [P, 5 * B])
        wt1 = sb("wt1", [P, J, P])
        wt2 = sb("wt2", [P, J, J, P])
        wsc = sb("wsc", [P, J, J, P])
        wsh = sb("wsh", [P, J, J, P])
        h1 = sb("t_h1", [P, J, B])
        h2 = sb("t_h2", [P, J, B])
        raw_in = sb("raw_in", [P, J, D])
        raw_out = sb("raw_out", [P, J, D])
        rows = sb("gs_rows", [2 * R, S])
        prod = sb("gs_prod", [2 * R, S])
        pick_index = sb("gs_pick_index", [2 * R, 2 * R])
        pick = sb("gs_pick", [2 * R, 2 * R])
        step_no = sb("gs_step", [2 * R, 1])
        later = sb("gs_later", [2 * R, 1])
        dots = sb("gs_dots", [2 * R, 1])
        norm = sb("gs_norm", [2 * R, 1])
        inv = sb("gs_inv", [2 * R, 1])
        coef = sb("gs_coef", [2 * R, 1])
        uv = sb("gs_uv", [P, J, 2 * R])
        u_head = sb("u_head", [R, R])
        gram = sb("gram", [R, R])
        mix = sb("mix", [R, R])
        resp_w = sb("resp_w", [R, D])

        small_ld = sem("small_ld")
        tw_ld = sem("tw_ld")
        win_ld = sem("win_ld")
        gs_ld = sem("gs_ld")
        rw_ld = sem("rw_ld")
        ident_made = sem("ident_made")
        angles = sem("angles")
        sines_made = sem("sines_made")
        t_full = sem("t_full")
        t_done = sem("t_done")
        pa_made = sem("pa_made")
        split_hi = sem("split_hi")
        split_lo = sem("split_lo")
        gs_ready = sem("gs_ready")
        gs_row = sem("gs_row")
        gs_dots = sem("gs_dots_done")
        gs_sq = sem("gs_sq")
        gs_norm = sem("gs_norm_done")
        gs_small = sem("gs_small")
        fin_pe = sem("fin_pe")
        fin_dve = sem("fin_dve")
        fin_act = sem("fin_act")

        waited = sem("gs_waited")

        block = ctx.enter_context(nc.Block())

        @block.sync
        def _(sp):
            sp.dma_start(smalls[:], io["smalls"]).then_inc(small_ld, 16)
            sp.dma_start(rows[:], io["uv_rows"]).then_inc(gs_ld, 16)
            sp.dma_start(pick_index[:], io["pick_index"]).then_inc(gs_ld, 16)
            sp.dma_start(wt1[:], io["t_w1"]).then_inc(tw_ld, 16)
            sp.dma_start(wt2[:], io["t_w2"]).then_inc(tw_ld, 16)
            sp.dma_start(wsc[:], io["w_sc"]).then_inc(tw_ld, 16)
            sp.dma_start(wsh[:], io["w_sh"]).then_inc(tw_ld, 16)
            sp.dma_start(raw_in[:], io["w_in"]).then_inc(win_ld, 16)
            sp.dma_start(raw_out[:], io["w_out"]).then_inc(win_ld, 16)
            sp.dma_start(keep["gamma_t"][:], io["gamma_t"]).then_inc(rw_ld, 16)
            sp.dma_start(keep["beta_t"][:], io["beta_t"]).then_inc(rw_ld, 16)
            sp.dma_start(resp_w[:], io["resp_w"]).then_inc(rw_ld, 16)

        @block.gpsimd
        def _(pool):
            pool.memset(ident[:], 0.0).then_inc(ident_made, 1)
            pool.memset(keep["ones"][:], 1.0)
            pool.memset(keep["minus_half"][:], -0.5)
            pool.memset(step_no[:], 0.0).then_inc(ident_made, 1)
            pool.wait_ge(ident_made, 2)
            pool.affine_select(out=ident[:], in_=ident[:], compare_op=ALU.not_equal, fill=1.0, base=0,
                               pattern=[[-1, P]], channel_multiplier=1).then_inc(ident_made, 1)

        @block.vector
        def _(dve):
            done = [0]

            def chain(ins):
                done[0] += 1
                ins.then_inc(angles, 1)
                dve.wait_ge(angles, done[0])

            dve.wait_ge(small_ld, 16)
            dve.tensor_scalar(angle[:, 0:B], small(smalls, "t"), 5000.0, small(smalls, "freq"), ALU.mult, ALU.mult)
            dve.tensor_copy(angle[:, B:2 * B], small(smalls, "theta"))
            dve.tensor_copy(angle[:, 2 * B:3 * B], small(smalls, "theta"))
            dve.tensor_copy(angle[:, 3 * B:4 * B], small(smalls, "phi"))
            chain(dve.tensor_copy(angle[:, 4 * B:5 * B], small(smalls, "phi")))
            chain(dve.scalar_tensor_tensor(turns[:], angle[:], 1.0 / TWO_PI, small(smalls, "quarter"), ALU.mult, ALU.add))
            chain(dve.tensor_scalar(turns[:], turns[:], ROUND, None, ALU.add))
            chain(dve.tensor_scalar(turns[:], turns[:], -ROUND, None, ALU.add))
            for part in (TWO_PI_1, TWO_PI_2, TWO_PI_3):
                chain(dve.scalar_tensor_tensor(angle[:], turns[:], -part, angle[:], ALU.mult, ALU.add))
            chain(dve.tensor_tensor(angle[:], angle[:], small(smalls, "half_pi"), ALU.add))
            chain(dve.tensor_scalar(angle[:], angle[:], SIN_MAX, -SIN_MAX, ALU.min, ALU.max))
            dve.wait_ge(sines_made, 1)
            sine = lambda k: sines[:, k * B:(k + 1) * B]
            dve.tensor_copy(pa[:, :, ST_], sine(1))
            dve.tensor_scalar(pa[:, :, NST], sine(1), -1.0, None, ALU.mult)
            dve.tensor_copy(pa[:, :, CT], sine(2))
            dve.tensor_copy(pa[:, :, SP_], sine(3))
            dve.tensor_scalar(pa[:, :, NSP], sine(3), -1.0, None, ALU.mult)
            dve.tensor_copy(pa[:, :, CP], sine(4)).then_inc(pa_made, 1)
            dve.wait_ge(win_ld, 32)
            for n, (raw, w) in enumerate(((raw_in, "w_in"), (raw_out, "w_out"))):
                for j in range(J):
                    dve.wait_ge(split_hi, J * n + j + 1)
                    dve.tensor_tensor(keep[w + "_lo"][:, j, :, :].rearrange("p a k -> p (a k)"), raw[:, j, :],
                                      keep[w + "_hi"][:, j, :, :].rearrange("p a k -> p (a k)").bitcast(F32),
                                      ALU.subtract).then_inc(split_lo, 1)
            dve.wait_ge(gs_ld, 32)
            dve.wait_ge(ident_made, 3)
            dve.tensor_scalar(pick[:], pick_index[:], step_no[:, 0:1], None, ALU.is_equal).then_inc(gs_ready, 1)
            with dve.Fori(0, R) as i:
                dve.wait_ge(gs_ready, i + 1)
                dve.tensor_scalar(later[:], small(smalls, "row")[0:2 * R, :], step_no[:, 0:1], -1.0, ALU.is_gt,
                                  ALU.mult).then_inc(gs_small, 1)
                dve.wait_ge(gs_small, i * 7 + 1)
                dve.tensor_scalar(step_no[:], step_no[:], 1.0, None, ALU.add).then_inc(gs_small, 1)
                dve.wait_ge(gs_row, i + 1)
                dve.tensor_tensor_reduce(prod[:], psum[0:2 * R, 0, :], rows[:], 1.0, 0.0, ALU.mult, ALU.add,
                                         dots[:]).then_inc(gs_dots, 1)
                dve.wait_ge(gs_norm, i + 1)
                dve.tensor_scalar(norm[:], norm[:], GS_EPS, None, ALU.add).then_inc(gs_small, 1)
                dve.wait_ge(gs_small, i * 7 + 3)
                dve.reciprocal(inv[:], norm[:]).then_inc(gs_small, 1)
                dve.wait_ge(gs_small, i * 7 + 4)
                dve.tensor_scalar(coef[:], dots[:], inv[:, 0:1], inv[:, 0:1], ALU.mult, ALU.mult).then_inc(gs_small, 1)
                dve.wait_ge(gs_small, i * 7 + 5)
                dve.tensor_scalar(coef[:], coef[:], later[:, 0:1], None, ALU.mult).then_inc(gs_small, 1)
                dve.wait_ge(gs_small, i * 7 + 6)
                dve.scalar_tensor_tensor(rows[:], psum[0:2 * R, 0, :], coef[:, 0:1], rows[:], ALU.mult,
                                         ALU.add).then_inc(gs_small, 1)
                dve.wait_ge(gs_small, i * 7 + 7)
                dve.tensor_scalar(pick[:], pick_index[:], step_no[:, 0:1], None, ALU.is_equal).then_inc(gs_ready, 1)
            dve.tensor_tensor_reduce(prod[:], rows[:], rows[:], 1.0, 0.0, ALU.mult, ALU.add, dots[:]).then_inc(fin_dve, 1)
            dve.wait_ge(fin_act, 1)
            dve.tensor_scalar(norm[:], norm[:], GS_EPS, None, ALU.add).then_inc(fin_dve, 1)
            dve.wait_ge(fin_dve, 2)
            dve.reciprocal(inv[:], norm[:]).then_inc(fin_dve, 1)
            dve.wait_ge(fin_dve, 3)
            dve.tensor_scalar(rows[:], rows[:], inv[:, 0:1], None, ALU.mult).then_inc(fin_dve, 1)
            dve.wait_ge(fin_dve, 4)
            dve.tensor_copy(u_head[:].rearrange("r (k j) -> r k j", j=J),
                            rows[0:R, :].rearrange("r (j k) -> r k j", j=J)[:, 0:R // J, :]).then_inc(fin_dve, 1)
            dve.wait_ge(fin_pe, 1)
            dve.tensor_copy(uv[:].rearrange("p j r -> p (j r)"), psum[:, 0, 0:J * 2 * R]).then_inc(fin_dve, 1)
            dve.wait_ge(fin_dve, 6)
            dve.tensor_copy(keep["uo"][:], uv[:, :, 0:R]).then_inc(fin_dve, 1)
            dve.wait_ge(fin_pe, 2)
            dve.tensor_copy(gram[:], psum[0:R, 1, 0:R]).then_inc(fin_dve, 1)
            dve.wait_ge(fin_pe, 3)
            dve.tensor_copy(mix[:], psum[0:R, 2, 0:R]).then_inc(fin_dve, 1)
            dve.wait_ge(fin_pe, 4)
            dve.tensor_copy(keep["steer"][:].rearrange("r j k -> r (j k)"), psum[0:R, 3, :]).then_inc(fin_dve, 1)

        @block.scalar
        def _(act):
            act.wait_ge(angles, 9)
            act.activation(sines[:], angle[:], ACT.Sin).then_inc(sines_made, 1)
            act.wait_ge(t_full, 1)
            for j in range(J):
                ins = act.activation(h1[:, j, :], psum[:, 4, j * B:(j + 1) * B], ACT.Silu, bias=small(smalls, "t_b1", j))
            ins.then_inc(t_done, 1)
            act.wait_ge(t_full, 2)
            for j in range(J):
                ins = act.activation(h2[:, j, :], psum[:, 5, j * B:(j + 1) * B], ACT.Identity, bias=small(smalls, "t_b2", j))
            ins.then_inc(t_done, 1)
            act.wait_ge(t_full, 3)
            for j in range(J):
                act.activation(pa[:, :, SCALE + j], psum[:, 6, j * B:(j + 1) * B], ACT.Identity, bias=small(smalls, "b_sc", j))
                ins = act.activation(pa[:, :, SHIFT + j], psum[:, 7, j * B:(j + 1) * B], ACT.Identity,
                                     bias=small(smalls, "b_sh", j))
            ins.then_inc(pa_made, 1)
            act.wait_ge(win_ld, 32)
            for raw, w in ((raw_in, "w_in"), (raw_out, "w_out")):
                for j in range(J):
                    act.activation(keep[w + "_hi"][:, j, :, :].rearrange("p a k -> p (a k)"), raw[:, j, :],
                                   ACT.Copy).then_inc(split_hi, 1)
            with act.Fori(0, R) as i:
                act.wait_ge(gs_sq, i + 1)
                act.activation(norm[:], psum[0:2 * R, 1, 0:1], ACT.Sqrt).then_inc(gs_norm, 1)
            act.wait_ge(fin_dve, 1)
            act.activation(norm[:], dots[:], ACT.Sqrt).then_inc(fin_act, 1)

        @block.tensor
        def _(pe):
            pe.wait_ge(tw_ld, 64)
            pe.wait_ge(sines_made, 1)
            for j in range(J):
                last = pe.matmul(psum[:, 4, j * B:(j + 1) * B], wt1[:, j, :], sines[:, 0:B], start=True, stop=True)
            last.then_inc(t_full, 1)
            pe.wait_ge(t_done, 1)
            for jo in range(J):
                for j in range(J):
                    last = pe.matmul(psum[:, 5, jo * B:(jo + 1) * B], wt2[:, j, jo, :], h1[:, j, :], start=(j == 0), stop=(j == J - 1))
            last.then_inc(t_full, 1)
            pe.wait_ge(t_done, 2)
            for k, w in ((6, wsc), (7, wsh)):
                for jo in range(J):
                    for j in range(J):
                        last = pe.matmul(psum[:, k, jo * B:(jo + 1) * B], w[:, j, jo, :], h2[:, j, :], start=(j == 0), stop=(j == J - 1))
            last.then_inc(t_full, 1)
            with pe.Fori(0, R) as i:
                wait_apart(pe, gs_ready, i + 1, waited)
                pe.matmul(psum[0:2 * R, 0, :], pick[:], rows[:], start=True, stop=True).then_inc(gs_row, 1)
                wait_apart(pe, gs_dots, i + 1, waited)
                pe.matmul(psum[0:2 * R, 1, 0:1], pick[:], dots[:], start=True, stop=True).then_inc(gs_sq, 1)
            pe.wait_ge(fin_dve, 5)
            pe.wait_ge(ident_made, 3)
            for j in range(J):
                last = pe.transpose(psum[:, 0, j * 2 * R:(j + 1) * 2 * R], rows[:, j * P:(j + 1) * P], ident[0:2 * R, 0:2 * R])
            last.then_inc(fin_pe, 1)
            pe.wait_ge(fin_dve, 7)
            for j in range(J):
                last = pe.matmul(psum[0:R, 1, 0:R], uv[:, j, R:2 * R], uv[:, j, R:2 * R], start=(j == 0), stop=(j == J - 1))
            last.then_inc(fin_pe, 1)
            pe.wait_ge(fin_dve, 8)
            pe.matmul(psum[0:R, 2, 0:R], u_head[:], gram[:], start=True, stop=True).then_inc(fin_pe, 1)
            pe.wait_ge(fin_dve, 9)
            pe.wait_ge(rw_ld, 48)
            pe.matmul(psum[0:R, 3, :], mix[:], resp_w[:], start=True, stop=True).then_inc(fin_pe, 1)


def first_phase(nc, io, keep, psum):
    pa, smalls = keep["pa"], keep["smalls"]
    with ExitStack() as ctx:
        def sb(name, shape, dt=F32):
            return [ctx.enter_context(nc.sbuf_tensor(f"{name}{s}", shape, dt)) for s in range(2)]

        sems = []

        def sem(name):
            pair = [nc.alloc_semaphore(f"{name}{s}") for s in range(2)]
            sems.extend(pair)
            return pair

        ctx.callback(clear_semaphores, nc, sems)

        x_in = sb("a_x", [P, J, S])
        rot = sb("a_rot", [P, J, S])
        z = sb("a_z", [P, J, S])
        hi = sb("a_hi", [P, J, S], F32R)
        lo = sb("a_lo", [P, J, S], F32R)
        res = sb("a_res", [P, J, S])
        cur = sb("a_cur", [P, N_PA])
        stats = sb("a_stats", [P, J, 6])
        mv = sb("a_mv", [P, 2])
        total = sb("a_total", [P, 1])
        spread = sb("a_spread", [P, 1])
        spread_sum = sb("a_spread_sum", [P, 1])
        away = sb("a_away", [P, 1])
        inv = sb("a_inv", [P, 1])
        nmean = sb("a_nmean", [P, 1])
        tok_sum = sb("a_tok_sum", [P, J])

        x_ld = sem("a_x_ld")
        x_used = sem("a_x_used")
        cur_set = sem("a_cur_set")
        cross = sem("a_cross")
        rotated = sem("a_rotated")
        stat = sem("a_stat")
        part_mv = sem("a_part_mv")
        mean_sum = sem("a_mean_sum")
        away_set = sem("a_away_set")
        spread_set = sem("a_spread_set")
        var_sum = sem("a_var_sum")
        var_set = sem("a_var_set")
        inv_set = sem("a_inv_set")
        nmean_set = sem("a_nmean_set")
        normed = sem("a_normed")
        scaled = sem("a_scaled")
        shifted = sem("a_shifted")
        silu = sem("a_silu")
        hi_set = sem("a_hi_set")
        lo_set = sem("a_lo_set")
        product = sem("a_product")
        biased = sem("a_biased")
        result = sem("a_result")
        pooled_set = sem("a_pooled_set")
        stored = sem("a_stored")

        dve_waited = ctx.enter_context(nc.semaphore("a_dve_waited"))
        pool_waited = ctx.enter_context(nc.semaphore("a_pool_waited"))

        x_dram, x1_dram = io["x"], io["x1"]
        bank = lambda s, j: psum[:, 4 * s + j, :]
        block = ctx.enter_context(nc.Block())

        @block.sync
        def _(sp):
            def load(s, q):
                sp.dma_start(x_in[s][:], sample_at(x_dram, 2 * q + s)).then_inc(x_ld[s], 16)

            def store(s, q):
                sp.wait_ge(result[s], 4 * q + 4)
                sp.dma_start(sample_at(x1_dram, 2 * q + s), res[s][:]).then_inc(stored[s], 16)

            for s in range(2):
                sp.sem_inc(stored[s], 16)
                load(s, 0)
            with sp.Fori(0, PAIRS - 1) as q:
                for s in range(2):
                    sp.wait_ge(x_used[s], q + 1)
                    load(s, q + 1)
                for s in range(2):
                    store(s, q)
            for s in range(2):
                store(s, PAIRS - 1)
            for s in range(2):
                sp.wait_ge(stored[s], 16 * (PAIRS + 1))

        @block.gpsimd
        def _(pool):
            def sums(s, q, st):
                n = 2 * q + st + 1
                wait_apart(pool, part_mv[s], n, pool_waited)
                pool.partition_all_reduce(total[s][:], mv[s][:, 0:1], P, RADD).then_inc(mean_sum[s], 1)
                wait_apart(pool, spread_set[s], n, pool_waited)
                pool.partition_all_reduce(spread_sum[s][:], spread[s][:], P, RADD).then_inc(var_sum[s], 1)
                wait_apart(pool, var_sum[s], n, pool_waited)
                pool.tensor_scalar(spread_sum[s][:], spread_sum[s][:], 1.0 / P, LN_EPS, ALU.mult, ALU.add).then_inc(var_set[s], 1)
                wait_apart(pool, var_set[s], n, pool_waited)
                pool.tensor_tensor(inv[s][:], spread_sum[s][:], keep["minus_half"][:, 0:1], ALU.pow).then_inc(inv_set[s], 1)
                for j in range(J):
                    pool.wait_ge(scaled[s], 8 * q + 4 * st + j + 1)
                    pool.tensor_tensor(z[s][:, j, :], z[s][:, j, :], keep["beta_t"][:, j, :],
                                       ALU.add).then_inc(shifted[s], 1)

            for s in range(2):
                sums(s, 0, 0)
            with pool.Fori(0, PAIRS - 1) as q:
                for s in range(2):
                    sums(s, q, 1)
                for s in range(2):
                    sums(s, q + 1, 0)
            for s in range(2):
                sums(s, PAIRS - 1, 1)

        @block.vector
        def _(dve):
            def rotate(s, q):
                b = 2 * q + s
                dve.tensor_copy(cur[s][:], pa[:, bass.ds(b, 1), :].rearrange("p b n -> p (b n)")).then_inc(cur_set[s], 1)
                dve.wait_ge(x_ld[s], 16 * (q + 1))
                dve.wait_ge(cur_set[s], q + 1)
                for j in range(J):
                    dve.wait_ge(cross[s], 4 * q + j + 1)
                    c = CT if j < 2 else CP
                    last = dve.scalar_tensor_tensor(rot[s][:, j, :], x_in[s][:, j, :], cur[s][:, c:c + 1], z[s][:, j, :],
                                                    ALU.mult, ALU.add).then_inc(rotated[s], 1)
                dve.wait_ge(rotated[s], 4 * q + 4)
                dve.sem_inc(x_used[s], 1)

            def norm(s, q, st):
                n = 2 * q + st + 1
                src = rot[s] if st == 0 else z[s]
                for j in range(J):
                    if st:
                        dve.wait_ge(biased[s], 4 * q + j + 1)
                    dve.bn_stats(stats[s][:, j, :], src[:, j, :]).then_inc(stat[s], 1)
                wait_apart(dve, stat[s], 4 * n, dve_waited)
                dve.bn_aggr(mv[s][:], stats[s][:].rearrange("p j n -> p (j n)")).then_inc(part_mv[s], 1)
                dve.wait_ge(mean_sum[s], n)
                dve.scalar_tensor_tensor(away[s][:], total[s][:], -1.0 / P, mv[s][:, 0:1], ALU.mult,
                                         ALU.add).then_inc(away_set[s], 1)
                dve.wait_ge(away_set[s], n)
                dve.scalar_tensor_tensor(spread[s][:], away[s][:], away[s][:, 0:1], mv[s][:, 1:2], ALU.mult,
                                         ALU.add).then_inc(spread_set[s], 1)
                dve.wait_ge(inv_set[s], n)
                dve.scalar_tensor_tensor(nmean[s][:], total[s][:], -1.0 / P, inv[s][:], ALU.mult,
                                         ALU.mult).then_inc(nmean_set[s], 1)
                for j in range(J):
                    dve.wait_ge(normed[s], 8 * q + 4 * st + j + 1)
                    dve.tensor_tensor(z[s][:, j, :], z[s][:, j, :], keep["gamma_t"][:, j, :],
                                      ALU.mult).then_inc(scaled[s], 1)
                for j in range(J):
                    dve.wait_ge(hi_set[s], 8 * q + 4 * st + j + 1)
                    dve.tensor_tensor(lo[s][:, j, :], z[s][:, j, :], hi[s][:, j, :].bitcast(F32),
                                      ALU.subtract).then_inc(lo_set[s], 1)

            def finish(s, q):
                b = 2 * q + s
                dve.wait_ge(stored[s], 16 * (q + 1))
                for j in range(J):
                    dve.wait_ge(product[s], 8 * q + 4 + j + 1)
                    dve.scalar_tensor_tensor(res[s][:, j, :], bank(s, j), small(smalls, "b_out", j), rot[s][:, j, :],
                                             ALU.add, ALU.add, accum_out=tok_sum[s][:, j:j + 1]).then_inc(result[s], 1)
                dve.wait_ge(result[s], 4 * q + 4)
                dve.tensor_copy(keep["pooled"][:, bass.ds(b, 1), :].rearrange("p b j -> p (b j)"),
                                tok_sum[s][:]).then_inc(pooled_set[s], 1)

            for s in range(2):
                rotate(s, 0)
                norm(s, 0, 0)
            with dve.Fori(0, PAIRS - 1) as q:
                norm(0, q, 1)
                norm(1, q, 1)
                for s in range(2):
                    finish(s, q)
                    rotate(s, q + 1)
                    norm(s, q + 1, 0)
            for s in range(2):
                norm(s, PAIRS - 1, 1)
            for s in range(2):
                finish(s, PAIRS - 1)

        @block.scalar
        def _(act):
            def crosses(s, q):
                act.wait_ge(x_ld[s], 16 * (q + 1))
                act.wait_ge(cur_set[s], q + 1)
                for j, c in enumerate((ST_, NST, SP_, NSP)):
                    act.activation(z[s][:, j, :], x_in[s][:, j ^ 1, :], ACT.Copy,
                                   scale=cur[s][:, c:c + 1]).then_inc(cross[s], 1)

            def norm(s, q, st):
                n = 2 * q + st + 1
                at = 8 * q + 4 * st
                src = rot[s] if st == 0 else z[s]
                if st:
                    for j in range(J):
                        act.wait_ge(product[s], 8 * q + j + 1)
                        act.activation(z[s][:, j, :], bank(s, j), ACT.Identity,
                                       bias=small(smalls, "b_in", j)).then_inc(biased[s], 1)
                act.wait_ge(nmean_set[s], n)
                for j in range(J):
                    act.activation(z[s][:, j, :], src[:, j, :], ACT.Identity, bias=nmean[s][:, 0:1],
                                   scale=inv[s][:, 0:1]).then_inc(normed[s], 1)
                for j in range(J):
                    act.wait_ge(shifted[s], at + j + 1)
                    act.activation(z[s][:, j, :], z[s][:, j, :], ACT.Silu, bias=cur[s][:, SHIFT + j:SHIFT + j + 1],
                                   scale=cur[s][:, SCALE + j:SCALE + j + 1]).then_inc(silu[s], 1)
                for j in range(J):
                    act.wait_ge(silu[s], at + j + 1)
                    act.activation(hi[s][:, j, :], z[s][:, j, :], ACT.Copy).then_inc(hi_set[s], 1)

            for s in range(2):
                crosses(s, 0)
                norm(s, 0, 0)
            with act.Fori(0, PAIRS - 1) as q:
                norm(0, q, 1)
                norm(1, q, 1)
                for s in range(2):
                    act.wait_ge(product[s], 8 * q + 8)
                    crosses(s, q + 1)
                    norm(s, q + 1, 0)
            for s in range(2):
                norm(s, PAIRS - 1, 1)

        @block.tensor
        def _(pe):
            def multiply(s, q, st, w):
                w_hi, w_lo = keep[w + "_hi"], keep[w + "_lo"]
                pe.wait_ge(lo_set[s], 8 * q + 4 * st + J)
                for jo in range(J):
                    three_pass(pe, bank(s, jo), [(w_hi[:, j, jo, :], w_lo[:, j, jo, :], hi[s][:, j, :], lo[s][:, j, :])
                                                 for j in range(J)]).then_inc(product[s], 1)

            with pe.Fori(0, PAIRS) as q:
                for s in range(2):
                    multiply(s, q, 0, "w_in")
                for s in range(2):
                    multiply(s, q, 1, "w_out")


class Ring:

    def __init__(self, start, names, per_round):
        self.at = {name: ((start + k) % 2, (start + k) // 2) for k, name in enumerate(names)}
        self.per_round = per_round

    def bank(self, name):
        return self.at[name][0]

    def full(self, name, n=0):
        return n * self.per_round + self.at[name][1] + 1

    def free(self, name, n=0):
        return n * self.per_round + self.at[name][1]


def before_names(s):
    return ([(s, "p")] + [(s, "resp", j) for j in range(J)], [(s, "tin", t) for t in range(T)],
            [(s, "tback", j) for j in range(J)])


def sample_names(s, ahead):
    p_resp, tin, tback = before_names(1 - s) if ahead else ([], [], [])
    qk = [[(s, "q", g), (s, "k", g)] for g in range(G)]
    return (qk[0] + qk[1] + p_resp[:1] + [(s, "v", t) for t in range(T)] + qk[2] + p_resp[1:] + qk[3] + tin + tback
            + [(s, "wo", j) for j in range(J)])


U_TILES = ((T - 1,), (T - 2, 0), (1,))
UNITS = HG * len(U_TILES)
S_USES = UNITS + 1


def attention_phase(nc, io, keep, psum):
    smalls, ident, pb, pooled = keep["smalls"], keep["ident"], keep["pb"], keep["pooled"]
    with ExitStack() as ctx:
        def sb(name, shape, dt=F32):
            return ctx.enter_context(nc.sbuf_tensor("b_" + name, shape, dt))

        def sem(name):
            return ctx.enter_context(nc.semaphore("b_" + name))

        w_hi = {n: sb(n + "_hi", [P, J, D], F32R) for n in ("wq", "wk", "wv", "wo")}
        w_lo = {n: sb(n + "_lo", [P, J, D], F32R) for n in ("wq", "wk", "wv", "wo")}
        xb = [sb(f"x{s}", [P, J, S]) for s in range(2)]
        tok = sb("tok", [P, J, S])
        xh = sb("xh", [P, J, S], F32R)
        xl = sb("xl", [P, J, S], F32R)
        v = sb("v", [P, T, D])
        qk4 = sb("qk4", [P, 4, S], F32R)
        stack = [sb(f"stack{n}", [P, 2, S], F32R) for n in range(2 * HG)]
        pt = [sb(f"pt{n}", [P, HG, S]) for n in range(2)]
        ctxs = sb("ctxs", [P, S])
        sums = sb("sums", [P, S])
        ch = sb("ch", [P, G, S], F32R)
        cl = sb("cl", [P, G, S], F32R)
        psb = sb("p", [R, S])
        mr = [sb(f"mr{n}", [2 * HG, S], F32R) for n in range(2)]
        mask = sb("mask", [P, S])
        mx = sb("mx", [P, T, HG])
        nm = sb("nm", [P, T, HG, 2], F32R)
        st = sb("st", [P, T, 6])
        mv = sb("mv", [P, T, 2])
        var = sb("var", [P, T])
        rstd = sb("rstd", [P, T])
        cur = [sb(f"cur{s}", [P, N_PB]) for s in range(2)]
        gate_w1 = sb("gate_w1", [P, J, P])
        gate_h = sb("gate_h", [P, B])
        gate_w2 = sb("gate_w2", [P, P])
        strength = sb("strength", [P, B])
        mod = sb("mod", [P, B])
        rbias = sb("rbias", [P, J])
        bias = sb("bias", [P, 3, G])

        raw_ld = [sem(f"raw_ld{n}") for n in range(4)]
        gw_ld = sem("gw_ld")
        w_hi_set, w_lo_set = sem("w_hi_set"), sem("w_lo_set")
        gate_full, gate_act, gate_dve = sem("gate_full"), sem("gate_act"), sem("gate_dve")
        beta_full, beta_set = sem("beta_full"), sem("beta_set")
        rows_made, mask_made = sem("rows_made"), sem("mask_made")
        x_ld = [sem(f"x_ld{s}") for s in range(2)]
        mid_st = [sem(f"mid_st{s}") for s in range(2)]
        base_st = sem("base_st")
        pj_full = [sem(f"pj_full{k}") for k in range(2)]
        pj_free = [sem(f"pj_free{k}") for k in range(2)]
        s_full = [sem(f"s_full{k}") for k in range(2)]
        s_free = [sem(f"s_free{k}") for k in range(2)]
        e_full = [sem(f"e_full{k}") for k in range(2)]
        e_free = [sem(f"e_free{k}") for k in range(2)]
        cur_set, p_set, steer_set, steered = sem("cur_set"), sem("p_set"), sem("steer_set"), sem("steered")
        tok_set, stat_set, mv_set = sem("tok_set"), sem("stat_set"), sem("mv_set")
        var_set, rstd_set, normed = sem("var_set"), sem("rstd_set"), sem("normed")
        xh_set, xl_set = sem("xh_set"), sem("xl_set")
        qk_hi, qk_lo, v_set = sem("qk_hi"), sem("qk_lo"), sem("v_set")
        stack_ld = [sem(f"stack_ld{n}") for n in range(2)]
        nm_hi, nm_lo, mr_set = sem("nm_hi"), sem("nm_lo"), sem("mr_set")
        mr_ld = [sem(f"mr_ld{n}") for n in range(2)]
        masked, pv_done, ctx_free = sem("masked"), sem("pv_done"), sem("ctx_free")
        rec_set, ctxn_set, ch_set, cl_set = sem("rec_set"), sem("ctxn_set"), sem("ch_set"), sem("cl_set")
        d_set, base_set, mid_set = sem("d_set"), sem("base_set"), sem("mid_set")
        waited = {e: sem("waited_" + e) for e in ("dve", "act", "pool", "pe", "sp")}

        pj = lambda k: psum[:, k, :]
        sc = lambda k: psum[:, 2 + k, :]
        ex = lambda k: psum[:, 4 + k, :]
        ctx_bank, sum_bank = psum[:, 6, :], psum[:, 7, :]

        first = [n for part in before_names(0) for n in part]
        lead = len(first)
        round_names = sample_names(0, True) + sample_names(1, True)
        last_names = sample_names(0, True) + sample_names(1, False)
        per_round = len(round_names) // 2
        prologue = Ring(0, first, 0)
        steady = Ring(lead, round_names, per_round)
        final = Ring(lead, last_names, per_round)
        s_ring = Ring(0, [(g, u) for g in range(G) for u in range(S_USES)], G * S_USES // 2)
        e_ring = Ring(0, [(g, j, h) for g in range(G) for j in range(T) for h in range(HG)], G * T * HG // 2)

        block = ctx.enter_context(nc.Block())

        @block.sync
        def _(sp):
            sp.dma_start(gate_w1[:], io["gate_w1"]).then_inc(gw_ld, 16)
            for n, (w, where) in enumerate((("wq", xb[0]), ("wk", xb[1]), ("wv", pt[0]), ("wo", pt[1]))):
                sp.dma_start(where[:], io[w]).then_inc(raw_ld[n], 16)
            sp.wait_ge(w_lo_set, 4 * J)
            sp.wait_ge(beta_full, 3)
            sp.sem_inc(mid_st[0], 16)
            sp.sem_inc(mid_st[1], 16)
            sp.sem_inc(base_st, 16)
            sp.dma_start(xb[0][:], sample_at(io["x1"], 0)).then_inc(x_ld[0], 16)

            def sample(i, s, ahead):
                b = 2 * i + s
                if ahead:
                    wait_apart(sp, mid_st[1 - s], 16 * (i + 1 + s), waited["sp"])
                    sp.dma_start(xb[1 - s][:], sample_at(io["x1"], b + 1)).then_inc(x_ld[1 - s], 16)

                def stack_rows(g):
                    wait_apart(sp, qk_lo, 8 * b + 2 * g + 2, waited["sp"])
                    if g >= 2:
                        for k in range(2):
                            wait_apart(sp, e_full[k], e_ring.full((g - 2, T - 1, HG - 2 + k), b), waited["sp"])
                    for h in range(HG):
                        for row, (a, step) in enumerate(((1, 1), (0, 2), (1, 2))):
                            sp.dma_start(stack[HG * (g % 2) + h][row * DH:(row + 1) * DH, :, :].bitcast(F32),
                                         qk4[h * DH:(h + 1) * DH, a:a + step + 1:step, :].bitcast(F32)
                                         ).then_inc(stack_ld[g % 2], 16)

                def max_rows(g):
                    sp.wait_ge(mr_set, G * b + g + 1)
                    for h in range(HG):
                        sp.dma_start(stack[HG * (g % 2) + h][3 * DH:3 * DH + 2, 0, :].bitcast(F32),
                                     mr[g % 2][2 * h:2 * h + 2, :].bitcast(F32)).then_inc(mr_ld[g % 2], 16)

                stack_rows(0)
                stack_rows(1)
                max_rows(0)
                stack_rows(2)
                max_rows(1)
                stack_rows(3)
                max_rows(2)
                max_rows(3)
                wait_apart(sp, base_set, J * (b + 1), waited["sp"])
                sp.dma_start(sample_at(io["base"], b), v[:]).then_inc(base_st, 16)
                wait_apart(sp, mid_set, J * (b + 1), waited["sp"])
                sp.dma_start(sample_at(io["mid"], b), xb[s][:]).then_inc(mid_st[s], 16)

            with sp.Fori(0, PAIRS - 1) as i:
                sample(i, 0, True)
                sample(i, 1, True)
            sample(PAIRS - 1, 0, True)
            sample(PAIRS - 1, 1, False)
            sp.wait_ge(base_st, 16 * (B + 1))
            for s in range(2):
                sp.wait_ge(mid_st[s], 16 * (PAIRS + 1))

        @block.gpsimd
        def _(pool):
            pool.memset(mask[:], 0.0).then_inc(mask_made, 1)
            pool.wait_ge(mask_made, 1)
            pool.affine_select(out=mask[:, S - P:S], in_=mask[:, S - P:S], compare_op=ALU.is_ge, fill=MASKED, base=0,
                               pattern=[[-1, P]], channel_multiplier=1).then_inc(mask_made, 1)

            def prepare_add(s, b):
                for j in range(J):
                    pool.wait_ge(steer_set, J * b + j + 1)
                    pool.tensor_tensor(xb[s][:, j, :], xb[s][:, j, :], tok[:, j, :], ALU.add).then_inc(steered, 1)

            def prepare_rstd(b):
                wait_apart(pool, mv_set, T * (b + 1), waited["pool"])
                pool.tensor_scalar(var[:], mv[:, :, 1], LN_EPS, None, ALU.add).then_inc(var_set, 1)
                wait_apart(pool, var_set, b + 1, waited["pool"])
                pool.tensor_tensor(rstd[:], var[:], keep["minus_half"][:], ALU.pow).then_inc(rstd_set, 1)

            def masks(g, b):
                for j in range(T):
                    for k in range(2):
                        wait_apart(pool, e_free[k], e_ring.full((g, j, HG - 2 + k), b) + 1, waited["pool"])
                    pool.affine_select(out=pt[j % 2][:, :, 0:P], in_=pt[j % 2][:, :, 0:P], compare_op=ALU.is_ge, fill=0.0,
                                       base=0, pattern=[[0, HG], [1, P]], channel_multiplier=-1).then_inc(masked, 1)

            def sample(i, s, ahead):
                b = 2 * i + s
                masks(0, b)
                if ahead:
                    prepare_add(1 - s, b + 1)
                masks(1, b)
                if ahead:
                    prepare_rstd(b + 1)
                masks(2, b)
                masks(3, b)
                for j in range(J):
                    pool.wait_ge(base_set, J * b + j + 1)
                    pool.tensor_tensor(xb[s][:, j, :], xb[s][:, j, :], tok[:, j, :], ALU.add).then_inc(mid_set, 1)

            prepare_add(0, 0)
            prepare_rstd(0)
            with pool.Fori(0, PAIRS - 1) as i:
                sample(i, 0, True)
                sample(i, 1, True)
            sample(PAIRS - 1, 0, True)
            sample(PAIRS - 1, 1, False)

        @block.vector
        def _(dve):
            for n in range(2 * HG):
                dve.memset(stack[n][3 * DH:3 * DH + 2, 1, :].bitcast(F32), 1.0).then_inc(rows_made, 1)
            for n, (w, where) in enumerate((("wq", xb[0]), ("wk", xb[1]), ("wv", pt[0]), ("wo", pt[1]))):
                for j in range(J):
                    dve.wait_ge(w_hi_set, J * n + j + 1)
                    scale = small(smalls, "gamma1", j) if w != "wo" else 1.0
                    dve.scalar_tensor_tensor(w_lo[w][:, j, :], where[:, j, :], scale, w_hi[w][:, j, :].bitcast(F32),
                                             ALU.mult, ALU.subtract).then_inc(w_lo_set, 1)
            for n, name in enumerate(("bq", "bk", "bv")):
                dve.wait_ge(beta_full, n + 1)
                dve.tensor_tensor(bias[:, n, :], psum[:, 2 + n, 0:G], small(smalls, name), ALU.add).then_inc(beta_set, 1)
            dve.tensor_scalar(gate_w2[:], ident[:], 0.0, small(smalls, "gate_w2"), ALU.mult, ALU.add).then_inc(gate_dve, 1)
            dve.tensor_tensor(rbias[:], small(smalls, "safety_bias"), small(smalls, "resp_b"), ALU.add).then_inc(gate_dve, 1)
            dve.wait_ge(gate_act, 3)
            dve.tensor_tensor(strength[:], strength[:], mod[:], ALU.mult).then_inc(gate_dve, 1)
            dve.wait_ge(gate_dve, 3)
            dve.tensor_copy(pb[:, :, STRENGTH], strength[:])
            for j in range(J):
                dve.tensor_scalar(pb[:, :, RBIAS + j], strength[:], rbias[:, j:j + 1], None, ALU.mult)
                dve.tensor_scalar(pb[:, :, GB2 + j], small(smalls, "gate"), small(smalls, "b2", j), None, ALU.mult)
            dve.tensor_copy(pb[:, :, GATE], small(smalls, "gate")).then_inc(gate_dve, 1)
            dve.wait_ge(mask_made, 2)
            dve.wait_ge(gate_dve, 4)
            for k in range(2):
                dve.sem_inc(s_free[k], 1)

            def prepare_scalars(s, b):
                dve.tensor_copy(cur[s][:], pb[:, bass.ds(b, 1), :].rearrange("p b n -> p (b n)")).then_inc(cur_set, 1)

            def prepare_norm(b):
                for t in range(T):
                    dve.wait_ge(tok_set, T * b + t + 1)
                    dve.bn_stats(st[:, t, :], tok[:, t, :]).then_inc(stat_set, 1)
                for t in range(T):
                    wait_apart(dve, stat_set, T * b + t + 1, waited["dve"])
                    dve.bn_aggr(mv[:, t, :], st[:, t, :]).then_inc(mv_set, 1)
                dve.wait_ge(rstd_set, b + 1)
                for t in range(T):
                    dve.tensor_scalar(tok[:, t, :], tok[:, t, :], mv[:, t, 0:1], rstd[:, t:t + 1], ALU.subtract,
                                      ALU.mult).then_inc(normed, 1)

            def prepare_lo(ring, i, s, b):
                for j in range(J):
                    k = ring.bank((s, "tback", j))
                    dve.wait_ge(xh_set, J * b + j + 1)
                    dve.tensor_tensor(xl[:, j, :], pj(k), xh[:, j, :].bitcast(F32), ALU.subtract).then_inc(xl_set, 1)
                    dve.wait_ge(xl_set, J * b + j + 1)
                    dve.sem_inc(pj_free[k], 1)

            def qk_low(ring, i, s, b, g, n):
                k = ring.bank((s, "qk"[n], g))
                if g:
                    dve.wait_ge(stack_ld[(g - 1) % 2], 384 * b + 192 * ((g - 1) // 2 + 1))
                wait_apart(dve, qk_hi, 8 * b + 2 * g + n + 1, waited["dve"])
                dve.scalar_tensor_tensor(qk4[:, 3 * n, :], pj(k), bias[:, n, g:g + 1], qk4[:, 1 + n, :].bitcast(F32),
                                         ALU.add, ALU.subtract).then_inc(qk_lo, 1)
                dve.wait_ge(qk_lo, 8 * b + 2 * g + n + 1)
                dve.sem_inc(pj_free[k], 1)

            def max_unit(g, u, b):
                h, tiles = u // len(U_TILES), U_TILES[u % len(U_TILES)]
                k = s_ring.bank((g, u))
                wait_apart(dve, s_full[k], s_ring.full((g, u), b), waited["dve"])
                at = 0
                for t in tiles:
                    width = P * (t + 1)
                    got = sc(k)[:, at:at + width]
                    last = dve.tensor_tensor_reduce(got, got, mask[:, S - width:S], 1.0, 2.0 * MASKED, ALU.add, ALU.max,
                                                    mx[:, t, h:h + 1])
                    at += width
                last.then_inc(s_free[k], 1)

            def minus_max(g, b):
                for u in (UNITS - 2, UNITS - 1):
                    wait_apart(dve, s_free[s_ring.bank((g, u))], s_ring.full((g, u), b) + 1, waited["dve"])
                dve.tensor_scalar(nm[:, :, :, 0], mx[:], -1.0, None, ALU.mult).then_inc(nm_hi, 1)
                dve.wait_ge(nm_hi, G * b + g + 1)
                dve.scalar_tensor_tensor(nm[:, :, :, 1], mx[:], -1.0, nm[:, :, :, 0].bitcast(F32), ALU.mult,
                                         ALU.subtract).then_inc(nm_lo, 1)

            def over_sums(g, c, b):
                if c == 0:
                    dve.wait_ge(ctx_free, 1 + G * b + g + 1)
                part = sums[:, c * P:(c + 1) * P]
                dve.reciprocal(part, part).then_inc(rec_set, 1)
                if c == T - 1:
                    dve.wait_ge(rec_set, T * (G * b + g + 1))
                    dve.tensor_tensor(ctxs[:], ctxs[:], sums[:], ALU.mult).then_inc(ctxn_set, 1)

            def ctx_low(g, b):
                dve.wait_ge(ch_set, G * b + g + 1)
                dve.scalar_tensor_tensor(cl[:, g, :], ctxs[:], bias[:, 2, g:g + 1], ch[:, g, :].bitcast(F32), ALU.add,
                                         ALU.subtract).then_inc(cl_set, 1)

            def sample(ring, i, s, ahead):
                b = 2 * i + s
                for g in range(2):
                    for n in range(2):
                        qk_low(ring, i, s, b, g, n)
                if ahead:
                    prepare_scalars(1 - s, b + 1)
                for g in range(G):
                    for u in range(UNITS):
                        max_unit(g, u, b)
                        if g in (1, 2) and u % 6 == 5:
                            qk_low(ring, i, s, b, g + 1, u // 6)
                        if g >= 2 and u % 3 == 2:
                            over_sums(g - 2, u // 3, b)
                    minus_max(g, b)
                    if g >= 2:
                        ctx_low(g - 2, b)
                    if g == 2 and ahead:
                        prepare_norm(b + 1)
                if ahead:
                    prepare_lo(ring, i, 1 - s, b + 1)
                for g in (G - 2, G - 1):
                    for c in range(T):
                        over_sums(g, c, b)
                    ctx_low(g, b)
                for j in range(J):
                    wait_apart(dve, d_set, J * b + j + 1, waited["dve"])
                    if j == 0:
                        dve.wait_ge(cur_set, b + 1)
                    dve.scalar_tensor_tensor(v[:, j, :], tok[:, j, :], cur[s][:, GATE:GATE + 1], xb[s][:, j, :], ALU.mult,
                                             ALU.add).then_inc(base_set, 1)

            prepare_scalars(0, 0)
            prepare_norm(0)
            prepare_lo(prologue, 0, 0, 0)
            with dve.Fori(0, PAIRS - 1) as i:
                sample(steady, i, 0, True)
                sample(steady, i, 1, True)
            sample(final, PAIRS - 1, 0, True)
            sample(final, PAIRS - 1, 1, False)

        @block.scalar
        def _(act):
            for n, (w, where) in enumerate((("wq", xb[0]), ("wk", xb[1]), ("wv", pt[0]), ("wo", pt[1]))):
                act.wait_ge(raw_ld[n], 16)
                for j in range(J):
                    scale = small(smalls, "gamma1", j) if w != "wo" else 1.0
                    act.activation(w_hi[w][:, j, :], where[:, j, :], ACT.Copy, scale=scale).then_inc(w_hi_set, 1)
            act.wait_ge(gate_full, 1)
            act.activation(gate_h[:], psum[:, 5, 0:B], ACT.Relu, bias=small(smalls, "gate_b1"), scale=1.0 / S).then_inc(gate_act, 1)
            act.wait_ge(gate_full, 2)
            act.activation(strength[:], psum[:, 6, 0:B], ACT.Sigmoid, bias=small(smalls, "gate_b2")).then_inc(gate_act, 1)
            act.activation(mod[:], small(smalls, "safety"), ACT.Sigmoid).then_inc(gate_act, 1)
            for k in range(2):
                act.sem_inc(e_free[k], 1)
            act.sem_inc(ctx_free, 1)

            def prepare_p(ring, i, s, b):
                k = ring.bank((s, "p"))
                act.wait_ge(pj_full[k], ring.full((s, "p"), i))
                act.activation(psb[:], pj(k)[0:R, :], ACT.Copy).then_inc(p_set, 1)
                act.wait_ge(p_set, b + 1)
                act.sem_inc(pj_free[k], 1)

            def prepare_steer(ring, i, s, b):
                act.wait_ge(cur_set, b + 1)
                for j in range(J):
                    k = ring.bank((s, "resp", j))
                    act.wait_ge(pj_full[k], ring.full((s, "resp", j), i))
                    act.activation(tok[:, j, :], pj(k), ACT.Identity, bias=cur[s][:, RBIAS + j:RBIAS + j + 1],
                                   scale=cur[s][:, STRENGTH:STRENGTH + 1]).then_inc(steer_set, 1)
                    act.wait_ge(steer_set, J * b + j + 1)
                    act.sem_inc(pj_free[k], 1)

            def prepare_tokens(ring, i, s, b):
                for t in range(T):
                    k = ring.bank((s, "tin", t))
                    act.wait_ge(pj_full[k], ring.full((s, "tin", t), i))
                    act.activation(tok[:, t, :], pj(k), ACT.Copy).then_inc(tok_set, 1)
                    act.wait_ge(tok_set, T * b + t + 1)
                    act.sem_inc(pj_free[k], 1)

            def prepare_hi(ring, i, s, b):
                for j in range(J):
                    k = ring.bank((s, "tback", j))
                    act.wait_ge(pj_full[k], ring.full((s, "tback", j), i))
                    act.activation(xh[:, j, :], pj(k), ACT.Copy).then_inc(xh_set, 1)

            def qk_high(ring, i, s, b, g, n):
                name = (s, "qk"[n], g)
                k = ring.bank(name)
                if g:
                    act.wait_ge(stack_ld[(g - 1) % 2], 384 * b + 192 * ((g - 1) // 2 + 1))
                act.wait_ge(pj_full[k], ring.full(name, i))
                act.activation(qk4[:, 1 + n, :], pj(k), ACT.Identity, bias=bias[:, n, g:g + 1]).then_inc(qk_hi, 1)

            def exponentials(g, j, heads, b):
                width = S - P * j
                if T * g + j >= 2:
                    act.wait_ge(pv_done, G * T * b + T * g + j - 1)
                for h in heads:
                    k = e_ring.bank((g, j, h))
                    act.wait_ge(e_full[k], e_ring.full((g, j, h), b))
                    act.activation(pt[j % 2][:, h, 0:width], ex(k)[:, 0:width], ACT.Exp,
                                   scale=INV_SQRT_DH).then_inc(e_free[k], 1)

            def context(g, b):
                if g:
                    act.wait_ge(cl_set, G * b + g)
                act.wait_ge(pv_done, G * T * b + T * (g + 1))
                act.activation(ctxs[:], ctx_bank, ACT.Copy)
                act.activation(sums[:], sum_bank, ACT.Copy).then_inc(ctx_free, 1)

            def ctx_high(g, b):
                act.wait_ge(ctxn_set, G * b + g + 1)
                act.activation(ch[:, g, :], ctxs[:], ACT.Identity, bias=bias[:, 2, g:g + 1]).then_inc(ch_set, 1)

            def max_rows(g, b):
                k = s_ring.bank((g, UNITS))
                if g >= 2:
                    act.wait_ge(mr_ld[g % 2], 128 * b + 64)
                act.wait_ge(s_full[k], s_ring.full((g, UNITS), b))
                act.activation(mr[g % 2][:], sc(k)[0:2 * HG, :], ACT.Copy).then_inc(mr_set, 1)
                act.wait_ge(mr_set, G * b + g + 1)
                act.sem_inc(s_free[k], 1)

            def sample(ring, i, s, ahead):
                b = 2 * i + s
                for g in range(2):
                    for n in range(2):
                        qk_high(ring, i, s, b, g, n)
                if ahead:
                    prepare_p(ring, i, 1 - s, b + 1)
                act.wait_ge(base_st, 16 * (b + 1))
                for t in range(T):
                    k = ring.bank((s, "v", t))
                    act.wait_ge(pj_full[k], ring.full((s, "v", t), i))
                    act.activation(v[:, t, :], pj(k), ACT.Copy).then_inc(v_set, 1)
                    act.wait_ge(v_set, T * b + t + 1)
                    act.sem_inc(pj_free[k], 1)
                max_rows(0, b)
                for g in range(1, G):
                    for u in range(UNITS):
                        if 3 <= u < 11:
                            exponentials(g - 1, (u - 3) // 2, (2 * ((u - 3) % 2), 2 * ((u - 3) % 2) + 1), b)
                        if g < 3 and u % 6 == 5:
                            qk_high(ring, i, s, b, g + 1, u // 6)
                    if g >= 2:
                        ctx_high(g - 2, b)
                    context(g - 1, b)
                    max_rows(g, b)
                    if ahead and g == 1:
                        prepare_steer(ring, i, 1 - s, b + 1)
                    if ahead and g == 2:
                        prepare_tokens(ring, i, 1 - s, b + 1)
                if ahead:
                    prepare_hi(ring, i, 1 - s, b + 1)
                for j in range(T):
                    exponentials(G - 1, j, range(HG), b)
                ctx_high(G - 2, b)
                context(G - 1, b)
                ctx_high(G - 1, b)
                for j in range(J):
                    k = ring.bank((s, "wo", j))
                    act.wait_ge(pj_full[k], ring.full((s, "wo", j), i))
                    act.activation(tok[:, j, :], pj(k), ACT.Identity, bias=small(smalls, "bo", j)).then_inc(d_set, 1)
                    act.wait_ge(d_set, J * b + j + 1)
                    act.sem_inc(pj_free[k], 1)

            prepare_p(prologue, 0, 0, 0)
            prepare_steer(prologue, 0, 0, 0)
            prepare_tokens(prologue, 0, 0, 0)
            prepare_hi(prologue, 0, 0, 0)
            act.wait_ge(beta_set, 3)
            with act.Fori(0, PAIRS - 1) as i:
                sample(steady, i, 0, True)
                sample(steady, i, 1, True)
            sample(final, PAIRS - 1, 0, True)
            sample(final, PAIRS - 1, 1, False)

        @block.tensor
        def _(pe):
            for n, where in enumerate((xb[0], xb[1], pt[0])):
                pe.wait_ge(raw_ld[n], 16)
                for g in range(G):
                    for j in range(J):
                        last = pe.matmul(psum[:, 2 + n, g:g + 1], where[:, j, g * P:(g + 1) * P], small(smalls, "beta1", j),
                                         start=(j == 0), stop=(j == J - 1))
                last.then_inc(beta_full, 1)
            pe.wait_ge(gw_ld, 16)
            for j in range(J):
                last = pe.matmul(psum[:, 5, 0:B], gate_w1[:, j, :], pooled[:, :, j], start=(j == 0), stop=(j == J - 1))
            last.then_inc(gate_full, 1)
            pe.wait_ge(gate_act, 1)
            pe.wait_ge(gate_dve, 1)
            pe.matmul(psum[:, 6, 0:B], gate_w2[:], gate_h[:], start=True, stop=True).then_inc(gate_full, 1)

            def claim(ring, i, name):
                k = ring.bank(name)
                if ring is not prologue or ring.free(name):
                    wait_apart(pe, pj_free[k], ring.free(name, i), waited["pe"])
                return k

            def prepare_p(ring, i, s, b):
                k = claim(ring, i, (s, "p"))
                wait_apart(pe, x_ld[s], 16 * (i + 1 + (1 - s) * (ring is not prologue)), waited["pe"])
                for j in range(J):
                    last = pe.matmul(pj(k)[0:R, :], keep["uo"][:, j, :], xb[s][:, j, :], start=(j == 0), stop=(j == J - 1))
                last.then_inc(pj_full[k], 1)

            def prepare_steer(ring, i, s, b):
                wait_apart(pe, p_set, b + 1, waited["pe"])
                for j in range(J):
                    k = claim(ring, i, (s, "resp", j))
                    pe.matmul(pj(k), keep["steer"][:, j, :], psb[:], start=True, stop=True).then_inc(pj_full[k], 1)

            def prepare_tokens(ring, i, s, b):
                wait_apart(pe, steered, J * (b + 1), waited["pe"])
                for t in range(T):
                    k = claim(ring, i, (s, "tin", t))
                    for j in range(J):
                        last = pe.transpose(pj(k)[:, j * P:(j + 1) * P], xb[s][:, j, t * P:(t + 1) * P], ident[:])
                    last.then_inc(pj_full[k], 1)

            def prepare_back(ring, i, s, b):
                wait_apart(pe, normed, T * (b + 1), waited["pe"])
                for j in range(J):
                    k = claim(ring, i, (s, "tback", j))
                    for t in range(T):
                        last = pe.transpose(pj(k)[:, t * P:(t + 1) * P], tok[:, t, j * P:(j + 1) * P], ident[:])
                    last.then_inc(pj_full[k], 1)

            def qk_product(k, g, n, parts):
                w = ("wq", "wk")[n]
                at = slice(g * P, (g + 1) * P)
                return three_pass(pe, pj(k), [(w_hi[w][:, j, at], w_lo[w][:, j, at], xh[:, j, :], xl[:, j, :]) for j in parts],
                                  start=parts[0] == 0, stop=parts[-1] == J - 1)

            def max_unit(g, u, b):
                h, tiles = u // len(U_TILES), U_TILES[u % len(U_TILES)]
                if u == 0:
                    wait_apart(pe, stack_ld[g % 2], 384 * b + 192 * (g // 2 + 1), waited["pe"])
                k = s_ring.bank((g, u))
                wait_apart(pe, s_free[k], s_ring.free((g, u), b) + 1, waited["pe"])
                both = stack[HG * (g % 2) + h]
                at = 0
                for t in tiles:
                    width = P * (t + 1)
                    last = pe.matmul(sc(k)[:, at:at + width], both[0:3 * DH, 0, t * P:(t + 1) * P], both[0:3 * DH, 1, 0:width],
                                     start=True, stop=True)
                    at += width
                last.then_inc(s_full[k], 1)

            def max_rows(g, b):
                k = s_ring.bank((g, UNITS))
                wait_apart(pe, nm_lo, G * b + g + 1, waited["pe"])
                wait_apart(pe, s_free[k], s_ring.free((g, UNITS), b) + 1, waited["pe"])
                for t in range(T):
                    last = pe.transpose(sc(k)[0:2 * HG, t * P:(t + 1) * P],
                                        nm[:, t, :, :].rearrange("p h n -> p (h n)").bitcast(F32), ident[:])
                last.then_inc(s_full[k], 1)

            def exp_scores(g, j, heads, b):
                if j == 0 and heads[0] == 0:
                    wait_apart(pe, mr_ld[g % 2], 128 * b + 64 * (g // 2 + 1), waited["pe"])
                width = S - P * j
                for h in heads:
                    k = e_ring.bank((g, j, h))
                    wait_apart(pe, e_free[k], e_ring.free((g, j, h), b) + 1, waited["pe"])
                    both = stack[HG * (g % 2) + h]
                    pe.matmul(ex(k)[:, 0:width], both[0:3 * DH + 2, 1, j * P:(j + 1) * P], both[0:3 * DH + 2, 0, j * P:S],
                              start=True, stop=True).then_inc(e_full[k], 1)

            def values(g, j, b):
                if j == 0:
                    wait_apart(pe, ctx_free, G * b + g + 1, waited["pe"])
                    wait_apart(pe, v_set, T * (b + 1), waited["pe"])
                wait_apart(pe, masked, G * T * b + T * g + j + 1, waited["pe"])
                width = S - P * j
                for bank, is_ctx in ((ctx_bank, True), (sum_bank, False)):
                    for h in range(HG):
                        at = slice(h * DH, (h + 1) * DH)
                        lhs = v[:, j, (HG * g + h) * DH:(HG * g + h + 1) * DH] if is_ctx else keep["ones"][:]
                        last = pe.matmul(bank[at, j * P:S], lhs, pt[j % 2][:, h, 0:width], start=(j == 0), stop=(j == T - 1),
                                         tile_position=(0, h * DH))
                last.then_inc(pv_done, 1)

            def sample(ring, i, s, ahead):
                b = 2 * i + s
                wait_apart(pe, xl_set, J * (b + 1), waited["pe"])
                for g in range(2):
                    for n in range(2):
                        k = claim(ring, i, (s, "qk"[n], g))
                        qk_product(k, g, n, range(J)).then_inc(pj_full[k], 1)
                if ahead:
                    prepare_p(ring, i, 1 - s, b + 1)
                for u in range(UNITS):
                    max_unit(0, u, b)
                    if u % 3 == 2:
                        t = u // 3
                        k = claim(ring, i, (s, "v", t))
                        at = slice(t * P, (t + 1) * P)
                        three_pass(pe, pj(k), [(xh[:, j, at], xl[:, j, at], w_hi["wv"][:, j, :], w_lo["wv"][:, j, :])
                                               for j in range(J)]).then_inc(pj_full[k], 1)
                max_rows(0, b)
                for g in range(1, G):
                    for u in range(UNITS):
                        max_unit(g, u, b)
                        if g < 3:
                            n, part = u // 6, u % 6
                            if part == 0:
                                k = claim(ring, i, (s, "qk"[n], g + 1))
                            if part < J:
                                last = qk_product(k, g + 1, n, (part,))
                                if part == J - 1:
                                    last.then_inc(pj_full[k], 1)
                        if 3 <= u < 11:
                            j, half = (u - 3) // 2, (u - 3) % 2
                            exp_scores(g - 1, j, (2 * half, 2 * half + 1), b)
                            if half and j:
                                values(g - 1, j - 1, b)
                    values(g - 1, T - 1, b)
                    max_rows(g, b)
                    if ahead and g == 1:
                        prepare_steer(ring, i, 1 - s, b + 1)
                    if ahead and g == 2:
                        prepare_tokens(ring, i, 1 - s, b + 1)
                if ahead:
                    prepare_back(ring, i, 1 - s, b + 1)
                for j in range(T):
                    exp_scores(G - 1, j, range(HG), b)
                    if j:
                        values(G - 1, j - 1, b)
                values(G - 1, T - 1, b)
                wait_apart(pe, cl_set, G * (b + 1), waited["pe"])
                for jo in range(J):
                    k = claim(ring, i, (s, "wo", jo))
                    at = slice(jo * P, (jo + 1) * P)
                    three_pass(pe, pj(k), [(w_hi["wo"][:, g, at], w_lo["wo"][:, g, at], ch[:, g, :], cl[:, g, :])
                                           for g in range(G)]).then_inc(pj_full[k], 1)

            prepare_p(prologue, 0, 0, 0)
            prepare_steer(prologue, 0, 0, 0)
            prepare_tokens(prologue, 0, 0, 0)
            prepare_back(prologue, 0, 0, 0)
            pe.wait_ge(w_lo_set, 4 * J)
            pe.wait_ge(rows_made, 2 * HG)
            pe.wait_ge(beta_set, 3)
            with pe.Fori(0, PAIRS - 1) as i:
                sample(steady, i, 0, True)
                sample(steady, i, 1, True)
            sample(final, PAIRS - 1, 0, True)
            sample(final, PAIRS - 1, 1, False)


def feed_forward_phase(nc, io, keep, psum):
    smalls, ident, pb = keep["smalls"], keep["ident"], keep["pb"]
    with ExitStack() as ctx:
        def sb(name, shape, dt=F32):
            return ctx.enter_context(nc.sbuf_tensor("c_" + name, shape, dt))

        def sem(name):
            return ctx.enter_context(nc.semaphore("c_" + name))

        w1_hi, w1_lo = sb("w1_hi", [P, J, FF], F32R), sb("w1_lo", [P, J, FF], F32R)
        w2_hi, w2_lo = sb("w2_hi", [P, M, D], F32R), sb("w2_lo", [P, M, D], F32R)
        x = sb("x", [P, J, S])
        tok = sb("tok", [P, J, S])
        base = sb("base", [P, J, S])
        h_hi = [sb(f"h_hi{s}", [P, J, S], F32R) for s in range(2)]
        h_lo = [sb(f"h_lo{s}", [P, J, S], F32R) for s in range(2)]
        act_f = [sb(f"act{k}", [P, S]) for k in range(2)]
        act_hi = [sb(f"act_hi{k}", [P, S], F32R) for k in range(2)]
        act_lo = [sb(f"act_lo{k}", [P, S], F32R) for k in range(2)]
        b1 = sb("b1", [P, M])
        st = sb("st", [P, T, 6])
        mv = sb("mv", [P, T, 2])
        var = sb("var", [P, T])
        rstd = sb("rstd", [P, T])
        cur = [sb(f"cur{s}", [P, N_PB]) for s in range(2)]

        raw_ld = [sem(f"raw_ld{n}") for n in range(3)]
        w_hi_set, w_lo_set, beta_full, b1_set = sem("w_hi_set"), sem("w_lo_set"), sem("beta_full"), sem("b1_set")
        x_ld, base_ld, out_st = sem("x_ld"), sem("base_ld"), sem("out_st")
        cur_set = sem("cur_set")
        tin_full, tok_set, stat_set, mv_set = sem("tin_full"), sem("tok_set"), sem("stat_set"), sem("mv_set")
        var_set, rstd_set, normed, tback_full = sem("var_set"), sem("rstd_set"), sem("normed"), sem("tback_full")
        h_hi_set, h_lo_set = sem("h_hi_set"), sem("h_lo_set")
        hidden_full, gelu_set, act_hi_set, act_lo_set = sem("hidden_full"), sem("gelu_set"), sem("act_hi_set"), sem("act_lo_set")
        added = sem("added")
        gated, out_set = sem("gated"), sem("out_set")
        waited = {e: sem("waited_" + e) for e in ("dve", "act", "pool", "pe", "sp")}

        hidden = lambda n: psum[:, n % 2, :]
        total = lambda j: psum[:, 2 + j, :]
        turn = lambda n: psum[:, 6 + n % 2, :]
        stage = (x, base, tok)
        chunks = [("w1", j) for j in range(J)] + [("w2", j) for j in range(J)]
        w2_part = lambda w, j: w[:, j * (M // J):(j + 1) * (M // J), :].rearrange("p m d -> p (m d)")
        flat = lambda a: a[:].rearrange("p j t -> p (j t)")

        block = ctx.enter_context(nc.Block())

        @block.sync
        def _(sp):
            for n, (w, j) in enumerate(chunks):
                if n >= 3:
                    sp.wait_ge(w_lo_set, n - 2)
                    if n - 3 < J:
                        sp.wait_ge(beta_full, n - 2)
                src = io[w][:, j, :] if w == "w1" else w2_part(io[w], j)
                sp.dma_start(flat(stage[n % 3]), src).then_inc(raw_ld[n % 3], 16)
            sp.wait_ge(w_lo_set, len(chunks))
            sp.dma_start(x[:], sample_at(io["mid"], 0)).then_inc(x_ld, 16)
            sp.dma_start(base[:], sample_at(io["base"], 0)).then_inc(base_ld, 16)

            def sample(i, s, ahead):
                b = 2 * i + s
                if ahead:
                    wait_apart(sp, tin_full, T * (b + 1), waited["sp"])
                    sp.dma_start(x[:], sample_at(io["mid"], b + 1)).then_inc(x_ld, 16)
                wait_apart(sp, out_set, J * (b + 1), waited["sp"])
                sp.dma_start(sample_at(io["out"], b), base[:]).then_inc(out_st, 16)
                if ahead:
                    wait_apart(sp, out_st, 16 * (b + 1), waited["sp"])
                    sp.dma_start(base[:], sample_at(io["base"], b + 1)).then_inc(base_ld, 16)

            with sp.Fori(0, PAIRS - 1) as i:
                sample(i, 0, True)
                sample(i, 1, True)
            sample(PAIRS - 1, 0, True)
            sample(PAIRS - 1, 1, False)
            sp.wait_ge(out_st, 16 * B)

        @block.gpsimd
        def _(pool):
            def norm(b):
                wait_apart(pool, mv_set, T * (b + 1), waited["pool"])
                pool.tensor_scalar(var[:], mv[:, :, 1], LN_EPS, None, ALU.add).then_inc(var_set, 1)
                wait_apart(pool, var_set, b + 1, waited["pool"])
                pool.tensor_tensor(rstd[:], var[:], keep["minus_half"][:], ALU.pow).then_inc(rstd_set, 1)

            def sample(i, s, ahead):
                b = 2 * i + s
                if ahead:
                    norm(b + 1)
                for j in range(J):
                    wait_apart(pool, gated, J * b + J + j + 1, waited["pool"])
                    pool.tensor_scalar(base[:, j, :], base[:, j, :], cur[s][:, GB2 + j:GB2 + j + 1], None,
                                       ALU.add).then_inc(out_set, 1)

            norm(0)
            with pool.Fori(0, PAIRS - 1) as i:
                sample(i, 0, True)
                sample(i, 1, True)
            sample(PAIRS - 1, 0, True)
            sample(PAIRS - 1, 1, False)

        @block.vector
        def _(dve):
            for n, (w, j) in enumerate(chunks):
                dve.wait_ge(w_hi_set, n + 1)
                if w == "w1":
                    part, scale, hi = w1_lo[:, j, :], small(smalls, "gamma2", j), w1_hi[:, j, :]
                else:
                    part, scale, hi = w2_part(w2_lo, j), 1.0, w2_part(w2_hi, j)
                dve.scalar_tensor_tensor(part, flat(stage[n % 3]), scale, hi.bitcast(F32), ALU.mult,
                                         ALU.subtract).then_inc(w_lo_set, 1)
            dve.wait_ge(beta_full, J)
            dve.tensor_tensor(b1[:], small(smalls, "b1"), psum[:, 0, 0:M], ALU.add).then_inc(b1_set, 1)
            for j in range(1, J):
                dve.wait_ge(b1_set, j)
                dve.tensor_tensor(b1[:], b1[:], psum[:, 0, j * M:(j + 1) * M], ALU.add).then_inc(b1_set, 1)
            dve.sem_inc(act_hi_set, 2)
            dve.sem_inc(act_lo_set, 2)
            dve.sem_inc(gated, J)

            def statistics(b, t):
                dve.wait_ge(tok_set, T * b + t + 1)
                dve.bn_stats(st[:, t, :], tok[:, t, :]).then_inc(stat_set, 1)
                wait_apart(dve, stat_set, T * b + t + 1, waited["dve"])
                dve.bn_aggr(mv[:, t, :], st[:, t, :]).then_inc(mv_set, 1)

            def normalise(b):
                dve.wait_ge(rstd_set, b + 1)
                for t in range(T):
                    dve.tensor_scalar(tok[:, t, :], tok[:, t, :], mv[:, t, 0:1], rstd[:, t:t + 1], ALU.subtract,
                                      ALU.mult).then_inc(normed, 1)

            def norm_low(s, b, j):
                dve.wait_ge(h_hi_set, J * b + j + 1)
                dve.tensor_tensor(h_lo[s][:, j, :], turn(j), h_hi[s][:, j, :].bitcast(F32), ALU.subtract).then_inc(h_lo_set, 1)

            def split(b, m):
                n, k = M * b + m, m % 2
                wait_apart(dve, gelu_set, n + 3, waited["dve"])
                wait_apart(dve, added, n + 1, waited["dve"])
                dve.tensor_copy(act_hi[k][:], act_f[k][:]).then_inc(act_hi_set, 1)
                dve.wait_ge(act_hi_set, n + 3)
                dve.tensor_tensor(act_lo[k][:], act_f[k][:], act_hi[k][:].bitcast(F32), ALU.subtract).then_inc(act_lo_set, 1)

            def sample(i, s, ahead):
                b = 2 * i + s
                dve.tensor_copy(cur[s][:], pb[:, bass.ds(b, 1), :].rearrange("p b n -> p (b n)")).then_inc(cur_set, 1)
                for m in range(M):
                    if ahead or m < M - 1:
                        split(b, m + 1)
                    if ahead and 2 <= m < 2 + T:
                        statistics(b + 1, m - 2)
                    if ahead and m == 2 + T:
                        normalise(b + 1)
                    if ahead and 9 <= m < 9 + J:
                        norm_low(1 - s, b + 1, m - 9)
                wait_apart(dve, base_ld, 16 * (b + 1), waited["dve"])
                wait_apart(dve, cur_set, b + 1, waited["dve"])
                wait_apart(dve, added, M * (b + 1) + 2, waited["dve"])
                for j in range(J):
                    dve.scalar_tensor_tensor(base[:, j, :], total(j), cur[s][:, GATE:GATE + 1], base[:, j, :], ALU.mult,
                                             ALU.add).then_inc(gated, 1)

            for t in range(T):
                statistics(0, t)
            normalise(0)
            for j in range(J):
                norm_low(0, 0, j)
            split(0, 0)
            with dve.Fori(0, PAIRS - 1) as i:
                sample(i, 0, True)
                sample(i, 1, True)
            sample(PAIRS - 1, 0, True)
            sample(PAIRS - 1, 1, False)

        @block.scalar
        def _(act):
            for n, (w, j) in enumerate(chunks):
                act.wait_ge(raw_ld[n % 3], 16 * (n // 3 + 1))
                if w == "w1":
                    part, scale = w1_hi[:, j, :], small(smalls, "gamma2", j)
                else:
                    part, scale = w2_part(w2_hi, j), 1.0
                act.activation(part, flat(stage[n % 3]), ACT.Copy, scale=scale).then_inc(w_hi_set, 1)
            act.sem_inc(gelu_set, 2)

            def tokens(b, t):
                act.wait_ge(tin_full, T * b + t + 1)
                act.activation(tok[:, t, :], turn(t), ACT.Copy).then_inc(tok_set, 1)

            def norm_high(s, b, j):
                act.wait_ge(tback_full, J * b + j + 1)
                act.activation(h_hi[s][:, j, :], turn(j), ACT.Copy).then_inc(h_hi_set, 1)

            def gelu(b, m):
                n, k = M * b + m, m % 2
                wait_apart(act, act_lo_set, n + 1, waited["act"])
                act.wait_ge(hidden_full, n + 1)
                act.activation(act_f[k][:], hidden(m), ACT.Gelu, bias=b1[:, m:m + 1]).then_inc(gelu_set, 1)

            def sample(i, s, ahead):
                b = 2 * i + s
                for m in range(M):
                    if m < M - 1:
                        gelu(b, m + 1)
                    elif ahead:
                        gelu(b + 1, 0)
                    if ahead and 2 <= m < 2 + T:
                        tokens(b + 1, m - 2)
                    if ahead and 9 <= m < 9 + J:
                        norm_high(1 - s, b + 1, m - 9)

            for t in range(T):
                tokens(0, t)
            for j in range(J):
                norm_high(0, 0, j)
            act.wait_ge(b1_set, J)
            gelu(0, 0)
            with act.Fori(0, PAIRS - 1) as i:
                sample(i, 0, True)
                sample(i, 1, True)
            sample(PAIRS - 1, 0, True)
            sample(PAIRS - 1, 1, False)

        @block.tensor
        def _(pe):
            for j in range(J):
                pe.wait_ge(raw_ld[j % 3], 16 * (j // 3 + 1))
                for m in range(M):
                    last = pe.matmul(psum[:, 0, j * M + m:j * M + m + 1], flat(stage[j % 3])[:, m * P:(m + 1) * P],
                                     small(smalls, "beta2", j), start=True, stop=True)
                last.then_inc(beta_full, 1)
            pe.sem_inc(added, 2)

            def tokens(b, t):
                if t == 0:
                    wait_apart(pe, x_ld, 16 * (b + 1), waited["pe"])
                if t >= 2:
                    wait_apart(pe, tok_set, T * b + t - 1, waited["pe"])
                for j in range(J):
                    last = pe.transpose(turn(t)[:, j * P:(j + 1) * P], x[:, j, t * P:(t + 1) * P], ident[:])
                last.then_inc(tin_full, 1)

            def back(b, j):
                if j == 0:
                    wait_apart(pe, normed, T * (b + 1), waited["pe"])
                if j >= 2:
                    wait_apart(pe, h_lo_set, J * b + j - 1, waited["pe"])
                for t in range(T):
                    last = pe.transpose(turn(j)[:, t * P:(t + 1) * P], tok[:, t, j * P:(j + 1) * P], ident[:])
                last.then_inc(tback_full, 1)

            def first_product(s, b, m):
                n, at = M * b + m, slice(m * P, (m + 1) * P)
                if m == 0:
                    wait_apart(pe, h_lo_set, J * (b + 1), waited["pe"])
                wait_apart(pe, gelu_set, n + 1, waited["pe"])
                three_pass(pe, hidden(m), [(w1_hi[:, j, at], w1_lo[:, j, at], h_hi[s][:, j, :], h_lo[s][:, j, :])
                                           for j in range(J)]).then_inc(hidden_full, 1)

            def second_product(b, m):
                n, k = M * b + m, m % 2
                wait_apart(pe, act_lo_set, n + 3, waited["pe"])
                for j in range(J):
                    if m == 0:
                        wait_apart(pe, gated, J * b + j + 1, waited["pe"])
                    at = slice(j * P, (j + 1) * P)
                    last = three_pass(pe, total(j), [(w2_hi[:, m, at], w2_lo[:, m, at], act_hi[k][:], act_lo[k][:])],
                                      start=m == 0, stop=m == M - 1)
                last.then_inc(added, 1)

            def sample(i, s, ahead):
                b = 2 * i + s
                for m in range(M):
                    if m < M - 1:
                        first_product(s, b, m + 1)
                    elif ahead:
                        first_product(1 - s, b + 1, 0)
                    second_product(b, m)
                    if ahead and 2 <= m < 2 + T:
                        tokens(b + 1, m - 2)
                    if ahead and 9 <= m < 9 + J:
                        back(b + 1, m - 9)

            for t in range(T):
                tokens(0, t)
            for j in range(J):
                back(0, j)
            pe.wait_ge(w_lo_set, len(chunks))
            pe.wait_ge(b1_set, J)
            first_product(0, 0, 0)
            with pe.Fori(0, PAIRS - 1) as i:
                sample(i, 0, True)
                sample(i, 1, True)
            sample(PAIRS - 1, 0, True)
            sample(PAIRS - 1, 1, False)


def host_arrays(x, condB_theta, condB_phi, condB_t, condB_safetyscore, condB_gatescore, **w):
    def rows_of(a):
        return a.reshape(P, J, *a.shape[1:])

    def cols_of(a):
        return np.moveaxis(a.reshape(*a.shape[:-1], P, J), -1, -2)

    def every(a):
        return np.broadcast_to(a.reshape(1, -1), (P, a.size))

    half = P // 2
    freq = np.exp(np.arange(half, dtype=np.float32) * np.float32(-np.log(10000.0) / (half - 1)))
    shift = np.zeros((P, 5 * B), np.float32)
    shift[half:, 0:B] = shift[:, 2 * B:3 * B] = shift[:, 4 * B:5 * B] = 0.25
    l1, l2, l3 = (lambda n, k=k: w[f"L{k}_cond_{n}"] for k in (1, 2, 3))
    vectors = {
        "t": every(condB_t), "theta": every(condB_theta), "phi": every(condB_phi),
        "safety": every(condB_safetyscore), "gate": every(condB_gatescore),
        "freq": np.concatenate([freq, freq])[:, None], "quarter": shift,
        "half_pi": (shift * np.float32(TWO_PI)).astype(np.float32),
        "t_b1": rows_of(l1("b1")), "t_b2": rows_of(l1("b2")), "b_sc": rows_of(l1("bsc")), "b_sh": rows_of(l1("bsh")),
        "b_in": rows_of(l1("b_in")), "b_out": rows_of(l1("b_out")), "gate_b1": l2("gate_b1")[:, None],
        "gate_w2": l2("gate_w2").T, "gate_b2": every(l2("gate_b2")), "safety_bias": rows_of(l2("safety_bias")),
        "resp_b": rows_of(l2("resp_b")), "bq": l3("bq").reshape(G, P).T, "bk": l3("bk").reshape(G, P).T,
        "bv": l3("bv").reshape(G, P).T, "bo": rows_of(l3("bo")), "b1": l3("b1").reshape(M, P).T, "b2": rows_of(l3("b2")),
        "gamma1": rows_of(l3("gamma1")), "beta1": rows_of(l3("beta1")), "gamma2": rows_of(l3("gamma2")),
        "beta2": rows_of(l3("beta2")), "row": (np.arange(P, dtype=np.float32) % R)[:, None],
    }
    of = np.arange(2 * R)
    arrays = {
        "x": x.reshape(B, S, P, J).transpose(0, 2, 3, 1),
        "smalls": np.concatenate([vectors[n] for n, _ in SMALLS], axis=1),
        "pick_index": (of[:, None] - R * (of[None, :] >= R)).astype(np.float32),
        "uv_rows": np.concatenate([cols_of(l2("U").T).reshape(R, D), cols_of(l2("V").T).reshape(R, D)]),
        "t_w1": cols_of(l1("W1")), "t_w2": rows_of(cols_of(l1("W2"))), "w_sc": rows_of(cols_of(l1("Wsc"))),
        "w_sh": rows_of(cols_of(l1("Wsh"))),
        "w_in": rows_of(l1("W_in").reshape(D, P, J).transpose(0, 2, 1).reshape(D, D)),
        "w_out": rows_of(l1("W_out").reshape(D, P, J).transpose(0, 2, 1).reshape(D, D)),
        "gamma_t": rows_of(l1("gamma").T), "beta_t": rows_of(l1("beta").T),
        "resp_w": cols_of(l2("resp_w").T).reshape(R, D), "gate_w1": rows_of(l2("gate_w1").T),
        "wq": rows_of(l3("Wq")), "wk": rows_of(l3("Wk")), "wv": rows_of(l3("Wv")),
        "wo": cols_of(l3("Wo")).reshape(G, P, D).transpose(1, 0, 2),
        "w1": rows_of(l3("W1")), "w2": cols_of(l3("W2")).reshape(M, P, D).transpose(1, 0, 2),
    }
    return {n: np.ascontiguousarray(a) for n, a in arrays.items()}


def build(nc, io):
    with ExitStack() as ctx:
        def sb(name, shape, dt=F32):
            return ctx.enter_context(nc.sbuf_tensor("k_" + name, shape, dt))

        psum = ctx.enter_context(nc.psum_tensor("psum", [P, 8, 512], F32))
        keep = {
            "smalls": sb("smalls", [P, N_SMALLS]), "ident": sb("ident", [P, P]), "ones": sb("ones", [P, DH]),
            "minus_half": sb("minus_half", [P, T]), "pa": sb("pa", [P, B, N_PA]), "pb": sb("pb", [P, B, N_PB]),
            "pooled": sb("pooled", [P, B, J]), "uo": sb("uo", [P, J, R]), "steer": sb("steer", [R, J, P]),
        }
        with ExitStack() as first:
            for n in ("w_in", "w_out"):
                for part in ("hi", "lo"):
                    keep[f"{n}_{part}"] = first.enter_context(nc.sbuf_tensor(f"k_{n}_{part}", [P, J, J, P], F32R))
            for n in ("gamma_t", "beta_t"):
                keep[n] = first.enter_context(nc.sbuf_tensor("k_" + n, [P, J, S], F32))
            setup_phase(nc, io, keep, psum)
            first_phase(nc, io, keep, psum)
        attention_phase(nc, io, keep, psum)
        feed_forward_phase(nc, io, keep, psum)


def kernel(**inputs):
    import concourse.bacc as bacc
    from concourse.bass_utils import run_bass_kernel_spmd

    nc = bacc.Bacc("TRN2", target_bir_lowering=False, num_devices=1)
    arrays = host_arrays(**{n: np.asarray(a) for n, a in inputs.items()})
    io = {n: nc.dram_tensor("in_" + n, a.shape, mybir.dt.from_np(a.dtype), kind="ExternalInput").ap()
          for n, a in arrays.items()}
    shape = (B, P, J, S)
    for n in ("x1", "mid", "base"):
        io[n] = nc.dram_tensor(n, shape, F32, kind="Internal").ap()
    io["out"] = nc.dram_tensor("out", shape, F32, kind="ExternalOutput").ap()
    build(nc, io)
    r = run_bass_kernel_spmd(nc, [{"in_" + n: a for n, a in arrays.items()}], core_ids=[0])
    return r.results[0]["out"].transpose(0, 3, 1, 2).reshape(B, S, D)
```

```python
from contextlib import ExitStack

import numpy as np

import concourse.bass as bass
import concourse.mybir as mybir
from concourse.alu_op_type import AluOpType as ALU

F32 = mybir.dt.float32
F32R = mybir.dt.float32r
ACT = mybir.ActivationFunctionType
RADD = bass.bass_isa.ReduceOp.add

P = 128
B, S, D = 8, 512, 512
J = D // P
T = S // P
H, DH = 16, 32
HG = P // DH
G = H // HG
R = 32
FF = 2048
M = FF // P
PAIRS = B // 2

LN_EPS = 1e-5
GS_EPS = 1e-8
MASKED = -1e30
INV_SQRT_DH = float(1.0 / np.sqrt(DH))

TWO_PI = 2.0 * np.pi
TWO_PI_1 = 6.28125
TWO_PI_2 = float(np.float32(np.round((TWO_PI - TWO_PI_1) * 2.0**21) / 2.0**21))
TWO_PI_3 = float(TWO_PI - TWO_PI_1 - TWO_PI_2)
ROUND = 12582912.0
SIN_MAX = 3.1415925

SMALLS = [
    ("t", B), ("theta", B), ("phi", B), ("safety", B), ("gate", B), ("freq", 1),
    ("quarter", 5 * B), ("half_pi", 5 * B), ("t_b1", J), ("t_b2", J), ("b_sc", J), ("b_sh", J),
    ("b_in", J), ("b_out", J), ("gate_b1", 1), ("gate_w2", 1), ("gate_b2", 1), ("safety_bias", J),
    ("resp_b", J), ("bq", G), ("bk", G), ("bv", G), ("bo", J), ("b1", M), ("b2", J),
    ("gamma1", J), ("beta1", J), ("gamma2", J), ("beta2", J), ("row", 1),
]
SMALL_AT, _n = {}, 0
for _name, _width in SMALLS:
    SMALL_AT[_name] = (_n, _width)
    _n += _width
N_SMALLS = _n

CT, ST_, NST, CP, SP_, NSP, SCALE, SHIFT = 0, 1, 2, 3, 4, 5, 6, 6 + J
N_PA = 6 + 2 * J
STRENGTH, GATE, GATE_1, GB2 = 0, 1, 2, 3
N_PB = 3 + J


def small(smalls, name, col=None):
    at, width = SMALL_AT[name]
    return smalls[:, at:at + width] if col is None else smalls[:, at + col:at + col + 1]


def sample_at(ap, b):
    return ap[bass.ds(b, 1), :, :, :].rearrange("b p j t -> (b p) j t")


def three_pass(pe, out, hi_lo_pairs, start=True, stop=True):
    n = len(hi_lo_pairs)
    for k, (w_hi, w_lo, x_hi, x_lo) in enumerate(hi_lo_pairs):
        pe.matmul(out, w_hi, x_hi, start=start and k == 0, stop=False)
        pe.matmul(out, w_hi, x_lo, start=False, stop=False)
        last = pe.matmul(out, w_lo, x_hi, start=False, stop=stop and k == n - 1)
    return last


def wait_apart(eng, sem, value, waited):
    eng.wait_ge(sem, value)
    eng.sem_inc(waited, 1)


def clear_semaphores(nc, sems):
    with nc.Block() as block:
        @block.gpsimd
        def _(pool):
            for sem in sems:
                pool.sem_clear(sem)
    for sem in sems:
        nc.release_semaphore(sem)


def setup_phase(nc, io, keep, psum):
    smalls, ident, pa = keep["smalls"], keep["ident"], keep["pa"]
    with ExitStack() as ctx:
        def sb(name, shape, dt=F32):
            return ctx.enter_context(nc.sbuf_tensor(name, shape, dt))

        sems = []

        def sem(name):
            sems.append(nc.alloc_semaphore(name))
            return sems[-1]

        ctx.callback(clear_semaphores, nc, sems)
        angle = sb("angle", [P, 5 * B])
        turns = sb("turns", [P, 5 * B])
        sines = sb("sines", [P, 5 * B])
        wt1 = sb("wt1", [P, J, P])
        wt2 = sb("wt2", [P, J, J, P])
        wsc = sb("wsc", [P, J, J, P])
        wsh = sb("wsh", [P, J, J, P])
        h1 = sb("t_h1", [P, J, B])
        h2 = sb("t_h2", [P, J, B])
        raw_in = sb("raw_in", [P, J, D])
        raw_out = sb("raw_out", [P, J, D])
        rows = sb("gs_rows", [2 * R, S])
        prod = sb("gs_prod", [2 * R, S])
        pick_index = sb("gs_pick_index", [2 * R, 2 * R])
        pick = sb("gs_pick", [2 * R, 2 * R])
        step_no = sb("gs_step", [2 * R, 1])
        later = sb("gs_later", [2 * R, 1])
        dots = sb("gs_dots", [2 * R, 1])
        norm = sb("gs_norm", [2 * R, 1])
        inv = sb("gs_inv", [2 * R, 1])
        coef = sb("gs_coef", [2 * R, 1])
        uv = sb("gs_uv", [P, J, 2 * R])
        u_head = sb("u_head", [R, R])
        gram = sb("gram", [R, R])
        mix = sb("mix", [R, R])
        resp_w = sb("resp_w", [R, D])

        small_ld = sem("small_ld")
        tw_ld = sem("tw_ld")
        win_ld = sem("win_ld")
        gs_ld = sem("gs_ld")
        rw_ld = sem("rw_ld")
        ident_made = sem("ident_made")
        angles = sem("angles")
        sines_made = sem("sines_made")
        t_full = sem("t_full")
        t_done = sem("t_done")
        pa_made = sem("pa_made")
        split_hi = sem("split_hi")
        split_lo = sem("split_lo")
        gs_ready = sem("gs_ready")
        gs_row = sem("gs_row")
        gs_dots = sem("gs_dots_done")
        gs_sq = sem("gs_sq")
        gs_norm = sem("gs_norm_done")
        gs_small = sem("gs_small")
        fin_pe = sem("fin_pe")
        fin_dve = sem("fin_dve")
        fin_act = sem("fin_act")

        waited = sem("gs_waited")

        block = ctx.enter_context(nc.Block())

        @block.sync
        def _(sp):
            sp.dma_start(smalls[:], io["smalls"]).then_inc(small_ld, 16)
            sp.dma_start(rows[:], io["uv_rows"]).then_inc(gs_ld, 16)
            sp.dma_start(pick_index[:], io["pick_index"]).then_inc(gs_ld, 16)
            sp.dma_start(wt1[:], io["t_w1"]).then_inc(tw_ld, 16)
            sp.dma_start(wt2[:], io["t_w2"]).then_inc(tw_ld, 16)
            sp.dma_start(wsc[:], io["w_sc"]).then_inc(tw_ld, 16)
            sp.dma_start(wsh[:], io["w_sh"]).then_inc(tw_ld, 16)
            sp.dma_start(raw_in[:], io["w_in"]).then_inc(win_ld, 16)
            sp.dma_start(raw_out[:], io["w_out"]).then_inc(win_ld, 16)
            sp.dma_start(keep["gamma_t"][:], io["gamma_t"]).then_inc(rw_ld, 16)
            sp.dma_start(keep["beta_t"][:], io["beta_t"]).then_inc(rw_ld, 16)
            sp.dma_start(resp_w[:], io["resp_w"]).then_inc(rw_ld, 16)

        @block.gpsimd
        def _(pool):
            pool.memset(ident[:], 0.0).then_inc(ident_made, 1)
            pool.memset(keep["ones"][:], 1.0)
            pool.memset(keep["minus_half"][:], -0.5)
            pool.memset(step_no[:], 0.0).then_inc(ident_made, 1)
            pool.wait_ge(ident_made, 2)
            pool.affine_select(out=ident[:], in_=ident[:], compare_op=ALU.not_equal, fill=1.0, base=0,
                               pattern=[[-1, P]], channel_multiplier=1).then_inc(ident_made, 1)

        @block.vector
        def _(dve):
            done = [0]

            def chain(ins):
                done[0] += 1
                ins.then_inc(angles, 1)
                dve.wait_ge(angles, done[0])

            dve.wait_ge(small_ld, 16)
            dve.tensor_scalar(angle[:, 0:B], small(smalls, "t"), 5000.0, small(smalls, "freq"), ALU.mult, ALU.mult)
            dve.tensor_copy(angle[:, B:2 * B], small(smalls, "theta"))
            dve.tensor_copy(angle[:, 2 * B:3 * B], small(smalls, "theta"))
            dve.tensor_copy(angle[:, 3 * B:4 * B], small(smalls, "phi"))
            chain(dve.tensor_copy(angle[:, 4 * B:5 * B], small(smalls, "phi")))
            chain(dve.scalar_tensor_tensor(turns[:], angle[:], 1.0 / TWO_PI, small(smalls, "quarter"), ALU.mult, ALU.add))
            chain(dve.tensor_scalar(turns[:], turns[:], ROUND, None, ALU.add))
            chain(dve.tensor_scalar(turns[:], turns[:], -ROUND, None, ALU.add))
            for part in (TWO_PI_1, TWO_PI_2, TWO_PI_3):
                chain(dve.scalar_tensor_tensor(angle[:], turns[:], -part, angle[:], ALU.mult, ALU.add))
            chain(dve.tensor_tensor(angle[:], angle[:], small(smalls, "half_pi"), ALU.add))
            chain(dve.tensor_scalar(angle[:], angle[:], SIN_MAX, -SIN_MAX, ALU.min, ALU.max))
            dve.wait_ge(sines_made, 1)
            sine = lambda k: sines[:, k * B:(k + 1) * B]
            dve.tensor_copy(pa[:, :, ST_], sine(1))
            dve.tensor_scalar(pa[:, :, NST], sine(1), -1.0, None, ALU.mult)
            dve.tensor_copy(pa[:, :, CT], sine(2))
            dve.tensor_copy(pa[:, :, SP_], sine(3))
            dve.tensor_scalar(pa[:, :, NSP], sine(3), -1.0, None, ALU.mult)
            dve.tensor_copy(pa[:, :, CP], sine(4)).then_inc(pa_made, 1)
            dve.wait_ge(win_ld, 32)
            for n, (raw, w) in enumerate(((raw_in, "w_in"), (raw_out, "w_out"))):
                for j in range(J):
                    dve.wait_ge(split_hi, J * n + j + 1)
                    dve.tensor_tensor(keep[w + "_lo"][:, j, :, :].rearrange("p a k -> p (a k)"), raw[:, j, :],
                                      keep[w + "_hi"][:, j, :, :].rearrange("p a k -> p (a k)").bitcast(F32),
                                      ALU.subtract).then_inc(split_lo, 1)
            dve.wait_ge(gs_ld, 32)
            dve.wait_ge(ident_made, 3)
            dve.tensor_scalar(pick[:], pick_index[:], step_no[:, 0:1], None, ALU.is_equal).then_inc(gs_ready, 1)
            with dve.Fori(0, R) as i:
                dve.wait_ge(gs_ready, i + 1)
                dve.tensor_scalar(later[:], small(smalls, "row")[0:2 * R, :], step_no[:, 0:1], -1.0, ALU.is_gt,
                                  ALU.mult).then_inc(gs_small, 1)
                dve.wait_ge(gs_small, i * 7 + 1)
                dve.tensor_scalar(step_no[:], step_no[:], 1.0, None, ALU.add).then_inc(gs_small, 1)
                dve.wait_ge(gs_row, i + 1)
                dve.tensor_tensor_reduce(prod[:], psum[0:2 * R, 0, :], rows[:], 1.0, 0.0, ALU.mult, ALU.add,
                                         dots[:]).then_inc(gs_dots, 1)
                dve.wait_ge(gs_norm, i + 1)
                dve.tensor_scalar(norm[:], norm[:], GS_EPS, None, ALU.add).then_inc(gs_small, 1)
                dve.wait_ge(gs_small, i * 7 + 3)
                dve.reciprocal(inv[:], norm[:]).then_inc(gs_small, 1)
                dve.wait_ge(gs_small, i * 7 + 4)
                dve.tensor_scalar(coef[:], dots[:], inv[:, 0:1], inv[:, 0:1], ALU.mult, ALU.mult).then_inc(gs_small, 1)
                dve.wait_ge(gs_small, i * 7 + 5)
                dve.tensor_scalar(coef[:], coef[:], later[:, 0:1], None, ALU.mult).then_inc(gs_small, 1)
                dve.wait_ge(gs_small, i * 7 + 6)
                dve.scalar_tensor_tensor(rows[:], psum[0:2 * R, 0, :], coef[:, 0:1], rows[:], ALU.mult,
                                         ALU.add).then_inc(gs_small, 1)
                dve.wait_ge(gs_small, i * 7 + 7)
                dve.tensor_scalar(pick[:], pick_index[:], step_no[:, 0:1], None, ALU.is_equal).then_inc(gs_ready, 1)
            dve.tensor_tensor_reduce(prod[:], rows[:], rows[:], 1.0, 0.0, ALU.mult, ALU.add, dots[:]).then_inc(fin_dve, 1)
            dve.wait_ge(fin_act, 1)
            dve.tensor_scalar(norm[:], norm[:], GS_EPS, None, ALU.add).then_inc(fin_dve, 1)
            dve.wait_ge(fin_dve, 2)
            dve.reciprocal(inv[:], norm[:]).then_inc(fin_dve, 1)
            dve.wait_ge(fin_dve, 3)
            dve.tensor_scalar(rows[:], rows[:], inv[:, 0:1], None, ALU.mult).then_inc(fin_dve, 1)
            dve.wait_ge(fin_dve, 4)
            dve.tensor_copy(u_head[:].rearrange("r (k j) -> r k j", j=J),
                            rows[0:R, :].rearrange("r (j k) -> r k j", j=J)[:, 0:R // J, :]).then_inc(fin_dve, 1)
            dve.wait_ge(fin_pe, 1)
            dve.tensor_copy(uv[:].rearrange("p j r -> p (j r)"), psum[:, 0, 0:J * 2 * R]).then_inc(fin_dve, 1)
            dve.wait_ge(fin_dve, 6)
            dve.tensor_copy(keep["uo"][:], uv[:, :, 0:R]).then_inc(fin_dve, 1)
            dve.wait_ge(fin_pe, 2)
            dve.tensor_copy(gram[:], psum[0:R, 1, 0:R]).then_inc(fin_dve, 1)
            dve.wait_ge(fin_pe, 3)
            dve.tensor_copy(mix[:], psum[0:R, 2, 0:R]).then_inc(fin_dve, 1)
            dve.wait_ge(fin_pe, 4)
            dve.tensor_copy(keep["steer"][0:R, :, :].rearrange("r j k -> r (j k)"), psum[0:R, 3, :]).then_inc(fin_dve, 1)

        @block.scalar
        def _(act):
            act.wait_ge(angles, 9)
            act.activation(sines[:], angle[:], ACT.Sin).then_inc(sines_made, 1)
            act.wait_ge(t_full, 1)
            for j in range(J):
                ins = act.activation(h1[:, j, :], psum[:, 4, j * B:(j + 1) * B], ACT.Silu, bias=small(smalls, "t_b1", j))
            ins.then_inc(t_done, 1)
            act.wait_ge(t_full, 2)
            for j in range(J):
                ins = act.activation(h2[:, j, :], psum[:, 5, j * B:(j + 1) * B], ACT.Identity, bias=small(smalls, "t_b2", j))
            ins.then_inc(t_done, 1)
            act.wait_ge(t_full, 3)
            for j in range(J):
                act.activation(pa[:, :, SCALE + j], psum[:, 6, j * B:(j + 1) * B], ACT.Identity, bias=small(smalls, "b_sc", j))
                ins = act.activation(pa[:, :, SHIFT + j], psum[:, 7, j * B:(j + 1) * B], ACT.Identity,
                                     bias=small(smalls, "b_sh", j))
            ins.then_inc(pa_made, 1)
            act.wait_ge(win_ld, 32)
            for raw, w in ((raw_in, "w_in"), (raw_out, "w_out")):
                for j in range(J):
                    act.activation(keep[w + "_hi"][:, j, :, :].rearrange("p a k -> p (a k)"), raw[:, j, :],
                                   ACT.Copy).then_inc(split_hi, 1)
            with act.Fori(0, R) as i:
                act.wait_ge(gs_sq, i + 1)
                act.activation(norm[:], psum[0:2 * R, 1, 0:1], ACT.Sqrt).then_inc(gs_norm, 1)
            act.wait_ge(fin_dve, 1)
            act.activation(norm[:], dots[:], ACT.Sqrt).then_inc(fin_act, 1)

        @block.tensor
        def _(pe):
            pe.wait_ge(tw_ld, 64)
            pe.wait_ge(sines_made, 1)
            for j in range(J):
                last = pe.matmul(psum[:, 4, j * B:(j + 1) * B], wt1[:, j, :], sines[:, 0:B], start=True, stop=True)
            last.then_inc(t_full, 1)
            pe.wait_ge(t_done, 1)
            for jo in range(J):
                for j in range(J):
                    last = pe.matmul(psum[:, 5, jo * B:(jo + 1) * B], wt2[:, j, jo, :], h1[:, j, :], start=(j == 0), stop=(j == J - 1))
            last.then_inc(t_full, 1)
            pe.wait_ge(t_done, 2)
            for k, w in ((6, wsc), (7, wsh)):
                for jo in range(J):
                    for j in range(J):
                        last = pe.matmul(psum[:, k, jo * B:(jo + 1) * B], w[:, j, jo, :], h2[:, j, :], start=(j == 0), stop=(j == J - 1))
            last.then_inc(t_full, 1)
            with pe.Fori(0, R) as i:
                wait_apart(pe, gs_ready, i + 1, waited)
                pe.matmul(psum[0:2 * R, 0, :], pick[:], rows[:], start=True, stop=True).then_inc(gs_row, 1)
                wait_apart(pe, gs_dots, i + 1, waited)
                pe.matmul(psum[0:2 * R, 1, 0:1], pick[:], dots[:], start=True, stop=True).then_inc(gs_sq, 1)
            pe.wait_ge(fin_dve, 5)
            pe.wait_ge(ident_made, 3)
            for j in range(J):
                last = pe.transpose(psum[:, 0, j * 2 * R:(j + 1) * 2 * R], rows[:, j * P:(j + 1) * P], ident[0:2 * R, 0:2 * R])
            last.then_inc(fin_pe, 1)
            pe.wait_ge(fin_dve, 7)
            for j in range(J):
                last = pe.matmul(psum[0:R, 1, 0:R], uv[:, j, R:2 * R], uv[:, j, R:2 * R], start=(j == 0), stop=(j == J - 1))
            last.then_inc(fin_pe, 1)
            pe.wait_ge(fin_dve, 8)
            pe.matmul(psum[0:R, 2, 0:R], u_head[:], gram[:], start=True, stop=True).then_inc(fin_pe, 1)
            pe.wait_ge(fin_dve, 9)
            pe.wait_ge(rw_ld, 48)
            pe.matmul(psum[0:R, 3, :], mix[:], resp_w[:], start=True, stop=True).then_inc(fin_pe, 1)


def first_phase(nc, io, keep, psum):
    pa, smalls = keep["pa"], keep["smalls"]
    with ExitStack() as ctx:
        def sb(name, shape, dt=F32):
            return [ctx.enter_context(nc.sbuf_tensor(f"{name}{s}", shape, dt)) for s in range(2)]

        sems = []

        def sem(name):
            pair = [nc.alloc_semaphore(f"{name}{s}") for s in range(2)]
            sems.extend(pair)
            return pair

        ctx.callback(clear_semaphores, nc, sems)

        x_in = sb("a_x", [P, J, S])
        rot = sb("a_rot", [P, J, S])
        z = sb("a_z", [P, J, S])
        hi = sb("a_hi", [P, J, S], F32R)
        lo = sb("a_lo", [P, J, S], F32R)
        res = sb("a_res", [P, J, S])
        cur = sb("a_cur", [P, N_PA])
        stats = sb("a_stats", [P, J, 6])
        mv = sb("a_mv", [P, 2])
        total = sb("a_total", [P, 1])
        spread = sb("a_spread", [P, 1])
        spread_sum = sb("a_spread_sum", [P, 1])
        away = sb("a_away", [P, 1])
        inv = sb("a_inv", [P, 1])
        nmean = sb("a_nmean", [P, 1])
        tok_sum = sb("a_tok_sum", [P, J])

        x_ld = sem("a_x_ld")
        x_used = sem("a_x_used")
        cur_set = sem("a_cur_set")
        cross = sem("a_cross")
        rotated = sem("a_rotated")
        stat = sem("a_stat")
        part_mv = sem("a_part_mv")
        mean_sum = sem("a_mean_sum")
        away_set = sem("a_away_set")
        spread_set = sem("a_spread_set")
        var_sum = sem("a_var_sum")
        var_set = sem("a_var_set")
        inv_set = sem("a_inv_set")
        nmean_set = sem("a_nmean_set")
        normed = sem("a_normed")
        scaled = sem("a_scaled")
        shifted = sem("a_shifted")
        silu = sem("a_silu")
        hi_set = sem("a_hi_set")
        lo_set = sem("a_lo_set")
        product = sem("a_product")
        biased = sem("a_biased")
        result = sem("a_result")
        pooled_set = sem("a_pooled_set")
        stored = sem("a_stored")

        dve_waited = ctx.enter_context(nc.semaphore("a_dve_waited"))
        pool_waited = ctx.enter_context(nc.semaphore("a_pool_waited"))

        x_dram, x1_dram = io["x"], io["x1"]
        bank = lambda s, j: psum[:, 4 * s + j, :]
        block = ctx.enter_context(nc.Block())

        @block.sync
        def _(sp):
            def load(s, q):
                sp.dma_start(x_in[s][:], sample_at(x_dram, 2 * q + s)).then_inc(x_ld[s], 16)

            def store(s, q):
                sp.wait_ge(result[s], 4 * q + 4)
                sp.dma_start(sample_at(x1_dram, 2 * q + s), res[s][:]).then_inc(stored[s], 16)

            for s in range(2):
                sp.sem_inc(stored[s], 16)
                load(s, 0)
            with sp.Fori(0, PAIRS - 1) as q:
                for s in range(2):
                    sp.wait_ge(x_used[s], q + 1)
                    load(s, q + 1)
                for s in range(2):
                    store(s, q)
            for s in range(2):
                store(s, PAIRS - 1)
            for s in range(2):
                sp.wait_ge(stored[s], 16 * (PAIRS + 1))

        @block.gpsimd
        def _(pool):
            def sums(s, q, st):
                n = 2 * q + st + 1
                wait_apart(pool, part_mv[s], n, pool_waited)
                pool.partition_all_reduce(total[s][:], mv[s][:, 0:1], P, RADD).then_inc(mean_sum[s], 1)
                wait_apart(pool, spread_set[s], n, pool_waited)
                pool.partition_all_reduce(spread_sum[s][:], spread[s][:], P, RADD).then_inc(var_sum[s], 1)
                wait_apart(pool, var_sum[s], n, pool_waited)
                pool.tensor_scalar(spread_sum[s][:], spread_sum[s][:], 1.0 / P, LN_EPS, ALU.mult, ALU.add).then_inc(var_set[s], 1)
                wait_apart(pool, var_set[s], n, pool_waited)
                pool.tensor_tensor(inv[s][:], spread_sum[s][:], keep["minus_half"][:, 0:1], ALU.pow).then_inc(inv_set[s], 1)
                for j in range(J):
                    pool.wait_ge(scaled[s], 8 * q + 4 * st + j + 1)
                    pool.tensor_tensor(z[s][:, j, :], z[s][:, j, :], keep["beta_t"][:, j, :],
                                       ALU.add).then_inc(shifted[s], 1)

            for s in range(2):
                sums(s, 0, 0)
            with pool.Fori(0, PAIRS - 1) as q:
                for s in range(2):
                    sums(s, q, 1)
                for s in range(2):
                    sums(s, q + 1, 0)
            for s in range(2):
                sums(s, PAIRS - 1, 1)

        @block.vector
        def _(dve):
            def rotate(s, q):
                b = 2 * q + s
                dve.tensor_copy(cur[s][:], pa[:, bass.ds(b, 1), :].rearrange("p b n -> p (b n)")).then_inc(cur_set[s], 1)
                dve.wait_ge(x_ld[s], 16 * (q + 1))
                dve.wait_ge(cur_set[s], q + 1)
                for j in range(J):
                    dve.wait_ge(cross[s], 4 * q + j + 1)
                    c = CT if j < 2 else CP
                    last = dve.scalar_tensor_tensor(rot[s][:, j, :], x_in[s][:, j, :], cur[s][:, c:c + 1], z[s][:, j, :],
                                                    ALU.mult, ALU.add).then_inc(rotated[s], 1)
                dve.wait_ge(rotated[s], 4 * q + 4)
                dve.sem_inc(x_used[s], 1)

            def norm(s, q, st):
                n = 2 * q + st + 1
                src = rot[s] if st == 0 else z[s]
                for j in range(J):
                    if st:
                        dve.wait_ge(biased[s], 4 * q + j + 1)
                    dve.bn_stats(stats[s][:, j, :], src[:, j, :]).then_inc(stat[s], 1)
                wait_apart(dve, stat[s], 4 * n, dve_waited)
                dve.bn_aggr(mv[s][:], stats[s][:].rearrange("p j n -> p (j n)")).then_inc(part_mv[s], 1)
                dve.wait_ge(mean_sum[s], n)
                dve.scalar_tensor_tensor(away[s][:], total[s][:], -1.0 / P, mv[s][:, 0:1], ALU.mult,
                                         ALU.add).then_inc(away_set[s], 1)
                dve.wait_ge(away_set[s], n)
                dve.scalar_tensor_tensor(spread[s][:], away[s][:], away[s][:, 0:1], mv[s][:, 1:2], ALU.mult,
                                         ALU.add).then_inc(spread_set[s], 1)
                dve.wait_ge(inv_set[s], n)
                dve.scalar_tensor_tensor(nmean[s][:], total[s][:], -1.0 / P, inv[s][:], ALU.mult,
                                         ALU.mult).then_inc(nmean_set[s], 1)
                for j in range(J):
                    dve.wait_ge(normed[s], 8 * q + 4 * st + j + 1)
                    dve.tensor_tensor(z[s][:, j, :], z[s][:, j, :], keep["gamma_t"][:, j, :],
                                      ALU.mult).then_inc(scaled[s], 1)
                for j in range(J):
                    dve.wait_ge(hi_set[s], 8 * q + 4 * st + j + 1)
                    dve.tensor_tensor(lo[s][:, j, :], z[s][:, j, :], hi[s][:, j, :].bitcast(F32),
                                      ALU.subtract).then_inc(lo_set[s], 1)

            def finish(s, q):
                b = 2 * q + s
                dve.wait_ge(stored[s], 16 * (q + 1))
                for j in range(J):
                    dve.wait_ge(product[s], 8 * q + 4 + j + 1)
                    dve.scalar_tensor_tensor(res[s][:, j, :], bank(s, j), small(smalls, "b_out", j), rot[s][:, j, :],
                                             ALU.add, ALU.add, accum_out=tok_sum[s][:, j:j + 1]).then_inc(result[s], 1)
                dve.wait_ge(result[s], 4 * q + 4)
                dve.tensor_copy(keep["pooled"][:, bass.ds(b, 1), :].rearrange("p b j -> p (b j)"),
                                tok_sum[s][:]).then_inc(pooled_set[s], 1)

            for s in range(2):
                rotate(s, 0)
                norm(s, 0, 0)
            with dve.Fori(0, PAIRS - 1) as q:
                norm(0, q, 1)
                norm(1, q, 1)
                for s in range(2):
                    finish(s, q)
                    rotate(s, q + 1)
                    norm(s, q + 1, 0)
            for s in range(2):
                norm(s, PAIRS - 1, 1)
            for s in range(2):
                finish(s, PAIRS - 1)

        @block.scalar
        def _(act):
            def crosses(s, q):
                act.wait_ge(x_ld[s], 16 * (q + 1))
                act.wait_ge(cur_set[s], q + 1)
                for j, c in enumerate((ST_, NST, SP_, NSP)):
                    act.activation(z[s][:, j, :], x_in[s][:, j ^ 1, :], ACT.Copy,
                                   scale=cur[s][:, c:c + 1]).then_inc(cross[s], 1)

            def norm(s, q, st):
                n = 2 * q + st + 1
                at = 8 * q + 4 * st
                src = rot[s] if st == 0 else z[s]
                if st:
                    for j in range(J):
                        act.wait_ge(product[s], 8 * q + j + 1)
                        act.activation(z[s][:, j, :], bank(s, j), ACT.Identity,
                                       bias=small(smalls, "b_in", j)).then_inc(biased[s], 1)
                act.wait_ge(nmean_set[s], n)
                for j in range(J):
                    act.activation(z[s][:, j, :], src[:, j, :], ACT.Identity, bias=nmean[s][:, 0:1],
                                   scale=inv[s][:, 0:1]).then_inc(normed[s], 1)
                for j in range(J):
                    act.wait_ge(shifted[s], at + j + 1)
                    act.activation(z[s][:, j, :], z[s][:, j, :], ACT.Silu, bias=cur[s][:, SHIFT + j:SHIFT + j + 1],
                                   scale=cur[s][:, SCALE + j:SCALE + j + 1]).then_inc(silu[s], 1)
                for j in range(J):
                    act.wait_ge(silu[s], at + j + 1)
                    act.activation(hi[s][:, j, :], z[s][:, j, :], ACT.Copy).then_inc(hi_set[s], 1)

            for s in range(2):
                crosses(s, 0)
                norm(s, 0, 0)
            with act.Fori(0, PAIRS - 1) as q:
                norm(0, q, 1)
                norm(1, q, 1)
                for s in range(2):
                    act.wait_ge(product[s], 8 * q + 8)
                    crosses(s, q + 1)
                    norm(s, q + 1, 0)
            for s in range(2):
                norm(s, PAIRS - 1, 1)

        @block.tensor
        def _(pe):
            def multiply(s, q, st, w):
                w_hi, w_lo = keep[w + "_hi"], keep[w + "_lo"]
                pe.wait_ge(lo_set[s], 8 * q + 4 * st + J)
                for jo in range(J):
                    three_pass(pe, bank(s, jo), [(w_hi[:, j, jo, :], w_lo[:, j, jo, :], hi[s][:, j, :], lo[s][:, j, :])
                                                 for j in range(J)]).then_inc(product[s], 1)

            with pe.Fori(0, PAIRS) as q:
                for s in range(2):
                    multiply(s, q, 0, "w_in")
                for s in range(2):
                    multiply(s, q, 1, "w_out")


class Ring:

    def __init__(self, start, names, per_round):
        self.at = {name: ((start + k) % 2, (start + k) // 2) for k, name in enumerate(names)}
        self.per_round = per_round

    def bank(self, name):
        return self.at[name][0]

    def full(self, name, n=0):
        return n * self.per_round + self.at[name][1] + 1

    def free(self, name, n=0):
        return n * self.per_round + self.at[name][1]


def before_names(s):
    return ([(s, "p")] + [(s, "resp", j) for j in range(J)] + [(s, "tin", t) for t in range(T)]
            + [(s, "tback", j) for j in range(J)] + [(s, n, g) for g in range(2) for n in "qk"])


def front_names(s, previous, ahead):
    qk = lambda g: [(s, "q", g), (s, "k", g)]
    p, resp, tin = (before_names(1 - s)[a:e] if ahead else [] for a, e in ((0, 1), (1, 1 + J), (1 + J, 1 + J + T)))
    wo = [(1 - s, "wo", j) for j in range(J) if previous]
    return qk(2) + [(s, "v", t) for t in range(T)] + qk(3) + p + resp + wo[:J // 2] + tin + wo[J // 2:]


def back_names(s):
    return before_names(1 - s)[1 + J + T:]


U_TILES = ((T - 1,), (T - 2, 0), (1,))
UNITS = HG * len(U_TILES)
ROWS_AT, EXP_AT = 1, 6
EXP_STEPS = 2 * T
LAST_AT = 3
S_NAMES = [n for g in range(G + 1) for n in
           [(g, u) for u in range(ROWS_AT + 1) if g < G] + [(g - 1, UNITS)] * (g > 0)
           + [(g, u) for u in range(ROWS_AT + 1, UNITS) if g < G]]

STACK_AT = {(0, 0): (0, 0), (0, 1): (1, 0), (0, 2): (2, 0), (0, 3): (0, 1),
            (1, 0): (1, 1), (1, 1): (0, 2), (1, 2): (2, 1), (1, 3): (1, 2)}
STACK_USES = (3, 3, 2)
STACK_DMAS = (12, 12, 13)


def stack_count(i, s, g):
    place, use = STACK_AT[s, g]
    return 16 * STACK_DMAS[place] * (STACK_USES[place] * i + use + 1)


def attention_phase(nc, io, keep, psum):
    smalls, ident, pb, pooled = keep["smalls"], keep["ident"], keep["pb"], keep["pooled"]
    with ExitStack() as ctx:
        def sb(name, shape, dt=F32):
            return ctx.enter_context(nc.sbuf_tensor("b_" + name, shape, dt))

        def sem(name):
            return ctx.enter_context(nc.semaphore("b_" + name))

        w_hi = {n: sb(n + "_hi", [P, J, D], F32R) for n in ("wq", "wk", "wv", "wo")}
        w_lo = {n: sb(n + "_lo", [P, J, D], F32R) for n in ("wq", "wk", "wv", "wo")}
        xb = [sb(f"x{s}", [P, J, S]) for s in range(2)]
        tok = sb("tok", [P, J, S])
        xhl = sb("xhl", [P, 2 * J, S], F32R)
        xh, xl = xhl[:, 0:J, :], xhl[:, J:2 * J, :]
        v = sb("v", [P, T, D])
        qk4 = [sb("qk4", [P, 4, S]), tok]
        stack = [sb(f"stack{n}", [P, 2 * HG, S], F32R) for n in range(2)] + [xhl]
        pt = [sb(f"pt{n}", [P, HG, S]) for n in range(2)]
        ctxs = sb("ctxs", [P, S])
        sums = sb("sums", [P, S])
        ch = sb("ch", [P, G + 1, S], F32R)
        cl = sb("cl", [P, G + 1, S], F32R)
        context_at = lambda s, g: G if (s, g) == (1, 0) else g
        psb = sb("p", [R + 1, S])
        mr = [sb(f"mr{n}", [2 * HG, S], F32R) for n in range(2)]
        mask = sb("mask", [P, S])
        mx = [sb(f"mx{n}", [P, T, HG]) for n in range(2)]
        nm = sb("nm", [P, T, HG, 2], F32R)
        st = sb("st", [P, T, 6])
        mv = sb("mv", [P, T, 2])
        var = sb("var", [P, T])
        rstd = sb("rstd", [P, T])
        cur = [sb(f"cur{s}", [P, N_PB]) for s in range(2)]
        gate_w1 = ctxs[:].rearrange("p (j k) -> p j k", j=J)
        gate_h = sb("gate_h", [P, B])
        gate_w2 = sums[:, 0:P]
        strength = sb("strength", [P, B])
        mod = sb("mod", [P, B])
        rbias = sb("rbias", [R + 1, D])
        bias = sb("bias", [P, 3, G])
        staged = (("wq", v), ("wk", xb[1]), ("wv", pt[0]), ("wo", pt[1]))

        raw_ld = [sem(f"raw_ld{n}") for n in range(4)]
        gw_ld = sem("gw_ld")
        w_hi_set, w_lo_set = sem("w_hi_set"), sem("w_lo_set")
        gate_full, gate_act, gate_dve = sem("gate_full"), sem("gate_act"), sem("gate_dve")
        beta_full, beta_set = sem("beta_full"), sem("beta_set")
        rows_made, mask_made = sem("rows_made"), sem("mask_made")
        x_ld = [sem(f"x_ld{s}") for s in range(2)]
        x2_st = [sem(f"x2_st{s}") for s in range(2)]
        d_st = [sem(f"d_st{s}") for s in range(2)]
        row_ld = sem("row_ld")
        pj_full = [sem(f"pj_full{k}") for k in range(2)]
        pj_free = [sem(f"pj_free{k}") for k in range(2)]
        s_full = [sem(f"s_full{k}") for k in range(2)]
        s_free = [sem(f"s_free{k}") for k in range(2)]
        e_full = [sem(f"e_full{k}") for k in range(2)]
        e_free = [sem(f"e_free{k}") for k in range(2)]
        cur_set = sem("cur_set")
        stat_set, mv_set = sem("stat_set"), sem("mv_set")
        var_set, rstd_set, normed = sem("var_set"), sem("rstd_set"), sem("normed")
        xh_set, qk_hi = sem("xh_set"), sem("qk_hi")
        stack_ld = [sem(f"stack_ld{n}") for n in range(3)]
        nm_hi, nm_lo, mr_set = sem("nm_hi"), sem("nm_lo"), sem("mr_set")
        mr_ld = [sem(f"mr_ld{n}") for n in range(4)]
        masked, pv_done, ctx_free = sem("masked"), sem("pv_done"), sem("ctx_free")
        rec_set, ctxn_set, ch_set, cl_set = sem("rec_set"), sem("ctxn_set"), sem("ch_set"), sem("cl_set")
        waited = {e: sem("waited_" + e) for e in ("dve", "act", "pool", "pe", "sp")}

        pj = lambda k: psum[:, k, :]
        sc = lambda k: psum[:, 2 + k, :]
        ex = lambda k: psum[:, 4 + k, :]
        ctx_bank, sum_bank = psum[:, 6, :], psum[:, 7, :]

        first = before_names(0) + front_names(0, False, True)
        lead = len(first)
        round_names = back_names(0) + front_names(1, True, True) + back_names(1) + front_names(0, True, True)
        last_names = back_names(0) + front_names(1, True, False) + [(1, "wo", j) for j in range(J)]
        per_round = len(round_names) // 2
        prologue = Ring(0, first, 0)
        steady = Ring(lead, round_names, per_round)
        final = Ring(lead, last_names, per_round)
        s_ring = Ring(0, S_NAMES, len(S_NAMES) // 2)
        e_ring = Ring(0, [(g, j, h) for g in range(G) for j in range(T) for h in range(HG)], G * T * HG // 2)

        def wait_freed(eng, name, ring, i, use):
            wait_apart(eng, pj_free[ring.bank(use)], ring.full(use, i), waited[name])

        def wait_before(eng, name, ring, i, use):
            wait_apart(eng, pj_free[ring.bank(use)], ring.free(use, i), waited[name])

        def exp_heads(half):
            return range(HG // 2 * half, HG // 2 * (half + 1))

        block = ctx.enter_context(nc.Block())

        @block.sync
        def _(sp):
            sp.dma_start(gate_w1, io["gate_w1"]).then_inc(gw_ld, 16)
            sp.dma_start(xb[0][:], sample_at(io["x1"], 0)).then_inc(x_ld[0], 16)
            sp.dma_start(rbias[R:R + 1, :], io["resp_b_row"]).then_inc(row_ld, 16)
            sp.dma_start(keep["steer"][R:R + 1, :, :], io["safety_bias_row"]).then_inc(row_ld, 16)
            for n, (w, where) in enumerate(staged):
                sp.dma_start(where[:], io[w]).then_inc(raw_ld[n], 16)
            sp.sem_inc(d_st[0], 16)
            sp.sem_inc(d_st[1], 16)

            def stack_rows(ring, i, s, g):
                for n in "qk":
                    wait_freed(sp, "sp", ring, i, (s, n, g))
                place = STACK_AT[s, g][0]
                for h in range(HG):
                    for row, (a, step) in enumerate(((1, 1), (0, 2), (1, 2))):
                        sp.dma_start(stack[place][row * DH:(row + 1) * DH, 2 * h:2 * h + 2, :].bitcast(F32),
                                     qk4[g % 2][h * DH:(h + 1) * DH, a:a + step + 1:step, :]
                                     ).then_inc(stack_ld[place], 16)

            def max_rows(s, g, b):
                place = STACK_AT[s, g][0]
                wait_apart(sp, mr_set, G * b + g + 1, waited["sp"])
                for h in range(HG):
                    sp.dma_start(stack[place][3 * DH:3 * DH + 2, 2 * h, :].bitcast(F32),
                                 mr[g % 2][2 * h:2 * h + 2, :].bitcast(F32)).then_inc(mr_ld[2 * (g % 2) + h // 2], 16)

            def steered_out(ring, n, i, s):
                for t in range(2):
                    wait_before(sp, "sp", ring, n, (s, "tin", t))
                sp.dma_start(sample_at(io["x2"], 2 * i + s), xb[s][:]).then_inc(x2_st[s], 16)

            def attention_out(ring, n, i, s):
                for j in (J - 2, J - 1):
                    wait_freed(sp, "sp", ring, n, (s, "wo", j))
                sp.dma_start(sample_at(io["d"], 2 * i + s), xb[1 - s][:]).then_inc(d_st[1 - s], 16)

            def front(ring, n, i, s, previous, ahead):
                b = 2 * i + s
                if ahead:
                    wait_apart(sp, d_st[1 - s], 16 * (i + 1), waited["sp"])
                    if not previous:
                        wait_apart(sp, w_lo_set, 4 * J, waited["sp"])
                        wait_apart(sp, beta_full, 3, waited["sp"])
                    sp.dma_start(xb[1 - s][:], sample_at(io["x1"], b + 1)).then_inc(x_ld[1 - s], 16)
                if previous:
                    for k in range(2):
                        wait_apart(sp, e_full[k], e_ring.full((G - 1, T - 1, HG - 2 + k), b - 1), waited["sp"])
                    stack_rows(ring, n, s, 1)
                max_rows(s, 0, b)
                wait_apart(sp, pj_full[ring.bank((s, "k", 3))], ring.full((s, "k", 3), n), waited["sp"])
                sp.dma_start(xhl[3 * DH:3 * DH + 2, 1::2, :].bitcast(F32),
                             stack[0][3 * DH:3 * DH + 2, 1::2, :].bitcast(F32)).then_inc(stack_ld[2], 16)
                stack_rows(ring, n, s, 2)
                max_rows(s, 1, b)
                for k in range(2):
                    wait_apart(sp, e_full[k], e_ring.full((0, T - 1, HG - 2 + k), b), waited["sp"])
                stack_rows(ring, n, s, 3)
                if ahead:
                    steered_out(ring, n, i + s, 1 - s)
                max_rows(s, 2, b)
                if previous:
                    attention_out(ring, n, i - 1 + s, 1 - s)

            def back(ring, n, i, s, ahead):
                max_rows(s, 3, 2 * i + s)
                if ahead:
                    stack_rows(ring, n, 1 - s, 0)

            steered_out(prologue, 0, 0, 0)
            for g in range(2):
                stack_rows(prologue, 0, 0, g)
            front(prologue, 0, 0, 0, False, True)
            with sp.Fori(0, PAIRS - 1) as i:
                back(steady, i, i, 0, True)
                front(steady, i, i, 1, True, True)
                back(steady, i, i, 1, True)
                front(steady, i, i + 1, 0, True, True)
            last = PAIRS - 1
            back(final, last, last, 0, True)
            front(final, last, last, 1, True, False)
            back(final, last, last, 1, False)
            attention_out(final, last, last, 1)
            for s in range(2):
                sp.wait_ge(x2_st[s], 16 * PAIRS)
                sp.wait_ge(d_st[s], 16 * (PAIRS + 1))

        @block.gpsimd
        def _(pool):
            pool.memset(mask[:], 0.0).then_inc(mask_made, 1)
            pool.wait_ge(mask_made, 1)
            pool.affine_select(out=mask[:, S - P:S], in_=mask[:, S - P:S], compare_op=ALU.is_ge, fill=MASKED, base=0,
                               pattern=[[-1, P]], channel_multiplier=1).then_inc(mask_made, 1)

            def prepare_rstd(b):
                wait_apart(pool, mv_set, T * (b + 1), waited["pool"])
                pool.tensor_scalar(var[:], mv[:, :, 1], LN_EPS, None, ALU.add).then_inc(var_set, 1)
                wait_apart(pool, var_set, b + 1, waited["pool"])
                pool.tensor_tensor(rstd[:], var[:], keep["minus_half"][:], ALU.pow).then_inc(rstd_set, 1)

            def masks(g, j, b):
                for k in range(2):
                    wait_apart(pool, e_free[k], e_ring.full((g, j, HG - 2 + k), b) + 1, waited["pool"])
                pool.affine_select(out=pt[j % 2][:, :, 0:P], in_=pt[j % 2][:, :, 0:P], compare_op=ALU.is_ge, fill=0.0,
                                   base=0, pattern=[[0, HG], [1, P]], channel_multiplier=-1).then_inc(masked, 1)

            def groups(b, which, ahead):
                for g in which:
                    for j in range(T):
                        masks(g, j, b)
                        if ahead and (g, j) == (1, T - 1):
                            prepare_rstd(b + 1)

            prepare_rstd(0)
            with pool.Fori(0, B - 1) as b:
                groups(b, range(G), True)
            groups(B - 1, range(G), False)

        @block.vector
        def _(dve):
            dve.tensor_scalar(gate_w2, ident[:], 0.0, small(smalls, "gate_w2"), ALU.mult, ALU.add).then_inc(gate_dve, 1)
            dve.wait_ge(row_ld, 32)
            dve.tensor_tensor(keep["steer"][R:R + 1, :, :].rearrange("r j k -> r (j k)"), rbias[R:R + 1, :],
                              keep["steer"][R:R + 1, :, :].rearrange("r j k -> r (j k)"), ALU.add).then_inc(gate_dve, 1)
            dve.memset(psb[R:R + 1, :], 1.0).then_inc(rows_made, 1)
            dve.wait_ge(gate_act, 3)
            dve.tensor_tensor(strength[:], strength[:], mod[:], ALU.mult).then_inc(gate_dve, 1)
            dve.wait_ge(gate_dve, 3)
            dve.tensor_copy(pb[:, :, STRENGTH], strength[:])
            for j in range(J):
                dve.tensor_scalar(pb[:, :, GB2 + j], small(smalls, "gate"), small(smalls, "b2", j), None, ALU.mult)
            dve.tensor_copy(pb[:, :, GATE], small(smalls, "gate"))
            dve.tensor_scalar(pb[:, :, GATE_1], small(smalls, "gate"), -1.0, None, ALU.add).then_inc(gate_dve, 1)
            for n in range(2):
                dve.memset(stack[n][3 * DH:3 * DH + 2, 1::2, :].bitcast(F32), 1.0).then_inc(rows_made, 1)
            dve.wait_ge(gate_dve, 4)
            for k in range(2):
                dve.sem_inc(s_free[k], 1)

            def folded_low(n):
                w, where = staged[n]
                for j in range(J):
                    dve.wait_ge(w_hi_set, J * n + j + 1)
                    scale = small(smalls, "gamma1", j) if w != "wo" else 1.0
                    dve.scalar_tensor_tensor(w_lo[w][:, j, :], where[:, j, :], scale, w_hi[w][:, j, :].bitcast(F32),
                                             ALU.mult, ALU.subtract).then_inc(w_lo_set, 1)

            def prepare_scalars(s, b):
                dve.tensor_copy(cur[s][:], pb[:, bass.ds(b, 1), :].rearrange("p b n -> p (b n)")).then_inc(cur_set, 1)

            def prepare_stats(ring, i, s, b, t):
                wait_freed(dve, "dve", ring, i, (s, "tin", t))
                dve.bn_stats(st[:, t, :], tok[:, t, :]).then_inc(stat_set, 1)
                wait_apart(dve, stat_set, T * b + t + 1, waited["dve"])
                dve.bn_aggr(mv[:, t, :], st[:, t, :]).then_inc(mv_set, 1)

            def prepare_steer(ring, i, s, b, j):
                k = ring.bank((s, "resp", j))
                if j == 0:
                    wait_apart(dve, cur_set, b + 1, waited["dve"])
                wait_apart(dve, pj_full[k], ring.full((s, "resp", j), i), waited["dve"])
                dve.scalar_tensor_tensor(xb[s][:, j, :], pj(k), cur[s][:, STRENGTH:STRENGTH + 1], xb[s][:, j, :], ALU.mult,
                                         ALU.add).then_inc(pj_free[k], 1)

            def prepare_norm(b, t):
                if t == 0:
                    wait_apart(dve, rstd_set, b + 1, waited["dve"])
                dve.tensor_scalar(tok[:, t, :], tok[:, t, :], mv[:, t, 0:1], rstd[:, t:t + 1], ALU.subtract,
                                  ALU.mult).then_inc(normed, 1)

            def prepare_lo(ring, i, s, b, j):
                k = ring.bank((s, "tback", j))
                wait_apart(dve, xh_set, J * b + j + 1, waited["dve"])
                dve.tensor_tensor(xl[:, j, :], pj(k), xh[:, j, :].bitcast(F32), ALU.subtract).then_inc(pj_free[k], 1)

            def qk_low(ring, i, s, b, g, n):
                k = ring.bank((s, "qk"[n], g))
                wait_apart(dve, qk_hi, 8 * b + 2 * g + n + 1, waited["dve"])
                dve.scalar_tensor_tensor(qk4[g % 2][:, 3 * n, :].bitcast(F32R), pj(k), bias[:, n, g:g + 1],
                                         qk4[g % 2][:, 1 + n, :], ALU.add, ALU.subtract).then_inc(pj_free[k], 1)

            def max_unit(g, u, b):
                h, tiles = u // len(U_TILES), U_TILES[u % len(U_TILES)]
                k = s_ring.bank((g, u))
                wait_apart(dve, s_full[k], s_ring.full((g, u), b), waited["dve"])
                at = 0
                for t in tiles:
                    width = P * (t + 1)
                    got = sc(k)[:, at:at + width]
                    last = dve.tensor_tensor_reduce(got, got, mask[:, S - width:S], 1.0, 2.0 * MASKED, ALU.add, ALU.max,
                                                    mx[g % 2][:, t, h:h + 1])
                    at += width
                last.then_inc(s_free[k], 1)

            def minus_max(g, b):
                for u in (UNITS - 2, UNITS - 1):
                    wait_apart(dve, s_free[s_ring.bank((g, u))], s_ring.full((g, u), b) + 1, waited["dve"])
                dve.tensor_scalar(nm[:, :, :, 0], mx[g % 2][:], -1.0, None, ALU.mult).then_inc(nm_hi, 1)
                dve.wait_ge(nm_hi, G * b + g + 1)
                dve.scalar_tensor_tensor(nm[:, :, :, 1], mx[g % 2][:], -1.0, nm[:, :, :, 0].bitcast(F32), ALU.mult,
                                         ALU.subtract).then_inc(nm_lo, 1)

            def over_sums(g, c, b):
                if c == 0:
                    dve.wait_ge(ctx_free, 1 + G * b + g + 1)
                part = sums[:, c * P:(c + 1) * P]
                dve.reciprocal(part, part).then_inc(rec_set, 1)
                if c == T - 1:
                    dve.wait_ge(rec_set, T * (G * b + g + 1))
                    dve.tensor_tensor(ctxs[:], ctxs[:], sums[:], ALU.mult).then_inc(ctxn_set, 1)

            def ctx_low(s, g, b):
                at = context_at(s, g)
                dve.wait_ge(ch_set, G * b + g + 1)
                dve.scalar_tensor_tensor(cl[:, at, :], ctxs[:], bias[:, 2, g:g + 1], ch[:, at, :].bitcast(F32), ALU.add,
                                         ALU.subtract).then_inc(cl_set, 1)

            def front(ring, n, i, s, previous, ahead):
                b = 2 * i + s
                for m in range(2):
                    qk_low(ring, n, s, b, 2, m)
                for u in range(UNITS):
                    max_unit(0, u, b)
                    if previous and 2 <= u < 2 + T:
                        over_sums(G - 1, u - 2, b - 1)
                minus_max(0, b)
                if previous:
                    ctx_low(1 - s, G - 1, b - 1)
                if ahead:
                    prepare_scalars(1 - s, b + 1)
                for u in range(UNITS):
                    max_unit(1, u, b)
                    if u in (3, 5):
                        qk_low(ring, n, s, b, 3, (u - 3) // 2)
                    if ahead and u >= UNITS - J + 1:
                        prepare_steer(ring, n, 1 - s, b + 1, u - (UNITS - J + 1))
                minus_max(1, b)
                if ahead:
                    prepare_steer(ring, n, 1 - s, b + 1, J - 1)
                for u in range(UNITS):
                    max_unit(2, u, b)
                    if 6 <= u < 6 + T:
                        over_sums(0, u - 6, b)
                    if ahead and u >= 10:
                        prepare_stats(ring, n, 1 - s, b + 1, u - 10)
                minus_max(2, b)
                ctx_low(s, 0, b)
                for u in range(UNITS):
                    max_unit(3, u, b)
                    if ahead and u < 2:
                        prepare_stats(ring, n, 1 - s, b + 1, 2 + u)
                    if ahead and u in (4, 5):
                        for t in (2 * u - 8, 2 * u - 7):
                            prepare_norm(b + 1, t)
                    if 6 <= u < 6 + T:
                        over_sums(1, u - 6, b)
                minus_max(3, b)
                ctx_low(s, 1, b)

            def back(ring, n, i, s, ahead):
                b = 2 * i + s
                if ahead:
                    for j in range(J):
                        prepare_lo(ring, n, 1 - s, b + 1, j)
                for c in range(T):
                    over_sums(2, c, b)
                if ahead:
                    for m in range(2):
                        qk_low(ring, n, 1 - s, b + 1, 0, m)
                ctx_low(s, 2, b)
                if ahead:
                    for m in range(2):
                        qk_low(ring, n, 1 - s, b + 1, 1, m)

            prepare_scalars(0, 0)
            folded_low(0)
            folded_low(1)
            for j in range(J):
                prepare_steer(prologue, 0, 0, 0, j)
            for t in range(T):
                prepare_stats(prologue, 0, 0, 0, t)
            for t in range(T):
                prepare_norm(0, t)
            for n, name in enumerate(("bq", "bk", "bv")):
                dve.wait_ge(beta_full, n + 1)
                dve.tensor_tensor(bias[:, n, :], psum[:, 2 + n, 0:G], small(smalls, name), ALU.add).then_inc(beta_set, 1)
            for j in range(J):
                prepare_lo(prologue, 0, 0, 0, j)
            dve.wait_ge(beta_set, 3)
            for g in range(2):
                for n in range(2):
                    qk_low(prologue, 0, 0, 0, g, n)
            folded_low(2)
            folded_low(3)
            dve.wait_ge(mask_made, 2)
            front(prologue, 0, 0, 0, False, True)
            with dve.Fori(0, PAIRS - 1) as i:
                back(steady, i, i, 0, True)
                front(steady, i, i, 1, True, True)
                back(steady, i, i, 1, True)
                front(steady, i, i + 1, 0, True, True)
            last = PAIRS - 1
            back(final, last, last, 0, True)
            front(final, last, last, 1, True, False)
            back(final, last, last, 1, False)
            for c in range(T):
                over_sums(G - 1, c, B - 1)
            ctx_low(1, G - 1, B - 1)

        @block.scalar
        def _(act):
            act.activation(mod[:], small(smalls, "safety"), ACT.Sigmoid).then_inc(gate_act, 1)
            act.wait_ge(gate_full, 1)
            act.activation(gate_h[:], psum[:, 5, 0:B], ACT.Relu, bias=small(smalls, "gate_b1"), scale=1.0 / S).then_inc(gate_act, 1)
            act.wait_ge(gate_full, 2)
            act.activation(strength[:], psum[:, 6, 0:B], ACT.Sigmoid, bias=small(smalls, "gate_b2")).then_inc(gate_act, 1)
            for k in range(2):
                act.sem_inc(e_free[k], 1)
            act.sem_inc(ctx_free, 1)

            def folded_high(n):
                w, where = staged[n]
                act.wait_ge(raw_ld[n], 16)
                for j in range(J):
                    scale = small(smalls, "gamma1", j) if w != "wo" else 1.0
                    act.activation(w_hi[w][:, j, :], where[:, j, :], ACT.Copy, scale=scale).then_inc(w_hi_set, 1)

            def prepare_p(ring, i, s):
                k = ring.bank((s, "p"))
                act.wait_ge(pj_full[k], ring.full((s, "p"), i))
                act.activation(psb[0:R, :], pj(k)[0:R, :], ACT.Copy).then_inc(pj_free[k], 1)

            def prepare_tokens(ring, i, s, t, stacked):
                k = ring.bank((s, "tin", t))
                if stacked and t == 0:
                    act.wait_ge(stack_ld[stacked[0]], stacked[1])
                act.wait_ge(pj_full[k], ring.full((s, "tin", t), i))
                act.activation(tok[:, t, :], pj(k), ACT.Copy).then_inc(pj_free[k], 1)

            def prepare_hi(ring, i, s, j):
                k = ring.bank((s, "tback", j))
                act.wait_ge(pj_full[k], ring.full((s, "tback", j), i))
                act.activation(xh[:, j, :], pj(k), ACT.Copy).then_inc(xh_set, 1)

            def qk_high(ring, i, s, g, n, stacked):
                name = (s, "qk"[n], g)
                k = ring.bank(name)
                if stacked:
                    act.wait_ge(stack_ld[stacked[0]], stacked[1])
                act.wait_ge(pj_full[k], ring.full(name, i))
                act.activation(qk4[g % 2][:, 1 + n, :].bitcast(F32R), pj(k), ACT.Identity, bias=bias[:, n, g:g + 1]).then_inc(qk_hi, 1)

            def exponentials(g, j, half, b):
                width = S - P * j
                if T * g + j >= 2 and half == 0:
                    act.wait_ge(pv_done, G * T * b + T * g + j - 1)
                for h in exp_heads(half):
                    k = e_ring.bank((g, j, h))
                    act.wait_ge(e_full[k], e_ring.full((g, j, h), b))
                    act.activation(pt[j % 2][:, h, 0:width], ex(k)[:, 0:width], ACT.Exp,
                                   scale=INV_SQRT_DH).then_inc(e_free[k], 1)

            def context(g, b):
                if g:
                    act.wait_ge(cl_set, G * b + g)
                act.wait_ge(pv_done, G * T * b + T * (g + 1))
                act.activation(sums[:], sum_bank, ACT.Copy)
                act.activation(ctxs[:], ctx_bank, ACT.Copy).then_inc(ctx_free, 1)

            def ctx_high(s, g, b):
                act.wait_ge(ctxn_set, G * b + g + 1)
                act.activation(ch[:, context_at(s, g), :], ctxs[:], ACT.Identity, bias=bias[:, 2, g:g + 1]).then_inc(ch_set, 1)

            def max_rows(g, b):
                k = s_ring.bank((g, UNITS))
                if g >= 2:
                    for half in range(2):
                        act.wait_ge(mr_ld[2 * (g % 2) + half], 64 * b + 32)
                act.wait_ge(s_full[k], s_ring.full((g, UNITS), b))
                act.activation(mr[g % 2][:], sc(k)[0:2 * HG, :], ACT.Copy).then_inc(mr_set, 1)
                act.wait_ge(mr_set, G * b + g + 1)
                act.sem_inc(s_free[k], 1)

            def stacking(i, s, g):
                return STACK_AT[s, g][0], stack_count(i, s, g)

            def attention_result(ring, n, s, j):
                k = ring.bank((s, "wo", j))
                act.wait_ge(pj_full[k], ring.full((s, "wo", j), n))
                act.activation(xb[1 - s][:, j, :], pj(k), ACT.Identity, bias=small(smalls, "bo", j)).then_inc(pj_free[k], 1)

            def steps(g, u, b):
                if u == LAST_AT + 1 and g >= 2:
                    context(g - 2, b)
                if u == 2 and 1 <= g <= G:
                    max_rows(g - 1, b)
                if g >= 2 and u < EXP_AT + EXP_STEPS - UNITS:
                    exponentials(g - 2, T - 1, u, b)
                if 1 <= g <= G and u >= EXP_AT:
                    exponentials(g - 1, (u - EXP_AT) // 2, (u - EXP_AT) % 2, b)

            def front(ring, n, i, s, previous, ahead):
                b = 2 * i + s
                for u in range(LAST_AT + 2):
                    if previous:
                        steps(G + 1, u, b - 1)
                    if u in (2, 4):
                        qk_high(ring, n, s, 2, (u - 2) // 2, stacking(i, s, 0))
                for t in range(T):
                    values_out(ring, n, s, b, t)
                    if previous and t == 2:
                        ctx_high(1 - s, G - 1, b - 1)
                for u in range(UNITS):
                    steps(1, u, b)
                    if u in (2, 4):
                        qk_high(ring, n, s, 3, (u - 2) // 2, stacking(i, s, 1))
                    if ahead and u == 8:
                        prepare_p(ring, n, 1 - s)
                for u in range(UNITS):
                    if previous and u == 4:
                        act.wait_ge(x2_st[s], 16 * (i + 1))
                    if previous and u in (4, 8):
                        attention_result(ring, n, 1 - s, (u - 4) // 4)
                    steps(2, u, b)
                    if ahead and u >= 10:
                        prepare_tokens(ring, n, 1 - s, u - 10, stacking(i, s, 3))
                ctx_high(s, 0, b)
                for u in range(UNITS):
                    if ahead and u < 2:
                        prepare_tokens(ring, n, 1 - s, 2 + u, None)
                    steps(3, u, b)
                    if previous and u in (5, 9):
                        attention_result(ring, n, 1 - s, 2 + (u - 5) // 4)
                ctx_high(s, 1, b)

            def values_out(ring, n, s, b, t):
                k = ring.bank((s, "v", t))
                act.wait_ge(pj_full[k], ring.full((s, "v", t), n))
                act.activation(v[:, t, :], pj(k), ACT.Copy).then_inc(pj_free[k], 1)

            def back(ring, n, i, s, ahead):
                b = 2 * i + s
                for u in range(UNITS):
                    if ahead and 3 <= u < 3 + J:
                        prepare_hi(ring, n, 1 - s, u - 3)
                    steps(4, u, b)
                    if ahead and u in (8, 9):
                        qk_high(ring, n, 1 - s, 0, u - 8, stacking(i, s, 2))
                    if ahead and u == 10:
                        qk_high(ring, n, 1 - s, 1, 0, None)
                ctx_high(s, 2, b)
                if ahead:
                    qk_high(ring, n, 1 - s, 1, 1, None)

            prepare_p(prologue, 0, 0)
            folded_high(0)
            folded_high(1)
            for t in range(T):
                prepare_tokens(prologue, 0, 0, t, None)
            folded_high(2)
            folded_high(3)
            for j in range(J):
                prepare_hi(prologue, 0, 0, j)
            act.wait_ge(beta_set, 3)
            for g in range(2):
                for n in range(2):
                    qk_high(prologue, 0, 0, g, n, None)
            front(prologue, 0, 0, 0, False, True)
            with act.Fori(0, PAIRS - 1) as i:
                back(steady, i, i, 0, True)
                front(steady, i, i, 1, True, True)
                back(steady, i, i, 1, True)
                front(steady, i, i + 1, 0, True, True)
            last = PAIRS - 1
            back(final, last, last, 0, True)
            front(final, last, last, 1, True, False)
            back(final, last, last, 1, False)
            for u in range(LAST_AT + 2):
                steps(G + 1, u, B - 1)
            ctx_high(1, G - 1, B - 1)
            act.wait_ge(d_st[0], 16 * PAIRS)
            for j in range(J):
                attention_result(final, last, 1, j)

        @block.tensor
        def _(pe):
            def claim(ring, i, name):
                k = ring.bank(name)
                if ring is not prologue or ring.free(name):
                    wait_apart(pe, pj_free[k], ring.free(name, i), waited["pe"])
                return k

            def prepare_p(ring, n, i, s, j):
                if j == 0:
                    wait_apart(pe, x_ld[s], 16 * (i + 1), waited["pe"])
                    claim(ring, n, (s, "p"))
                k = ring.bank((s, "p"))
                last = pe.matmul(pj(k)[0:R, :], keep["uo"][:, j, :], xb[s][:, j, :], start=(j == 0), stop=(j == J - 1))
                if j == J - 1:
                    last.then_inc(pj_full[k], 1)

            def prepare_steer(ring, i, s, j):
                if j == 0:
                    wait_freed(pe, "pe", ring, i, (s, "p"))
                k = claim(ring, i, (s, "resp", j))
                pe.matmul(pj(k), keep["steer"][:, j, :], psb[:], start=True, stop=True).then_inc(pj_full[k], 1)

            def prepare_tokens(ring, i, s, t):
                if t == 0:
                    wait_before(pe, "pe", ring, i, (s, "tin", 1))
                k = claim(ring, i, (s, "tin", t))
                for j in range(J):
                    last = pe.transpose(pj(k)[:, j * P:(j + 1) * P], xb[s][:, j, t * P:(t + 1) * P], ident[:])
                last.then_inc(pj_full[k], 1)

            def prepare_back(ring, i, s, b, j):
                if j == 0:
                    wait_apart(pe, normed, T * (b + 1), waited["pe"])
                k = claim(ring, i, (s, "tback", j))
                for t in range(T):
                    last = pe.transpose(pj(k)[:, t * P:(t + 1) * P], tok[:, t, j * P:(j + 1) * P], ident[:])
                last.then_inc(pj_full[k], 1)

            def qk_piece(ring, i, s, g, n, j):
                name, w, at = (s, "qk"[n], g), ("wq", "wk")[n], slice(g * P, (g + 1) * P)
                if (g, n, j) == (0, 0, 0):
                    for last in (J - 2, J - 1):
                        wait_freed(pe, "pe", ring, i, (s, "tback", last))
                k = claim(ring, i, name) if j == 0 else ring.bank(name)
                last = three_pass(pe, pj(k), [(w_hi[w][:, j, at], w_lo[w][:, j, at], xh[:, j, :], xl[:, j, :])],
                                  start=j == 0, stop=j == J - 1)
                if j == J - 1:
                    last.then_inc(pj_full[k], 1)

            def v_piece(ring, i, s, t, j):
                name, at = (s, "v", t), slice(t * P, (t + 1) * P)
                k = claim(ring, i, name) if j == 0 else ring.bank(name)
                last = three_pass(pe, pj(k), [(xh[:, j, at], xl[:, j, at], w_hi["wv"][:, j, :], w_lo["wv"][:, j, :])],
                                  start=j == 0, stop=j == J - 1)
                if j == J - 1:
                    last.then_inc(pj_full[k], 1)

            def max_unit(i, s, g, u, b):
                h, tiles = u // len(U_TILES), U_TILES[u % len(U_TILES)]
                place = STACK_AT[s, g][0]
                if u == 0:
                    wait_apart(pe, stack_ld[place], stack_count(i, s, g), waited["pe"])
                k = s_ring.bank((g, u))
                wait_apart(pe, s_free[k], s_ring.free((g, u), b) + 1, waited["pe"])
                at = 0
                for t in tiles:
                    width = P * (t + 1)
                    last = pe.matmul(sc(k)[:, at:at + width], stack[place][0:3 * DH, 2 * h, t * P:(t + 1) * P],
                                     stack[place][0:3 * DH, 2 * h + 1, 0:width], start=True, stop=True)
                    at += width
                last.then_inc(s_full[k], 1)

            def max_rows(g, b):
                k = s_ring.bank((g, UNITS))
                wait_apart(pe, nm_lo, G * b + g + 1, waited["pe"])
                wait_apart(pe, s_free[k], s_ring.free((g, UNITS), b) + 1, waited["pe"])
                for t in range(T):
                    last = pe.transpose(sc(k)[0:2 * HG, t * P:(t + 1) * P],
                                        nm[:, t, :, :].rearrange("p h n -> p (h n)").bitcast(F32), ident[:])
                last.then_inc(s_full[k], 1)

            def exp_scores(s, g, j, half, b):
                place = STACK_AT[s, g][0]
                if j == 0:
                    wait_apart(pe, mr_ld[2 * (g % 2) + half], 64 * b + 32 * (g // 2 + 1), waited["pe"])
                width = S - P * j
                for h in exp_heads(half):
                    k = e_ring.bank((g, j, h))
                    wait_apart(pe, e_free[k], e_ring.free((g, j, h), b) + 1, waited["pe"])
                    pe.matmul(ex(k)[:, 0:width], stack[place][0:3 * DH + 2, 2 * h + 1, j * P:(j + 1) * P],
                              stack[place][0:3 * DH + 2, 2 * h, j * P:S], start=True, stop=True).then_inc(e_full[k], 1)

            def values(g, j, b):
                if j == 0:
                    wait_apart(pe, ctx_free, G * b + g + 1, waited["pe"])
                wait_apart(pe, masked, G * T * b + T * g + j + 1, waited["pe"])
                width = S - P * j
                for bank, is_ctx in ((ctx_bank, True), (sum_bank, False)):
                    for h in range(HG):
                        at = slice(h * DH, (h + 1) * DH)
                        lhs = v[:, j, (HG * g + h) * DH:(HG * g + h + 1) * DH] if is_ctx else keep["ones"][:]
                        last = pe.matmul(bank[at, j * P:S], lhs, pt[j % 2][:, h, 0:width], start=(j == 0), stop=(j == T - 1),
                                         tile_position=(0, h * DH))
                last.then_inc(pv_done, 1)

            def wo_piece(ring, n, s, b, jo, g):
                name, at, slot = (s, "wo", jo), slice(jo * P, (jo + 1) * P), context_at(s, g)
                if (jo, g) == (0, 0):
                    wait_apart(pe, cl_set, G * (b + 1), waited["pe"])
                k = claim(ring, n, name) if g == 0 else ring.bank(name)
                last = three_pass(pe, pj(k), [(w_hi["wo"][:, g, at], w_lo["wo"][:, g, at], ch[:, slot, :], cl[:, slot, :])],
                                  start=g == 0, stop=g == G - 1)
                if g == G - 1:
                    last.then_inc(pj_full[k], 1)

            def exp_step(s, g, q, b):
                j, half = q // 2, q % 2
                exp_scores(s, g, j, half, b)
                if half and j:
                    values(g, j - 1, b)

            def steps(s, g, u, b):
                if u == ROWS_AT and 1 <= g <= G:
                    max_rows(g - 1, b)
                if g >= 2 and u < EXP_AT + EXP_STEPS - UNITS:
                    exp_step(s, g - 2, UNITS - EXP_AT + u, b)
                if g >= 2 and u == LAST_AT:
                    values(g - 2, T - 1, b)
                if 1 <= g <= G and u >= EXP_AT:
                    exp_step(s, g - 1, u - EXP_AT, b)

            def front(ring, n, i, s, previous, ahead):
                b = 2 * i + s
                for u in range(LAST_AT + 1):
                    if previous:
                        steps(1 - s, G + 1, u, b - 1)
                    for part in (2 * u, 2 * u + 1):
                        qk_piece(ring, n, s, 2, part // J, part % J)
                for u in range(UNITS):
                    max_unit(i, s, 0, u, b)
                    for part in range(T * J * u // UNITS, T * J * (u + 1) // UNITS):
                        v_piece(ring, n, s, part // J, part % J)
                for u in range(UNITS):
                    max_unit(i, s, 1, u, b)
                    steps(s, 1, u, b)
                    if u < J:
                        for part in (2 * u, 2 * u + 1):
                            qk_piece(ring, n, s, 3, part // J, part % J)
                    if ahead and J <= u < 2 * J:
                        prepare_p(ring, n, i + s, 1 - s, u - J)
                    if ahead and u >= UNITS - J:
                        prepare_steer(ring, n, 1 - s, u - (UNITS - J))
                for u in range(UNITS):
                    max_unit(i, s, 2, u, b)
                    steps(s, 2, u, b)
                    if previous and u < 2 * G:
                        wo_piece(ring, n, 1 - s, b - 1, u // G, u % G)
                    if ahead and u >= UNITS - T:
                        prepare_tokens(ring, n, 1 - s, u - (UNITS - T))
                for u in range(UNITS):
                    max_unit(i, s, 3, u, b)
                    steps(s, 3, u, b)
                    if previous and u < 2 * G:
                        wo_piece(ring, n, 1 - s, b - 1, 2 + u // G, u % G)

            def back(ring, n, i, s, ahead):
                b = 2 * i + s
                for u in range(UNITS):
                    steps(s, 4, u, b)
                    if ahead and 2 <= u < 2 + J:
                        prepare_back(ring, n, 1 - s, b + 1, u - 2)
                    if ahead and u >= 6:
                        for part in range(3 * (u - 6), min(3 * (u - 5), 4 * J)):
                            qk_piece(ring, n, 1 - s, part // (2 * J), part // J % 2, part % J)

            pe.wait_ge(gw_ld, 16)
            for j in range(J):
                last = pe.matmul(psum[:, 5, 0:B], gate_w1[:, j, :], pooled[:, :, j], start=(j == 0), stop=(j == J - 1))
            last.then_inc(gate_full, 1)
            pe.wait_ge(gate_act, 2)
            pe.wait_ge(gate_dve, 1)
            pe.matmul(psum[:, 6, 0:B], gate_w2, gate_h[:], start=True, stop=True).then_inc(gate_full, 1)
            for j in range(J):
                prepare_p(prologue, 0, 0, 0, j)
            pe.wait_ge(rows_made, 1)
            for j in range(J):
                prepare_steer(prologue, 0, 0, j)
            for n in range(3):
                pe.wait_ge(raw_ld[n], 16)
                for g in range(G):
                    for j in range(J):
                        last = pe.matmul(psum[:, 2 + n, g:g + 1], staged[n][1][:, j, g * P:(g + 1) * P],
                                         small(smalls, "beta1", j), start=(j == 0), stop=(j == J - 1))
                last.then_inc(beta_full, 1)
            for t in range(T):
                prepare_tokens(prologue, 0, 0, t)
            for j in range(J):
                prepare_back(prologue, 0, 0, 0, j)
            pe.wait_ge(w_lo_set, 2 * J)
            for g in range(2):
                for n in range(2):
                    for j in range(J):
                        qk_piece(prologue, 0, 0, g, n, j)
            pe.wait_ge(w_lo_set, 4 * J)
            pe.wait_ge(rows_made, 3)
            pe.wait_ge(beta_set, 3)
            front(prologue, 0, 0, 0, False, True)
            with pe.Fori(0, PAIRS - 1) as i:
                back(steady, i, i, 0, True)
                front(steady, i, i, 1, True, True)
                back(steady, i, i, 1, True)
                front(steady, i, i + 1, 0, True, True)
            last = PAIRS - 1
            back(final, last, last, 0, True)
            front(final, last, last, 1, True, False)
            back(final, last, last, 1, False)
            for u in range(LAST_AT + 1):
                steps(1, G + 1, u, B - 1)
            for j in range(J):
                for g in range(G):
                    wo_piece(final, last, 1, B - 1, j, g)


def feed_forward_phase(nc, io, keep, psum):
    smalls, ident, pb = keep["smalls"], keep["ident"], keep["pb"]
    MID_AT, TIN_AT, BACK_AT = 4, 5, 10
    with ExitStack() as ctx:
        def sb(name, shape, dt=F32):
            return ctx.enter_context(nc.sbuf_tensor("c_" + name, shape, dt))

        def sem(name):
            return ctx.enter_context(nc.semaphore("c_" + name))

        w1_hi, w1_lo = sb("w1_hi", [P, J, FF], F32R), sb("w1_lo", [P, J, FF], F32R)
        w2_hi, w2_lo = sb("w2_hi", [P, M, D], F32R), sb("w2_lo", [P, M, D], F32R)
        x = sb("x", [P, J, S])
        d = sb("d", [P, J, S])
        tok = sb("tok", [P, J, S])
        base = sb("base", [P, J, S])
        h_hi = [sb(f"h_hi{s}", [P, J, S], F32R) for s in range(2)]
        h_lo = [sb(f"h_lo{s}", [P, J, S], F32R) for s in range(2)]
        act_f = sb("act", [P, S])
        act_hi = [sb(f"act_hi{k}", [P, S], F32R) for k in range(2)]
        act_lo = [sb(f"act_lo{k}", [P, S], F32R) for k in range(2)]
        b1 = sb("b1", [P, M])
        st = sb("st", [P, T, 6])
        mv = sb("mv", [P, T, 2])
        var = sb("var", [P, T])
        rstd = sb("rstd", [P, T])
        cur = [sb(f"cur{s}", [P, N_PB]) for s in range(2)]

        raw_ld = [sem(f"raw_ld{n}") for n in range(4)]
        w_hi_set, w_lo_set, beta_full, b1_set = sem("w_hi_set"), sem("w_lo_set"), sem("beta_full"), sem("b1_set")
        x_ld, d_ld, out_st = sem("x_ld"), sem("d_ld"), sem("out_st")
        mid_set, base_set = sem("mid_set"), sem("base_set")
        cur_set = sem("cur_set")
        tin_full, tok_set, stat_set, mv_set = sem("tin_full"), sem("tok_set"), sem("stat_set"), sem("mv_set")
        var_set, rstd_set, normed, tback_full = sem("var_set"), sem("rstd_set"), sem("normed"), sem("tback_full")
        h_hi_set, h_lo_set = sem("h_hi_set"), sem("h_lo_set")
        hidden_full, gelu_set, act_hi_set, act_lo_set = sem("hidden_full"), sem("gelu_set"), sem("act_hi_set"), sem("act_lo_set")
        added = sem("added")
        gated, out_set = sem("gated"), sem("out_set")
        waited = {e: sem("waited_" + e) for e in ("dve", "act", "pool", "pe", "sp")}

        hidden = lambda n: psum[:, n % 2, :]
        total = lambda j: psum[:, 2 + j, :]
        turn = lambda n: psum[:, 6 + n % 2, :]
        stage = (x, d, base, tok)
        n_stage = len(stage)
        chunks = [("w1", j) for j in range(J)] + [("w2", j) for j in range(J)]
        w2_part = lambda w, j: w[:, j * (M // J):(j + 1) * (M // J), :].rearrange("p m d -> p (m d)")
        flat = lambda a: a[:].rearrange("p j t -> p (j t)")

        block = ctx.enter_context(nc.Block())

        @block.sync
        def _(sp):
            for n, (w, j) in enumerate(chunks):
                if n >= n_stage:
                    sp.wait_ge(w_lo_set, n - n_stage + 1)
                    sp.wait_ge(beta_full, n - n_stage + 1)
                src = io[w][:, j, :] if w == "w1" else w2_part(io[w], j)
                sp.dma_start(flat(stage[n % n_stage]), src).then_inc(raw_ld[n % n_stage], 16)
            sp.sem_inc(out_st, 16)

            def load(b):
                sp.dma_start(x[:], sample_at(io["x2"], b)).then_inc(x_ld, 16)
                sp.dma_start(d[:], sample_at(io["d"], b)).then_inc(d_ld, 16)

            def sample(b, ahead):
                if ahead:
                    wait_apart(sp, base_set, J * (b + 1), waited["sp"])
                    load(b + 1)
                wait_apart(sp, out_set, J * (b + 1), waited["sp"])
                sp.dma_start(sample_at(io["out"], b), base[:]).then_inc(out_st, 16)

            sp.wait_ge(w_lo_set, len(chunks))
            load(0)
            with sp.Fori(0, B - 1) as b:
                sample(b, True)
            sample(B - 1, False)
            sp.wait_ge(out_st, 16 * (B + 1))

        @block.gpsimd
        def _(pool):
            def norm(b):
                wait_apart(pool, mv_set, T * (b + 1), waited["pool"])
                pool.tensor_scalar(var[:], mv[:, :, 1], LN_EPS, None, ALU.add).then_inc(var_set, 1)
                wait_apart(pool, var_set, b + 1, waited["pool"])
                pool.tensor_tensor(rstd[:], var[:], keep["minus_half"][:], ALU.pow).then_inc(rstd_set, 1)

            def sample(i, s, ahead):
                b = 2 * i + s
                if ahead:
                    norm(b + 1)
                for j in range(J):
                    wait_apart(pool, gated, J * b + J + j + 1, waited["pool"])
                    pool.tensor_scalar(base[:, j, :], base[:, j, :], cur[s][:, GB2 + j:GB2 + j + 1], None,
                                       ALU.add).then_inc(out_set, 1)

            norm(0)
            with pool.Fori(0, PAIRS - 1) as i:
                sample(i, 0, True)
                sample(i, 1, True)
            sample(PAIRS - 1, 0, True)
            sample(PAIRS - 1, 1, False)

        @block.vector
        def _(dve):
            for n, (w, j) in enumerate(chunks):
                dve.wait_ge(w_hi_set, n + 1)
                if w == "w1":
                    part, scale, hi = w1_lo[:, j, :], small(smalls, "gamma2", j), w1_hi[:, j, :]
                else:
                    part, scale, hi = w2_part(w2_lo, j), 1.0, w2_part(w2_hi, j)
                dve.scalar_tensor_tensor(part, flat(stage[n % n_stage]), scale, hi.bitcast(F32), ALU.mult,
                                         ALU.subtract).then_inc(w_lo_set, 1)
            dve.wait_ge(beta_full, J)
            dve.tensor_tensor(b1[:], small(smalls, "b1"), psum[:, 0, 0:M], ALU.add).then_inc(b1_set, 1)
            for j in range(1, J):
                dve.wait_ge(b1_set, j)
                dve.tensor_tensor(b1[:], b1[:], psum[:, 0, j * M:(j + 1) * M], ALU.add).then_inc(b1_set, 1)
            dve.sem_inc(act_hi_set, 2)
            dve.sem_inc(act_lo_set, 2)
            dve.sem_inc(gated, J)

            def add_attention(b, j):
                if j == 0:
                    wait_apart(dve, x_ld, 16 * (b + 1), waited["dve"])
                    wait_apart(dve, d_ld, 16 * (b + 1), waited["dve"])
                dve.tensor_tensor(x[:, j, :], x[:, j, :], d[:, j, :], ALU.add).then_inc(mid_set, 1)

            def start_result(s, b, j):
                if j == 0:
                    wait_apart(dve, out_st, 16 * (b + 1), waited["dve"])
                    wait_apart(dve, cur_set, b + 1, waited["dve"])
                    wait_apart(dve, mid_set, J * (b + 1), waited["dve"])
                dve.scalar_tensor_tensor(base[:, j, :], d[:, j, :], cur[s][:, GATE_1:GATE_1 + 1], x[:, j, :], ALU.mult,
                                         ALU.add).then_inc(base_set, 1)

            def statistics(b, t):
                dve.wait_ge(tok_set, T * b + t + 1)
                dve.bn_stats(st[:, t, :], tok[:, t, :]).then_inc(stat_set, 1)
                wait_apart(dve, stat_set, T * b + t + 1, waited["dve"])
                dve.bn_aggr(mv[:, t, :], st[:, t, :]).then_inc(mv_set, 1)

            def normalise(b):
                dve.wait_ge(rstd_set, b + 1)
                for t in range(T):
                    dve.tensor_scalar(tok[:, t, :], tok[:, t, :], mv[:, t, 0:1], rstd[:, t:t + 1], ALU.subtract,
                                      ALU.mult).then_inc(normed, 1)

            def norm_low(s, b, j):
                dve.wait_ge(h_hi_set, J * b + j + 1)
                dve.tensor_tensor(h_lo[s][:, j, :], turn(j), h_hi[s][:, j, :].bitcast(F32), ALU.subtract).then_inc(h_lo_set, 1)

            def split(b, m):
                n, k = M * b + m, m % 2
                wait_apart(dve, gelu_set, n + 3, waited["dve"])
                wait_apart(dve, added, n + 1, waited["dve"])
                dve.tensor_copy(act_hi[k][:], act_f[:]).then_inc(act_hi_set, 1)
                dve.wait_ge(act_hi_set, n + 3)
                dve.tensor_tensor(act_lo[k][:], act_f[:], act_hi[k][:].bitcast(F32), ALU.subtract).then_inc(act_lo_set, 1)

            def sample(i, s, ahead):
                b = 2 * i + s
                dve.tensor_copy(cur[s][:], pb[:, bass.ds(b, 1), :].rearrange("p b n -> p (b n)")).then_inc(cur_set, 1)
                for m in range(M):
                    if m < M - 1:
                        split(b, m + 1)
                    elif ahead:
                        split(b + 1, 0)
                    if m == 2:
                        for j in range(J):
                            start_result(s, b, j)
                    if ahead and m == MID_AT:
                        for j in range(J):
                            add_attention(b + 1, j)
                    if ahead and TIN_AT <= m < TIN_AT + T:
                        statistics(b + 1, m - TIN_AT)
                    if ahead and m == TIN_AT + T:
                        normalise(b + 1)
                    if ahead and BACK_AT <= m < BACK_AT + J:
                        norm_low(1 - s, b + 1, m - BACK_AT)
                wait_apart(dve, base_set, J * (b + 1), waited["dve"])
                wait_apart(dve, added, M * (b + 1) + 2, waited["dve"])
                for j in range(J):
                    dve.scalar_tensor_tensor(base[:, j, :], total(j), cur[s][:, GATE:GATE + 1], base[:, j, :], ALU.mult,
                                             ALU.add).then_inc(gated, 1)

            for j in range(J):
                add_attention(0, j)
            for t in range(T):
                statistics(0, t)
            normalise(0)
            for j in range(J):
                norm_low(0, 0, j)
            split(0, 0)
            with dve.Fori(0, PAIRS - 1) as i:
                sample(i, 0, True)
                sample(i, 1, True)
            sample(PAIRS - 1, 0, True)
            sample(PAIRS - 1, 1, False)

        @block.scalar
        def _(act):
            for n, (w, j) in enumerate(chunks):
                act.wait_ge(raw_ld[n % n_stage], 16 * (n // n_stage + 1))
                if w == "w1":
                    part, scale = w1_hi[:, j, :], small(smalls, "gamma2", j)
                else:
                    part, scale = w2_part(w2_hi, j), 1.0
                act.activation(part, flat(stage[n % n_stage]), ACT.Copy, scale=scale).then_inc(w_hi_set, 1)
            act.sem_inc(gelu_set, 2)

            def tokens(b, t):
                act.wait_ge(tin_full, T * b + t + 1)
                act.activation(tok[:, t, :], turn(t), ACT.Copy).then_inc(tok_set, 1)

            def norm_high(s, b, j):
                act.wait_ge(tback_full, J * b + j + 1)
                act.activation(h_hi[s][:, j, :], turn(j), ACT.Copy).then_inc(h_hi_set, 1)

            def gelu(b, m):
                n = M * b + m
                wait_apart(act, act_lo_set, n + 2, waited["act"])
                act.wait_ge(hidden_full, n + 1)
                act.activation(act_f[:], hidden(m), ACT.Gelu, bias=b1[:, m:m + 1]).then_inc(gelu_set, 1)

            def sample(i, s, ahead):
                b = 2 * i + s
                for m in range(M):
                    if m < M - 1:
                        gelu(b, m + 1)
                    elif ahead:
                        gelu(b + 1, 0)
                    if ahead and TIN_AT <= m < TIN_AT + T:
                        tokens(b + 1, m - TIN_AT)
                    if ahead and BACK_AT <= m < BACK_AT + J:
                        norm_high(1 - s, b + 1, m - BACK_AT)

            for t in range(T):
                tokens(0, t)
            for j in range(J):
                norm_high(0, 0, j)
            act.wait_ge(b1_set, J)
            gelu(0, 0)
            with act.Fori(0, PAIRS - 1) as i:
                sample(i, 0, True)
                sample(i, 1, True)
            sample(PAIRS - 1, 0, True)
            sample(PAIRS - 1, 1, False)

        @block.tensor
        def _(pe):
            for j in range(J):
                pe.wait_ge(raw_ld[j % n_stage], 16 * (j // n_stage + 1))
                for m in range(M):
                    last = pe.matmul(psum[:, 0, j * M + m:j * M + m + 1], flat(stage[j % n_stage])[:, m * P:(m + 1) * P],
                                     small(smalls, "beta2", j), start=True, stop=True)
                last.then_inc(beta_full, 1)
            pe.sem_inc(added, 2)

            def tokens(b, t):
                if t == 0:
                    wait_apart(pe, mid_set, J * (b + 1), waited["pe"])
                if t >= 2:
                    wait_apart(pe, tok_set, T * b + t - 1, waited["pe"])
                for j in range(J):
                    last = pe.transpose(turn(t)[:, j * P:(j + 1) * P], x[:, j, t * P:(t + 1) * P], ident[:])
                last.then_inc(tin_full, 1)

            def back(b, j):
                if j == 0:
                    wait_apart(pe, normed, T * (b + 1), waited["pe"])
                if j >= 2:
                    wait_apart(pe, h_lo_set, J * b + j - 1, waited["pe"])
                for t in range(T):
                    last = pe.transpose(turn(j)[:, t * P:(t + 1) * P], tok[:, t, j * P:(j + 1) * P], ident[:])
                last.then_inc(tback_full, 1)

            def first_product(s, b, m):
                n, at = M * b + m, slice(m * P, (m + 1) * P)
                if m == 0:
                    wait_apart(pe, h_lo_set, J * (b + 1), waited["pe"])
                wait_apart(pe, gelu_set, n + 1, waited["pe"])
                three_pass(pe, hidden(m), [(w1_hi[:, j, at], w1_lo[:, j, at], h_hi[s][:, j, :], h_lo[s][:, j, :])
                                           for j in range(J)]).then_inc(hidden_full, 1)

            def second_product(b, m):
                n, k = M * b + m, m % 2
                wait_apart(pe, act_lo_set, n + 3, waited["pe"])
                for j in range(J):
                    if m == 0:
                        wait_apart(pe, gated, J * b + j + 1, waited["pe"])
                    at = slice(j * P, (j + 1) * P)
                    last = three_pass(pe, total(j), [(w2_hi[:, m, at], w2_lo[:, m, at], act_hi[k][:], act_lo[k][:])],
                                      start=m == 0, stop=m == M - 1)
                last.then_inc(added, 1)

            def sample(i, s, ahead):
                b = 2 * i + s
                for m in range(M):
                    if m < M - 1:
                        first_product(s, b, m + 1)
                    elif ahead:
                        first_product(1 - s, b + 1, 0)
                    second_product(b, m)
                    if ahead and TIN_AT <= m < TIN_AT + T:
                        tokens(b + 1, m - TIN_AT)
                    if ahead and BACK_AT <= m < BACK_AT + J:
                        back(b + 1, m - BACK_AT)

            for t in range(T):
                tokens(0, t)
            for j in range(J):
                back(0, j)
            pe.wait_ge(w_lo_set, len(chunks))
            pe.wait_ge(b1_set, J)
            first_product(0, 0, 0)
            with pe.Fori(0, PAIRS - 1) as i:
                sample(i, 0, True)
                sample(i, 1, True)
            sample(PAIRS - 1, 0, True)
            sample(PAIRS - 1, 1, False)


def host_arrays(x, condB_theta, condB_phi, condB_t, condB_safetyscore, condB_gatescore, **w):
    def rows_of(a):
        return a.reshape(P, J, *a.shape[1:])

    def cols_of(a):
        return np.moveaxis(a.reshape(*a.shape[:-1], P, J), -1, -2)

    def every(a):
        return np.broadcast_to(a.reshape(1, -1), (P, a.size))

    half = P // 2
    freq = np.exp(np.arange(half, dtype=np.float32) * np.float32(-np.log(10000.0) / (half - 1)))
    shift = np.zeros((P, 5 * B), np.float32)
    shift[half:, 0:B] = shift[:, 2 * B:3 * B] = shift[:, 4 * B:5 * B] = 0.25
    l1, l2, l3 = (lambda n, k=k: w[f"L{k}_cond_{n}"] for k in (1, 2, 3))
    vectors = {
        "t": every(condB_t), "theta": every(condB_theta), "phi": every(condB_phi),
        "safety": every(condB_safetyscore), "gate": every(condB_gatescore),
        "freq": np.concatenate([freq, freq])[:, None], "quarter": shift,
        "half_pi": (shift * np.float32(TWO_PI)).astype(np.float32),
        "t_b1": rows_of(l1("b1")), "t_b2": rows_of(l1("b2")), "b_sc": rows_of(l1("bsc")), "b_sh": rows_of(l1("bsh")),
        "b_in": rows_of(l1("b_in")), "b_out": rows_of(l1("b_out")), "gate_b1": l2("gate_b1")[:, None],
        "gate_w2": l2("gate_w2").T, "gate_b2": every(l2("gate_b2")), "safety_bias": rows_of(l2("safety_bias")),
        "resp_b": rows_of(l2("resp_b")), "bq": l3("bq").reshape(G, P).T, "bk": l3("bk").reshape(G, P).T,
        "bv": l3("bv").reshape(G, P).T, "bo": rows_of(l3("bo")), "b1": l3("b1").reshape(M, P).T, "b2": rows_of(l3("b2")),
        "gamma1": rows_of(l3("gamma1")), "beta1": rows_of(l3("beta1")), "gamma2": rows_of(l3("gamma2")),
        "beta2": rows_of(l3("beta2")), "row": (np.arange(P, dtype=np.float32) % R)[:, None],
    }
    of = np.arange(2 * R)
    arrays = {
        "x": x.reshape(B, S, P, J).transpose(0, 2, 3, 1),
        "smalls": np.concatenate([vectors[n] for n, _ in SMALLS], axis=1),
        "pick_index": (of[:, None] - R * (of[None, :] >= R)).astype(np.float32),
        "uv_rows": np.concatenate([cols_of(l2("U").T).reshape(R, D), cols_of(l2("V").T).reshape(R, D)]),
        "t_w1": cols_of(l1("W1")), "t_w2": rows_of(cols_of(l1("W2"))), "w_sc": rows_of(cols_of(l1("Wsc"))),
        "w_sh": rows_of(cols_of(l1("Wsh"))),
        "w_in": rows_of(l1("W_in").reshape(D, P, J).transpose(0, 2, 1).reshape(D, D)),
        "w_out": rows_of(l1("W_out").reshape(D, P, J).transpose(0, 2, 1).reshape(D, D)),
        "gamma_t": rows_of(l1("gamma").T), "beta_t": rows_of(l1("beta").T),
        "safety_bias_row": cols_of(l2("safety_bias"))[None], "resp_b_row": cols_of(l2("resp_b")).reshape(1, D),
        "resp_w": cols_of(l2("resp_w").T).reshape(R, D), "gate_w1": rows_of(l2("gate_w1").T),
        "wq": rows_of(l3("Wq")), "wk": rows_of(l3("Wk")), "wv": rows_of(l3("Wv")),
        "wo": cols_of(l3("Wo")).reshape(G, P, D).transpose(1, 0, 2),
        "w1": rows_of(l3("W1")), "w2": cols_of(l3("W2")).reshape(M, P, D).transpose(1, 0, 2),
    }
    return {n: np.ascontiguousarray(a) for n, a in arrays.items()}


def build(nc, io):
    with ExitStack() as ctx:
        def sb(name, shape, dt=F32):
            return ctx.enter_context(nc.sbuf_tensor("k_" + name, shape, dt))

        psum = ctx.enter_context(nc.psum_tensor("psum", [P, 8, 512], F32))
        keep = {
            "smalls": sb("smalls", [P, N_SMALLS]), "ident": sb("ident", [P, P]), "ones": sb("ones", [P, DH]),
            "minus_half": sb("minus_half", [P, T]), "pa": sb("pa", [P, B, N_PA]), "pb": sb("pb", [P, B, N_PB]),
            "pooled": sb("pooled", [P, B, J]), "uo": sb("uo", [P, J, R]), "steer": sb("steer", [R + 1, J, P]),
        }
        with ExitStack() as first:
            for n in ("w_in", "w_out"):
                for part in ("hi", "lo"):
                    keep[f"{n}_{part}"] = first.enter_context(nc.sbuf_tensor(f"k_{n}_{part}", [P, J, J, P], F32R))
            for n in ("gamma_t", "beta_t"):
                keep[n] = first.enter_context(nc.sbuf_tensor("k_" + n, [P, J, S], F32))
            setup_phase(nc, io, keep, psum)
            first_phase(nc, io, keep, psum)
        attention_phase(nc, io, keep, psum)
        feed_forward_phase(nc, io, keep, psum)


def kernel(**inputs):
    import concourse.bacc as bacc
    from concourse.bass_utils import run_bass_kernel_spmd

    nc = bacc.Bacc("TRN2", target_bir_lowering=False, num_devices=1)
    arrays = host_arrays(**{n: np.asarray(a) for n, a in inputs.items()})
    io = {n: nc.dram_tensor("in_" + n, a.shape, mybir.dt.from_np(a.dtype), kind="ExternalInput").ap()
          for n, a in arrays.items()}
    shape = (B, P, J, S)
    for n in ("x1", "x2", "d"):
        io[n] = nc.dram_tensor(n, shape, F32, kind="Internal").ap()
    io["out"] = nc.dram_tensor("out", shape, F32, kind="ExternalOutput").ap()
    build(nc, io)
    r = run_bass_kernel_spmd(nc, [{"in_" + n: a for n, a in arrays.items()}], core_ids=[0])
    return r.results[0]["out"].transpose(0, 3, 1, 2).reshape(B, S, D)
```

```python
from contextlib import ExitStack

import numpy as np

import concourse.bass as bass
import concourse.mybir as mybir
from concourse.alu_op_type import AluOpType as ALU

F32 = mybir.dt.float32
F32R = mybir.dt.float32r
ACT = mybir.ActivationFunctionType
RADD = bass.bass_isa.ReduceOp.add

P = 128
B, S, D = 8, 512, 512
J = D // P
T = S // P
H, DH = 16, 32
HG = P // DH
G = H // HG
R = 32
FF = 2048
M = FF // P
PAIRS = B // 2

LN_EPS = 1e-5
GS_EPS = 1e-8
MASKED = -1e30
INV_SQRT_DH = float(1.0 / np.sqrt(DH))

TWO_PI = 2.0 * np.pi
TWO_PI_1 = 6.28125
TWO_PI_2 = float(np.float32(np.round((TWO_PI - TWO_PI_1) * 2.0**21) / 2.0**21))
TWO_PI_3 = float(TWO_PI - TWO_PI_1 - TWO_PI_2)
ROUND = 12582912.0
SIN_MAX = 3.1415925

SMALLS = [
    ("t", B), ("theta", B), ("phi", B), ("safety", B), ("gate", B), ("freq", 1),
    ("quarter", 5 * B), ("half_pi", 5 * B), ("t_b1", J), ("t_b2", J), ("b_sc", J), ("b_sh", J),
    ("b_in", J), ("b_out", J), ("gate_b1", 1), ("gate_w2", 1), ("gate_b2", 1), ("safety_bias", J),
    ("resp_b", J), ("bq", G), ("bk", G), ("bv", G), ("bo", J), ("b1", M), ("b2", J),
    ("gamma1", J), ("beta1", J), ("gamma2", J), ("beta2", J),
]
SMALL_AT, _n = {}, 0
for _name, _width in SMALLS:
    SMALL_AT[_name] = (_n, _width)
    _n += _width
N_SMALLS = _n

CT, ST_, NST, CP, SP_, NSP, SCALE, SHIFT = 0, 1, 2, 3, 4, 5, 6, 6 + J
N_PA = 6 + 2 * J
STRENGTH, GATE, GATE_1, GB2 = 0, 1, 2, 3
N_PB = 3 + J


def small(smalls, name, col=None):
    at, width = SMALL_AT[name]
    return smalls[:, at:at + width] if col is None else smalls[:, at + col:at + col + 1]


def aligned(address):
    return -(-address // 32) * 32


def sample_at(ap, b):
    return ap[bass.ds(b, 1), :, :, :].rearrange("b p j t -> (b p) j t")


def three_pass(pe, out, hi_lo_pairs, start=True, stop=True):
    n = len(hi_lo_pairs)
    for k, (w_hi, w_lo, x_hi, x_lo) in enumerate(hi_lo_pairs):
        pe.matmul(out, w_hi, x_hi, start=start and k == 0, stop=False)
        pe.matmul(out, w_hi, x_lo, start=False, stop=False)
        last = pe.matmul(out, w_lo, x_hi, start=False, stop=stop and k == n - 1)
    return last


def wait_apart(eng, sem, value, waited):
    eng.wait_ge(sem, value)
    eng.sem_inc(waited, 1)


def clear_semaphores(nc, sems):
    with nc.Block() as block:
        @block.gpsimd
        def _(pool):
            for sem in sems:
                pool.sem_clear(sem)
    for sem in sems:
        nc.release_semaphore(sem)


def setup_phase(nc, io, keep, psum):
    smalls, ident, pa = keep["smalls"], keep["ident"], keep["pa"]
    with ExitStack() as ctx:
        def sb(name, shape, dt=F32):
            return ctx.enter_context(nc.sbuf_tensor(name, shape, dt))

        sems = []

        def sem(name):
            sems.append(nc.alloc_semaphore(name))
            return sems[-1]

        ctx.callback(clear_semaphores, nc, sems)
        angle = sb("angle", [P, 5 * B])
        turns = sb("turns", [P, 5 * B])
        sines = sb("sines", [P, 5 * B])
        wt1 = sb("wt1", [P, J, P])
        wt2, wsc, wsh = (keep["raw"][:, n, :, :].rearrange("p j (a k) -> p j a k", a=J) for n in range(3))
        h1 = sb("t_h1", [P, J, B])
        h2 = sb("t_h2", [P, J, B])
        raw_in, raw_out = keep["raw"][:, 3, :, :], keep["raw"][:, 4, :, :]

        small_ld = sem("small_ld")
        tw_ld = [sem(f"tw_ld{n}") for n in range(4)]
        win_ld = sem("win_ld")
        ident_made = sem("ident_made")
        angles = sem("angles")
        sines_made = sem("sines_made")
        t_full = sem("t_full")
        t_done = sem("t_done")
        pa_made = sem("pa_made")
        split_hi = sem("split_hi")
        split_lo = sem("split_lo")

        block = ctx.enter_context(nc.Block())

        @block.sync
        def _(sp):
            sp.dma_start(smalls[:], io["smalls"]).then_inc(small_ld, 16)
            sp.dma_start(wt1[:], io["t_w1"]).then_inc(tw_ld[0], 16)
            sp.dma_start(wt2, io["t_w2"]).then_inc(tw_ld[1], 16)
            sp.dma_start(wsc, io["w_sc"]).then_inc(tw_ld[2], 16)
            sp.dma_start(wsh, io["w_sh"]).then_inc(tw_ld[3], 16)
            ahead = keep["ahead"]
            sp.dma_start(keep["samples"][:, 0, :, :], sample_at(io["x"], 0)).then_inc(ahead["x0"], 16)
            sp.dma_start(raw_in, io["w_in"]).then_inc(win_ld, 16)
            sp.dma_start(keep["gamma_t"][:], io["gamma_t"]).then_inc(ahead["gamma_beta"], 16)
            sp.dma_start(keep["beta_t"][:], io["beta_t"]).then_inc(ahead["gamma_beta"], 16)
            sp.dma_start(keep["gs_x"][:], io["uv"]).then_inc(ahead["uv"], 16)
            sp.dma_start(keep["samples"][:, 1, :, :], sample_at(io["x"], 1)).then_inc(ahead["x1"], 16)
            sp.dma_start(raw_out, io["w_out"]).then_inc(ahead["w_out"], 16)

        @block.gpsimd
        def _(pool):
            pool.memset(ident[:], 0.0).then_inc(ident_made, 1)
            pool.memset(keep["ones"][:], 1.0)
            pool.memset(keep["minus_half"][:], -0.5)
            pool.wait_ge(ident_made, 1)
            pool.affine_select(out=ident[:], in_=ident[:], compare_op=ALU.not_equal, fill=1.0, base=0,
                               pattern=[[-1, P]], channel_multiplier=1).then_inc(ident_made, 1)

        @block.vector
        def _(dve):
            done = [0]

            def chain(ins):
                done[0] += 1
                ins.then_inc(angles, 1)
                dve.wait_ge(angles, done[0])

            dve.wait_ge(small_ld, 16)
            dve.tensor_scalar(angle[:, 0:B], small(smalls, "t"), 5000.0, small(smalls, "freq"), ALU.mult, ALU.mult)
            dve.tensor_copy(angle[:, B:2 * B], small(smalls, "theta"))
            dve.tensor_copy(angle[:, 2 * B:3 * B], small(smalls, "theta"))
            dve.tensor_copy(angle[:, 3 * B:4 * B], small(smalls, "phi"))
            chain(dve.tensor_copy(angle[:, 4 * B:5 * B], small(smalls, "phi")))
            chain(dve.scalar_tensor_tensor(turns[:], angle[:], 1.0 / TWO_PI, small(smalls, "quarter"), ALU.mult, ALU.add))
            chain(dve.tensor_scalar(turns[:], turns[:], ROUND, None, ALU.add))
            chain(dve.tensor_scalar(turns[:], turns[:], -ROUND, None, ALU.add))
            for part in (TWO_PI_1, TWO_PI_2, TWO_PI_3):
                chain(dve.scalar_tensor_tensor(angle[:], turns[:], -part, angle[:], ALU.mult, ALU.add))
            chain(dve.tensor_tensor(angle[:], angle[:], small(smalls, "half_pi"), ALU.add))
            chain(dve.tensor_scalar(angle[:], angle[:], SIN_MAX, -SIN_MAX, ALU.min, ALU.max))
            dve.wait_ge(sines_made, 1)
            sine = lambda k: sines[:, k * B:(k + 1) * B]
            dve.tensor_copy(pa[:, :, ST_], sine(1))
            dve.tensor_scalar(pa[:, :, NST], sine(1), -1.0, None, ALU.mult)
            dve.tensor_copy(pa[:, :, CT], sine(2))
            dve.tensor_copy(pa[:, :, SP_], sine(3))
            dve.tensor_scalar(pa[:, :, NSP], sine(3), -1.0, None, ALU.mult)
            dve.tensor_copy(pa[:, :, CP], sine(4)).then_inc(pa_made, 1)
            dve.wait_ge(win_ld, 16)
            for j in range(J):
                dve.wait_ge(split_hi, j + 1)
                dve.tensor_tensor(keep["w_in_lo"][:, j, :, :].rearrange("p a k -> p (a k)"), raw_in[:, j, :],
                                  keep["w_in_hi"][:, j, :, :].rearrange("p a k -> p (a k)").bitcast(F32),
                                  ALU.subtract).then_inc(split_lo, 1)

        @block.scalar
        def _(act):
            act.wait_ge(angles, 9)
            act.activation(sines[:], angle[:], ACT.Sin).then_inc(sines_made, 1)
            act.wait_ge(t_full, 1)
            for j in range(J):
                ins = act.activation(h1[:, j, :], psum[:, 4, j * B:(j + 1) * B], ACT.Silu, bias=small(smalls, "t_b1", j))
            ins.then_inc(t_done, 1)
            act.wait_ge(t_full, 2)
            for j in range(J):
                ins = act.activation(h2[:, j, :], psum[:, 5, j * B:(j + 1) * B], ACT.Identity, bias=small(smalls, "t_b2", j))
            ins.then_inc(t_done, 1)
            act.wait_ge(t_full, 3)
            for j in range(J):
                act.activation(pa[:, :, SCALE + j], psum[:, 6, j * B:(j + 1) * B], ACT.Identity, bias=small(smalls, "b_sc", j))
                ins = act.activation(pa[:, :, SHIFT + j], psum[:, 7, j * B:(j + 1) * B], ACT.Identity,
                                     bias=small(smalls, "b_sh", j))
            ins.then_inc(pa_made, 1)
            act.wait_ge(win_ld, 16)
            for j in range(J):
                act.activation(keep["w_in_hi"][:, j, :, :].rearrange("p a k -> p (a k)"), raw_in[:, j, :],
                               ACT.Copy).then_inc(split_hi, 1)

        @block.tensor
        def _(pe):
            pe.wait_ge(tw_ld[0], 16)
            pe.wait_ge(sines_made, 1)
            for j in range(J):
                last = pe.matmul(psum[:, 4, j * B:(j + 1) * B], wt1[:, j, :], sines[:, 0:B], start=True, stop=True)
            last.then_inc(t_full, 1)
            pe.wait_ge(tw_ld[1], 16)
            pe.wait_ge(t_done, 1)
            for jo in range(J):
                for j in range(J):
                    last = pe.matmul(psum[:, 5, jo * B:(jo + 1) * B], wt2[:, j, jo, :], h1[:, j, :], start=(j == 0), stop=(j == J - 1))
            last.then_inc(t_full, 1)
            pe.wait_ge(t_done, 2)
            for k, w in ((6, wsc), (7, wsh)):
                pe.wait_ge(tw_ld[k - 4], 16)
                for jo in range(J):
                    for j in range(J):
                        last = pe.matmul(psum[:, k, jo * B:(jo + 1) * B], w[:, j, jo, :], h2[:, j, :], start=(j == 0), stop=(j == J - 1))
            last.then_inc(t_full, 1)


def first_phase(nc, io, keep, psum):
    pa, smalls = keep["pa"], keep["smalls"]
    with ExitStack() as ctx:
        def sb(name, shape, dt=F32):
            return [ctx.enter_context(nc.sbuf_tensor(f"{name}{s}", shape, dt)) for s in range(2)]

        sems = []

        def sem(name):
            pair = [nc.alloc_semaphore(f"{name}{s}") for s in range(2)]
            sems.extend(pair)
            return pair

        ctx.callback(clear_semaphores, nc, sems)

        x_in = [keep["samples"][:, s, :, :] for s in range(2)]
        rot = sb("a_rot", [P, J, S])
        z = sb("a_z", [P, J, S])
        hi, lo = ([a[:, J * part:J * (part + 1), :] for a in (keep["normed"], keep["stack"][0])] for part in range(2))
        res = [keep["tokens"], keep["result"]]
        cur = sb("a_cur", [P, N_PA])
        stats = sb("a_stats", [P, J, 6])
        mv = sb("a_mv", [P, 2])
        total = sb("a_total", [P, 1])
        spread = sb("a_spread", [P, 1])
        spread_sum = sb("a_spread_sum", [P, 1])
        away = sb("a_away", [P, 1])
        inv = sb("a_inv", [P, 1])
        nmean = sb("a_nmean", [P, 1])
        tok_sum = sb("a_tok_sum", [P, J])

        def one(name, shape):
            return ctx.enter_context(nc.sbuf_tensor("gs_" + name, shape, F32))

        gs_x, gs_q, gs_norm = keep["gs_x"], keep["gs_q"], keep["gs_norm"]
        ones = one("ones", [P, P])
        half = one("half", [P, 2])
        minus_two = one("minus_two", [P, 2])
        eps = one("eps", [P, 2])
        part = one("part", [P, 2, J, R])
        dots = one("dots", [P, 2, R])
        root = one("root", [P, 2])
        square = one("square", [P, 2])
        coef = one("coef", [P, 2, R])

        x_ld = sem("a_x_ld")
        x_used = sem("a_x_used")
        cur_set = sem("a_cur_set")
        cross = sem("a_cross")
        rotated = sem("a_rotated")
        stat = sem("a_stat")
        part_mv = sem("a_part_mv")
        mean_sum = sem("a_mean_sum")
        away_set = sem("a_away_set")
        spread_set = sem("a_spread_set")
        var_sum = sem("a_var_sum")
        var_set = sem("a_var_set")
        inv_set = sem("a_inv_set")
        nmean_set = sem("a_nmean_set")
        scaled = sem("a_scaled")
        shifted = sem("a_shifted")
        silu = sem("a_silu")
        hi_set = sem("a_hi_set")
        lo_set = sem("a_lo_set")
        product = sem("a_product")
        biased = sem("a_biased")
        result = sem("a_result")
        pooled_set = sem("a_pooled_set")
        stored = sem("a_stored")

        def single(name):
            sems.append(nc.alloc_semaphore(name))
            return sems[-1]

        gs_made = single("gs_made")
        gs_part = single("gs_part")
        gs_step = single("gs_step")
        gs_sum = single("gs_sum")
        gs_dots = single("gs_dots")
        gs_chain = single("gs_chain")
        w_hi_set = single("a_w_hi_set")
        w_lo_set = single("a_w_lo_set")
        dve_waited, pool_waited, pe_waited = single("a_dve_waited"), single("a_pool_waited"), single("a_pe_waited")

        x_dram, x1_dram = io["x"], io["x1"]
        w_hi, w_lo = (lambda n: keep["weights"][:, 2 * n, :, :]), (lambda n: keep["weights"][:, 2 * n + 1, :, :])
        w_out = lambda part, j: keep["w_out_" + part][:, j, :, :].rearrange("p a k -> p (a k)")
        w_out_raw = keep["raw"][:, 4, :, :]
        w_raw = lambda n: keep["raw"][:, 2 * n + 1, :, :]
        bank = lambda s, j: psum[:, 4 * s + j, :]
        block = ctx.enter_context(nc.Block())

        @block.sync
        def _(sp):
            def load(s, q):
                sp.dma_start(x_in[s], sample_at(x_dram, 2 * q + s)).then_inc(x_ld[s], 16)

            def store(s, q):
                sp.wait_ge(result[s], 4 * q + 4)
                sp.dma_start(sample_at(x1_dram, 2 * q + s), res[s][:]).then_inc(stored[s], 16)

            for s in range(2):
                sp.sem_inc(stored[s], 16)
                sp.wait_ge(keep["ahead"][f"x{s}"], 16)
                sp.sem_inc(x_ld[s], 16)
            sp.wait_ge(keep["ahead"]["w_out"], 16)
            for n, w in enumerate(("wq", "wk", "wv")):
                sp.dma_start(w_raw(n), io[w]).then_inc(keep["w_ld"][n], 16)
            with sp.Fori(0, PAIRS - 1) as q:
                for s in range(2):
                    sp.wait_ge(x_used[s], q + 1)
                    load(s, q + 1)
                for s in range(2):
                    store(s, q)
            for s in range(2):
                store(s, PAIRS - 1)
            for s in range(2):
                sp.wait_ge(stored[s], 16 * (PAIRS + 1))

        @block.gpsimd
        def _(pool):
            pool.memset(half[:], 0.5)
            pool.memset(minus_two[:], -2.0)
            pool.memset(eps[:], GS_EPS)
            pool.memset(ones[:], 1.0).then_inc(gs_made, 1)

            def column(i):
                return gs_x[:, :, :, bass.ds(i, 1)].to_broadcast([P, 2, J, R])

            def gs_products(i):
                if not isinstance(i, int) or i:
                    wait_apart(pool, gs_chain, 6 * i, pool_waited)
                pool.tensor_tensor(part[:], gs_x[:], column(i), ALU.mult).then_inc(gs_part, 1)
                pool.tensor_copy(gs_q[:, :, :, bass.ds(i, 1)], gs_x[:, :, :, bass.ds(i, 1)]).then_inc(gs_chain, 1)

            def gs_update(i):
                norm = gs_norm[:, :, bass.ds(i, 1)].rearrange("p h o -> p (h o)")
                wait_apart(pool, gs_dots, i + 1, pool_waited)
                pool.tensor_tensor(root[:], dots[:, :, bass.ds(i, 1)].rearrange("p h o -> p (h o)"), half[:],
                                   ALU.pow).then_inc(gs_chain, 1)
                wait_apart(pool, gs_chain, 6 * i + 2, pool_waited)
                pool.tensor_tensor(norm, root[:], eps[:], ALU.add).then_inc(gs_chain, 1)
                wait_apart(pool, gs_chain, 6 * i + 3, pool_waited)
                pool.tensor_tensor(square[:], norm, minus_two[:], ALU.pow).then_inc(gs_chain, 1)
                pool.wait_ge(gs_chain, 6 * i + 4)
                pool.tensor_tensor(coef[:], dots[:], square[:].unsqueeze(2).to_broadcast([P, 2, R]),
                                   ALU.mult).then_inc(gs_chain, 1)
                wait_apart(pool, gs_chain, 6 * i + 5, pool_waited)
                pool.tensor_tensor(part[:], column(i), coef[:].unsqueeze(2).to_broadcast([P, 2, J, R]),
                                   ALU.mult).then_inc(gs_step, 1)
                pool.wait_ge(gs_step, i + 1)
                pool.tensor_tensor(gs_x[:], gs_x[:], part[:], ALU.subtract).then_inc(gs_chain, 1)

            def statistics(s, q, st):
                n = 2 * q + st + 1
                wait_apart(pool, part_mv[s], n, pool_waited)
                pool.partition_all_reduce(total[s][:], mv[s][:, 0:1], P, RADD).then_inc(mean_sum[s], 1)
                wait_apart(pool, spread_set[s], n, pool_waited)
                pool.partition_all_reduce(spread_sum[s][:], spread[s][:], P, RADD).then_inc(var_sum[s], 1)
                wait_apart(pool, var_sum[s], n, pool_waited)
                pool.tensor_scalar(spread_sum[s][:], spread_sum[s][:], 1.0 / P, LN_EPS, ALU.mult, ALU.add).then_inc(var_set[s], 1)
                wait_apart(pool, var_set[s], n, pool_waited)
                pool.tensor_tensor(inv[s][:], spread_sum[s][:], keep["minus_half"][:, 0:1], ALU.pow).then_inc(inv_set[s], 1)

            def block_ops(k, nxt):
                if not isinstance(k, int) or k:
                    gs_update(2 * k - 1)
                gs_products(2 * k)
                if nxt:
                    statistics(*nxt)
                gs_update(2 * k)
                gs_products(2 * k + 1)

            statistics(0, 0, 0)
            pool.wait_ge(gs_made, 1)
            pool.wait_ge(keep["ahead"]["uv"], 16)
            block_ops(0, (1, 0, 0))
            with pool.Fori(0, PAIRS - 1) as q:
                block_ops(4 * q + 1, (0, q, 1))
                block_ops(4 * q + 2, (1, q, 1))
                block_ops(4 * q + 3, (0, q + 1, 0))
                block_ops(4 * q + 4, (1, q + 1, 0))
            last = PAIRS - 1
            block_ops(4 * last + 1, (0, last, 1))
            block_ops(4 * last + 2, (1, last, 1))
            block_ops(4 * last + 3, None)
            gs_update(R - 1)

        @block.vector
        def _(dve):
            def scalars(s, q):
                b = 2 * q + s
                dve.tensor_copy(cur[s][:], pa[:, bass.ds(b, 1), :].rearrange("p b n -> p (b n)")).then_inc(cur_set[s], 1)

            def rotate(s, q):
                dve.wait_ge(x_ld[s], 16 * (q + 1))
                dve.wait_ge(cur_set[s], q + 1)
                if not isinstance(q, int) or q:
                    dve.wait_ge(result[s], 4 * q)
                for j in range(J):
                    dve.wait_ge(cross[s], 4 * q + j + 1)
                    c = CT if j < 2 else CP
                    dve.scalar_tensor_tensor(rot[s][:, j, :], x_in[s][:, j, :], cur[s][:, c:c + 1], z[s][:, j, :],
                                             ALU.mult, ALU.add).then_inc(rotated[s], 1)
                dve.wait_ge(rotated[s], 4 * q + 4)
                dve.sem_inc(x_used[s], 1)

            def tile_statistics(s, q, st):
                src = rot[s] if st == 0 else z[s]
                for j in range(J):
                    if st:
                        dve.wait_ge(biased[s], 4 * q + j + 1)
                    dve.bn_stats(stats[s][:, j, :], src[:, j, :]).then_inc(stat[s], 1)
                wait_apart(dve, stat[s], 4 * (2 * q + st + 1), dve_waited)
                dve.bn_aggr(mv[s][:], stats[s][:].rearrange("p j n -> p (j n)")).then_inc(part_mv[s], 1)

            def spread_ops(s, q, st):
                n = 2 * q + st + 1
                dve.wait_ge(mean_sum[s], n)
                dve.scalar_tensor_tensor(away[s][:], total[s][:], -1.0 / P, mv[s][:, 0:1], ALU.mult,
                                         ALU.add).then_inc(away_set[s], 1)
                dve.wait_ge(away_set[s], n)
                dve.scalar_tensor_tensor(spread[s][:], away[s][:], away[s][:, 0:1], mv[s][:, 1:2], ALU.mult,
                                         ALU.add).then_inc(spread_set[s], 1)
                dve.tensor_scalar(nmean[s][:], total[s][:], -1.0 / P, None, ALU.mult).then_inc(nmean_set[s], 1)

            def centre(s, q, st, j):
                src = rot[s] if st == 0 else z[s]
                if j == 0:
                    dve.wait_ge(nmean_set[s], 2 * q + st + 1)
                dve.scalar_tensor_tensor(z[s][:, j, :], src[:, j, :], nmean[s][:, 0:1], keep["gamma_t"][:, j, :], ALU.add,
                                         ALU.mult).then_inc(scaled[s], 1)

            def shift(s, q, st, j):
                if j == 0:
                    wait_apart(dve, inv_set[s], 2 * q + st + 1, dve_waited)
                dve.wait_ge(scaled[s], 8 * q + 4 * st + j + 1)
                dve.scalar_tensor_tensor(z[s][:, j, :], z[s][:, j, :], inv[s][:, 0:1], keep["beta_t"][:, j, :], ALU.mult,
                                         ALU.add).then_inc(shifted[s], 1)

            def low(s, q, st, j):
                dve.wait_ge(hi_set[s], 8 * q + 4 * st + j + 1)
                dve.tensor_tensor(lo[s][:, j, :], z[s][:, j, :], hi[s][:, j, :].bitcast(F32),
                                  ALU.subtract).then_inc(lo_set[s], 1)

            def finish(s, q):
                b = 2 * q + s
                dve.wait_ge(stored[s], 16 * (q + 1))
                for j in range(J):
                    dve.wait_ge(product[s], 8 * q + 4 + j + 1)
                    dve.scalar_tensor_tensor(res[s][:, j, :], bank(s, j), small(smalls, "b_out", j), rot[s][:, j, :],
                                             ALU.add, ALU.add, accum_out=tok_sum[s][:, j:j + 1]).then_inc(result[s], 1)

            def token_sums(s, q):
                b = 2 * q + s
                dve.wait_ge(result[s], 4 * q + 4)
                dve.tensor_copy(keep["pooled"][:, bass.ds(b, 1), :].rearrange("p b j -> p (b j)"),
                                tok_sum[s][:]).then_inc(pooled_set[s], 1)

            def weight_low(n):
                dve.wait_ge(w_hi_set, J * (n + 2))
                for j in range(J):
                    last = dve.tensor_tensor(w_lo(n)[:, j, :], w_raw(n)[:, j, :], w_hi(n)[:, j, :].bitcast(F32), ALU.subtract)
                last.then_inc(w_lo_set, J)

            def block_ops(now, nxt, finished):
                if nxt and nxt[2] == 0:
                    scalars(*nxt[:2])
                centre(*now, 0)
                centre(*now, 1)
                shift(*now, 0)
                centre(*now, 2)
                shift(*now, 1)
                centre(*now, 3)
                shift(*now, 2)
                shift(*now, 3)
                low(*now, 0)
                low(*now, 1)
                if finished:
                    finish(*finished)
                low(*now, 2)
                if nxt and nxt[2] == 1:
                    low(*now, 3)
                    tile_statistics(*nxt)
                if nxt and nxt[2] == 0:
                    rotate(*nxt[:2])
                if not nxt or nxt[2] == 0:
                    low(*now, 3)
                if nxt and nxt[2] == 0:
                    tile_statistics(*nxt)
                if finished:
                    token_sums(*finished)
                if nxt:
                    spread_ops(*nxt)

            scalars(0, 0)
            rotate(0, 0)
            tile_statistics(0, 0, 0)
            spread_ops(0, 0, 0)
            dve.wait_ge(keep["ahead"]["gamma_beta"], 32)
            block_ops((0, 0, 0), (1, 0, 0), None)
            for j in range(J):
                dve.wait_ge(w_hi_set, j + 1)
                dve.tensor_tensor(w_out("lo", j), w_out_raw[:, j, :], w_out("hi", j).bitcast(F32), ALU.subtract).then_inc(w_lo_set, 1)
            with dve.Fori(0, PAIRS - 1) as q:
                block_ops((1, q, 0), (0, q, 1), None)
                block_ops((0, q, 1), (1, q, 1), None)
                block_ops((1, q, 1), (0, q + 1, 0), (0, q))
                block_ops((0, q + 1, 0), (1, q + 1, 0), (1, q))
            last = PAIRS - 1
            block_ops((1, last, 0), (0, last, 1), None)
            block_ops((0, last, 1), (1, last, 1), None)
            weight_low(0)
            block_ops((1, last, 1), None, (0, last))
            weight_low(1)
            finish(1, last)
            token_sums(1, last)
            weight_low(2)

        @block.scalar
        def _(act):
            def crosses(s, q):
                act.wait_ge(x_ld[s], 16 * (q + 1))
                if not isinstance(q, int) or q:
                    act.wait_ge(lo_set[s], 8 * q)
                act.wait_ge(cur_set[s], q + 1)
                for j, c in enumerate((ST_, NST, SP_, NSP)):
                    act.activation(z[s][:, j, :], x_in[s][:, j ^ 1, :], ACT.Copy,
                                   scale=cur[s][:, c:c + 1]).then_inc(cross[s], 1)

            def bias(s, q, j):
                act.wait_ge(product[s], 8 * q + j + 1)
                act.activation(z[s][:, j, :], bank(s, j), ACT.Identity, bias=small(smalls, "b_in", j)).then_inc(biased[s], 1)

            def silu_high(s, q, st, j):
                at = 8 * q + 4 * st
                act.wait_ge(shifted[s], at + j + 1)
                act.activation(z[s][:, j, :], z[s][:, j, :], ACT.Silu, bias=cur[s][:, SHIFT + j:SHIFT + j + 1],
                               scale=cur[s][:, SCALE + j:SCALE + j + 1]).then_inc(silu[s], 1)
                act.wait_ge(silu[s], at + j + 1)
                act.activation(hi[s][:, j, :], z[s][:, j, :], ACT.Copy).then_inc(hi_set[s], 1)

            def gs_copy(i, s):
                act.wait_ge(gs_sum, i + 1)
                act.activation(dots[:].rearrange("p h r -> p (h r)"), bank(s, 0)[:, 0:2 * R], ACT.Copy).then_inc(gs_dots, 1)

            def block_ops(k, now, nxt):
                if nxt and nxt[2] == 0:
                    crosses(*nxt[:2])
                silu_high(*now, 0)
                silu_high(*now, 1)
                silu_high(*now, 2)
                if not isinstance(k, int) or k:
                    gs_copy(2 * k - 1, now[0])
                silu_high(*now, 3)
                if nxt and nxt[2] == 1:
                    for j in range(J):
                        bias(*nxt[:2], j)
                gs_copy(2 * k, 1 - now[0])

            def weight_high(n):
                act.wait_ge(keep["w_ld"][n], 16)
                for j in range(J):
                    last = act.activation(w_hi(n)[:, j, :], w_raw(n)[:, j, :], ACT.Copy)
                last.then_inc(w_hi_set, J)

            crosses(0, 0)
            block_ops(0, (0, 0, 0), (1, 0, 0))
            act.wait_ge(keep["ahead"]["w_out"], 16)
            for j in range(J):
                act.activation(w_out("hi", j), w_out_raw[:, j, :], ACT.Copy).then_inc(w_hi_set, 1)
            with act.Fori(0, PAIRS - 1) as q:
                block_ops(4 * q + 1, (1, q, 0), (0, q, 1))
                block_ops(4 * q + 2, (0, q, 1), (1, q, 1))
                block_ops(4 * q + 3, (1, q, 1), (0, q + 1, 0))
                block_ops(4 * q + 4, (0, q + 1, 0), (1, q + 1, 0))
            last = PAIRS - 1
            block_ops(4 * last + 1, (1, last, 0), (0, last, 1))
            weight_high(0)
            block_ops(4 * last + 2, (0, last, 1), (1, last, 1))
            weight_high(1)
            block_ops(4 * last + 3, (1, last, 1), None)
            weight_high(2)
            gs_copy(R - 1, 0)

        @block.tensor
        def _(pe):
            def gs_total(i, s):
                wait_apart(pe, gs_part, i + 1, pe_waited)
                for j in range(J):
                    last = pe.matmul(bank(s, 0)[:, 0:2 * R].rearrange("p (h r) -> p h r", h=2), ones[:], part[:, :, j, :],
                                     start=j == 0, stop=j == J - 1)
                last.then_inc(gs_sum, 1)

            def block_ops(k, now, nxt):
                s, q, st = now
                w_hi, w_lo = (keep[("w_in", "w_out")[st] + part] for part in ("_hi", "_lo"))
                if not isinstance(k, int) or k:
                    wait_apart(pe, gs_dots, 2 * k, pe_waited)
                for j in range(J):
                    wait_apart(pe, lo_set[s], 8 * q + 4 * st + j + 1, pe_waited)
                    for jo in range(J):
                        last = three_pass(pe, bank(s, jo), [(w_hi[:, j, jo, :], w_lo[:, j, jo, :], hi[s][:, j, :], lo[s][:, j, :])],
                                          start=j == 0, stop=j == J - 1)
                        if j == J - 1:
                            last.then_inc(product[s], 1)
                    if j == 1:
                        if nxt and nxt[2]:
                            wait_apart(pe, biased[1 - s], 4 * nxt[1] + 1, pe_waited)
                        elif not isinstance(k, int) or k:
                            wait_apart(pe, result[1 - s], 4 * (nxt[1] - 1 if nxt else q) + 1, pe_waited)
                        gs_total(2 * k, 1 - s)
                gs_total(2 * k + 1, 1 - s)

            pe.wait_ge(gs_made, 1)
            block_ops(0, (0, 0, 0), (1, 0, 0))
            pe.wait_ge(w_lo_set, J)
            with pe.Fori(0, PAIRS - 1) as q:
                block_ops(4 * q + 1, (1, q, 0), (0, q, 1))
                block_ops(4 * q + 2, (0, q, 1), (1, q, 1))
                block_ops(4 * q + 3, (1, q, 1), (0, q + 1, 0))
                block_ops(4 * q + 4, (0, q + 1, 0), (1, q + 1, 0))
            last = PAIRS - 1
            block_ops(4 * last + 1, (1, last, 0), (0, last, 1))
            block_ops(4 * last + 2, (0, last, 1), (1, last, 1))
            block_ops(4 * last + 3, (1, last, 1), None)


class Ring:

    def __init__(self, start, names, per_round):
        self.at = {name: ((start + k) % 2, (start + k) // 2) for k, name in enumerate(names)}
        self.per_round = per_round

    def bank(self, name):
        return self.at[name][0]

    def full(self, name, n=0):
        return n * self.per_round + self.at[name][1] + 1

    def free(self, name, n=0):
        return n * self.per_round + self.at[name][1]


def before_names(s):
    return ([(s, "p")] + [(s, "resp", j) for j in range(J)] + [(s, "tin", t) for t in range(T)]
            + [(s, "tback", j) for j in range(J)] + [(s, n, g) for g in range(2) for n in "qk"])


def front_names(s, previous, ahead):
    qk = lambda g: [(s, "q", g), (s, "k", g)]
    p, resp, tin = (before_names(1 - s)[a:e] if ahead else [] for a, e in ((0, 1), (1, 1 + J), (1 + J, 1 + J + T)))
    wo = [(1 - s, "wo", j) for j in range(J) if previous]
    return qk(2) + [(s, "v", t) for t in range(T)] + qk(3) + p + resp + wo[:J // 2] + tin + wo[J // 2:]


def back_names(s):
    return before_names(1 - s)[1 + J + T:]


U_TILES = ((T - 1,), (T - 2, 0), (1,))
UNITS = HG * len(U_TILES)
ROWS_AT, EXP_AT = 1, 6
EXP_STEPS = 2 * T
LAST_AT = 3
S_NAMES = [n for g in range(G + 1) for n in
           [(g, u) for u in range(ROWS_AT + 1) if g < G] + [(g - 1, UNITS)] * (g > 0)
           + [(g, u) for u in range(ROWS_AT + 1, UNITS) if g < G]]

STACK_AT = {(0, 0): (0, 0), (0, 1): (1, 0), (0, 2): (2, 0), (0, 3): (0, 1),
            (1, 0): (1, 1), (1, 1): (0, 2), (1, 2): (2, 1), (1, 3): (1, 2)}
STACK_USES = (3, 3, 2)
STACK_DMAS = (12, 12, 13)


AFTER = 2


def stack_count(i, s, g):
    place, use = STACK_AT[s, g]
    return 16 * STACK_DMAS[place] * (STACK_USES[place] * i + use + 1)


def attention_phase(nc, io, keep, psum):
    smalls, ident, pb, pooled = keep["smalls"], keep["ident"], keep["pb"], keep["pooled"]
    with ExitStack() as ctx:
        def sb(name, shape, dt=F32):
            return ctx.enter_context(nc.sbuf_tensor("b_" + name, shape, dt))

        def sem(name):
            return ctx.enter_context(nc.semaphore("b_" + name))

        w_hi, w_lo = ({n: keep["weights"][:, 2 * k + part, :, :] for k, n in enumerate(("wq", "wk", "wv"))}
                      for part in range(2))
        w_hi["wo"], w_lo["wo"] = sb("wo_hi", [P, J, D], F32R), sb("wo_lo", [P, J, D], F32R)
        xb = [keep["result"], keep["tokens"], keep["samples"][:, 0, :, :]]
        tok = keep["samples"][:, 1, :, :]
        tok_at = (tok, tok, keep["tokens"])
        scaled = lambda s, j: tok_at[s][:, :, j * P:(j + 1) * P]
        by_tile = lambda a: a.rearrange("p (t k) -> p t k", t=T)
        xhl = keep["normed"]
        xh, xl = xhl[:, 0:J, :], xhl[:, J:2 * J, :]
        v = sb("v", [P, T, D])
        qk4 = [keep["samples"][:, 0, :, :], tok]
        stack = keep["stack"] + [xhl]
        pt = [sb(f"pt{n}", [P, HG, S]) for n in range(2)]
        wo_raw = pt[1]
        ctxs = sb("ctxs", [P, S])
        sums = sb("sums", [P, S])
        ch = sb("ch", [P, G + 1, S], F32R)
        cl = sb("cl", [P, G + 1, S], F32R)
        w1_hi = [stack[n // 2][:, HG * (n % 2):HG * (n % 2 + 1), :].rearrange("p h t -> p (h t)") for n in range(J)]
        w1_raw, w1_lo = ([keep[k][:, n, :, :].rearrange("p j d -> p (j d)") for n in range(J)] for k in ("raw", "weights"))
        context_at = lambda s, g: G if (s, g) == (1, 0) else g
        psb = sb("p", [R + 1, S])
        mr = [sb(f"mr{n}", [2 * HG, S], F32R) for n in range(2)]
        mask = sb("mask", [P, S])
        mx = [sb(f"mx{n}", [P, T, HG]) for n in range(2)]
        nm = sb("nm", [P, T, HG, 2], F32R)
        st = sb("st", [P, T, 6])
        mv = sb("mv", [P, T, 2])
        var = sb("var", [P, T])
        rstd = sb("rstd", [P, T])
        cur = [sb(f"cur{s}", [P, N_PB]) for s in range(2)]
        gate_w1 = ctxs[:].rearrange("p (j k) -> p j k", j=J)
        gate_h = sb("gate_h", [P, B])
        gate_w2 = sums[:, 0:P]
        strength = sb("strength", [P, B])
        mod = sb("mod", [P, B])
        rbias = tok[R:R + 1, 0, :]
        v_o = tok[:, 1, 0:J * R].rearrange("p (j r) -> p j r", j=J)
        u_head, gram, mix = (tok[0:R, 2, n * R:(n + 1) * R] for n in range(3))
        resp_w = tok[0:R, 3, :]
        bias = tuple(small(smalls, n) for n in ("bq", "bk", "bv"))

        wo_ld, mid_set = sem("wo_ld"), sem("mid_set")
        gw_ld = sem("gw_ld")
        w_hi_set, w_lo_set = sem("w_hi_set"), sem("w_lo_set")
        gate_full, gate_act, gate_dve = sem("gate_full"), sem("gate_act"), sem("gate_dve")
        rows_made, mask_made = sem("rows_made"), sem("mask_made")
        x_ld = [sem(f"x_ld{s}") for s in range(2)]
        x2_st = [sem(f"x2_st{s}") for s in range(2)]
        d_st = keep["d_st"]
        row_ld = sem("row_ld")
        u_set, steer_full, steer_dve = sem("u_set"), sem("steer_full"), sem("steer_dve")
        pj_full = [sem(f"pj_full{k}") for k in range(2)]
        pj_free = [sem(f"pj_free{k}") for k in range(2)]
        s_full = [sem(f"s_full{k}") for k in range(2)]
        s_free = [sem(f"s_free{k}") for k in range(2)]
        e_full = [sem(f"e_full{k}") for k in range(2)]
        e_free = [sem(f"e_free{k}") for k in range(2)]
        cur_set = sem("cur_set")
        stat_set, mv_set = sem("stat_set"), sem("mv_set")
        var_set, rstd_set, normed = sem("var_set"), sem("rstd_set"), sem("normed")
        xh_set, xl_set, qk_hi = sem("xh_set"), sem("xl_set"), sem("qk_hi")
        stack_ld = [sem(f"stack_ld{n}") for n in range(3)]
        nm_hi, nm_lo, mr_set = sem("nm_hi"), sem("nm_lo"), sem("mr_set")
        mr_ld = [sem(f"mr_ld{n}") for n in range(4)]
        masked, pv_done, ctx_free = sem("masked"), sem("pv_done"), sem("ctx_free")
        rec_set, ctxn_set, ch_set, cl_set = sem("rec_set"), sem("ctxn_set"), sem("ch_set"), sem("cl_set")
        waited = {e: sem("waited_" + e) for e in ("dve", "act", "pool", "pe", "sp")}

        pj = lambda k: psum[:, k, :]
        sc = lambda k: psum[:, 2 + k, :]
        ex = lambda k: psum[:, 4 + k, :]
        ctx_bank, sum_bank = psum[:, 6, :], psum[:, 7, :]

        first = before_names(0) + front_names(0, False, True)
        lead = len(first)
        round_names = back_names(0) + front_names(1, True, True) + back_names(1) + front_names(0, True, True)
        last_names = back_names(0) + front_names(1, True, False) + [
            (AFTER, n, t) for n in ("tin", "tback") for t in range(T)] + [(1, "wo", j) for j in range(J)]
        per_round = len(round_names) // 2
        prologue = Ring(0, first, 0)
        steady = Ring(lead, round_names, per_round)
        final = Ring(lead, last_names, per_round)
        s_ring = Ring(0, S_NAMES, len(S_NAMES) // 2)
        e_ring = Ring(0, [(g, j, h) for g in range(G) for j in range(T) for h in range(HG)], G * T * HG // 2)

        def wait_freed(eng, name, ring, i, use):
            wait_apart(eng, pj_free[ring.bank(use)], ring.full(use, i), waited[name])

        def wait_before(eng, name, ring, i, use):
            wait_apart(eng, pj_free[ring.bank(use)], ring.free(use, i), waited[name])

        def exp_heads(half):
            return range(HG // 2 * half, HG // 2 * (half + 1))

        block = ctx.enter_context(nc.Block())

        @block.sync
        def _(sp):
            sp.dma_start(gate_w1, io["gate_w1"]).then_inc(gw_ld, 16)
            sp.dma_start(xb[0][:], sample_at(io["x1"], 0)).then_inc(x_ld[0], 16)
            sp.dma_start(resp_w, io["resp_w"]).then_inc(row_ld, 16)
            sp.dma_start(rbias, io["resp_b_row"]).then_inc(row_ld, 16)
            sp.dma_start(keep["steer"][R:R + 1, :, :], io["safety_bias_row"]).then_inc(row_ld, 16)
            sp.dma_start(wo_raw[:], io["wo"]).then_inc(wo_ld, 16)
            sp.sem_inc(d_st[0], 16)
            sp.sem_inc(d_st[1], 16)

            def stack_rows(ring, i, s, g):
                for n in "qk":
                    wait_freed(sp, "sp", ring, i, (s, n, g))
                place = STACK_AT[s, g][0]
                for h in range(HG):
                    for row, (a, step) in enumerate(((1, 1), (0, 2), (1, 2))):
                        sp.dma_start(stack[place][row * DH:(row + 1) * DH, 2 * h:2 * h + 2, :].bitcast(F32),
                                     qk4[g % 2][h * DH:(h + 1) * DH, a:a + step + 1:step, :]
                                     ).then_inc(stack_ld[place], 16)

            def max_rows(s, g, b):
                place = STACK_AT[s, g][0]
                wait_apart(sp, mr_set, G * b + g + 1, waited["sp"])
                for h in range(HG):
                    sp.dma_start(stack[place][3 * DH:3 * DH + 2, 2 * h, :].bitcast(F32),
                                 mr[g % 2][2 * h:2 * h + 2, :].bitcast(F32)).then_inc(mr_ld[2 * (g % 2) + h // 2], 16)

            def steered_out(ring, n, i, s):
                for t in range(2):
                    wait_before(sp, "sp", ring, n, (s, "tin", t))
                sp.dma_start(sample_at(io["x2"], 2 * i + s), xb[s][:]).then_inc(x2_st[s], 16)

            def attention_out(ring, n, i, s):
                for j in (J - 2, J - 1):
                    wait_freed(sp, "sp", ring, n, (s, "wo", j))
                sp.dma_start(sample_at(io["d"], 2 * i + s), xb[1 - s][:]).then_inc(d_st[1 - s], 16)

            def sample_ahead(i):
                for g in (2, 3):
                    sp.wait_ge(stack_ld[STACK_AT[1, g][0]], stack_count(i, 1, g))
                sp.wait_ge(x2_st[0], 16)
                sp.dma_start(keep["samples"][:, 0, :, :], sample_at(io["x2"], 0)).then_inc(keep["sample_ld"], 16)
                sp.wait_ge(d_st[1], 32)
                sp.dma_start(keep["samples"][:, 1, :, :], sample_at(io["d"], 0)).then_inc(keep["sample_ld"], 16)

            def front(ring, n, i, s, previous, ahead):
                b = 2 * i + s
                if ahead:
                    wait_apart(sp, d_st[1 - s], 16 * (i + 1), waited["sp"])
                    sp.dma_start(xb[1 - s][:], sample_at(io["x1"], b + 1)).then_inc(x_ld[1 - s], 16)
                if previous:
                    for k in range(2):
                        wait_apart(sp, e_full[k], e_ring.full((G - 1, T - 1, HG - 2 + k), b - 1), waited["sp"])
                    stack_rows(ring, n, s, 1)
                max_rows(s, 0, b)
                wait_apart(sp, pj_full[ring.bank((s, "k", 3))], ring.full((s, "k", 3), n), waited["sp"])
                sp.dma_start(xhl[3 * DH:3 * DH + 2, 1::2, :].bitcast(F32),
                             stack[0][3 * DH:3 * DH + 2, 1::2, :].bitcast(F32)).then_inc(stack_ld[2], 16)
                stack_rows(ring, n, s, 2)
                max_rows(s, 1, b)
                for k in range(2):
                    wait_apart(sp, e_full[k], e_ring.full((0, T - 1, HG - 2 + k), b), waited["sp"])
                stack_rows(ring, n, s, 3)
                if ahead:
                    steered_out(ring, n, i + s, 1 - s)
                max_rows(s, 2, b)
                if not ahead:
                    sample_ahead(i)
                if previous:
                    attention_out(ring, n, i - 1 + s, 1 - s)

            def back(ring, n, i, s, ahead):
                max_rows(s, 3, 2 * i + s)
                if ahead:
                    stack_rows(ring, n, 1 - s, 0)

            def w_ahead(n):
                src = io["w1"][:, n, :] if n < J else io["w2"][:, (n - J) * (M // J):(n - J + 1) * (M // J), :].rearrange("p m d -> p (m d)")
                return keep["raw"][:, n, :, :].rearrange("p j d -> p (j d)"), src

            steered_out(prologue, 0, 0, 0)
            for g in range(2):
                stack_rows(prologue, 0, 0, g)
            front(prologue, 0, 0, 0, False, True)
            with sp.Fori(0, PAIRS - 1) as i:
                back(steady, i, i, 0, True)
                front(steady, i, i, 1, True, True)
                back(steady, i, i, 1, True)
                front(steady, i, i + 1, 0, True, True)
            last = PAIRS - 1
            back(final, last, last, 0, True)
            front(final, last, last, 1, True, False)
            back(final, last, last, 1, False)
            for n in range(6):
                sp.dma_start(*w_ahead(n)).then_inc(keep["w_ld"][n], 16)
            attention_out(final, last, last, 1)
            for s in range(2):
                sp.wait_ge(x2_st[s], 16 * PAIRS)

        @block.gpsimd
        def _(pool):
            pool.memset(mask[:], 0.0).then_inc(mask_made, 1)
            pool.wait_ge(mask_made, 1)
            pool.affine_select(out=mask[:, S - P:S], in_=mask[:, S - P:S], compare_op=ALU.is_ge, fill=MASKED, base=0,
                               pattern=[[-1, P]], channel_multiplier=1).then_inc(mask_made, 1)

            def prepare_rstd(b):
                wait_apart(pool, mv_set, T * (b + 1), waited["pool"])
                pool.tensor_scalar(var[:], mv[:, :, 1], LN_EPS, None, ALU.add).then_inc(var_set, 1)
                wait_apart(pool, var_set, b + 1, waited["pool"])
                pool.tensor_tensor(rstd[:], var[:], keep["minus_half"][:], ALU.pow).then_inc(rstd_set, 1)

            def masks(g, j, b):
                for k in range(2):
                    wait_apart(pool, e_free[k], e_ring.full((g, j, HG - 2 + k), b) + 1, waited["pool"])
                pool.affine_select(out=pt[j % 2][:, :, 0:P], in_=pt[j % 2][:, :, 0:P], compare_op=ALU.is_ge, fill=0.0,
                                   base=0, pattern=[[0, HG], [1, P]], channel_multiplier=-1).then_inc(masked, 1)

            def groups(b, which, ahead):
                for g in which:
                    for j in range(T):
                        masks(g, j, b)
                        if ahead and (g, j) == (1, T - 1):
                            prepare_rstd(b + 1)

            prepare_rstd(0)
            with pool.Fori(0, B - 1) as b:
                groups(b, range(G), True)
            groups(B - 1, range(G - 1), False)
            prepare_rstd(B)
            groups(B - 1, (G - 1,), False)

        @block.vector
        def _(dve):
            dve.reciprocal(keep["gs_norm"][:], keep["gs_norm"][:]).then_inc(u_set, 1)
            dve.wait_ge(u_set, 1)
            dve.tensor_tensor(v_o, keep["gs_q"][:, 1, :, :], keep["gs_norm"][:, 1:2, :].to_broadcast([P, J, R]), ALU.mult)
            dve.tensor_tensor(keep["uo"][:], keep["gs_q"][:, 0, :, :], keep["gs_norm"][:, 0:1, :].to_broadcast([P, J, R]),
                              ALU.mult).then_inc(u_set, 1)
            dve.wait_ge(steer_full, 1)
            dve.tensor_copy(u_head.rearrange("r (k j) -> r j k", j=J),
                            psum[0:R, 2, :].rearrange("r (j k) -> r j k", j=J)[:, :, 0:R // J])
            dve.tensor_copy(gram, psum[0:R, 3, 0:R]).then_inc(steer_dve, 1)
            dve.wait_ge(steer_full, 2)
            dve.tensor_copy(mix, psum[0:R, 4, 0:R]).then_inc(steer_dve, 1)
            dve.wait_ge(steer_full, 3)
            dve.tensor_copy(keep["steer"][0:R, :, :].rearrange("r j k -> r (j k)"), psum[0:R, 7, :]).then_inc(steer_dve, 1)
            dve.tensor_scalar(gate_w2, ident[:], 0.0, small(smalls, "gate_w2"), ALU.mult, ALU.add).then_inc(gate_dve, 1)
            dve.wait_ge(row_ld, 48)
            dve.tensor_tensor(keep["steer"][R:R + 1, :, :].rearrange("r j k -> r (j k)"), rbias,
                              keep["steer"][R:R + 1, :, :].rearrange("r j k -> r (j k)"), ALU.add).then_inc(gate_dve, 1)
            dve.memset(psb[R:R + 1, :], 1.0).then_inc(rows_made, 1)
            dve.wait_ge(gate_act, 3)
            dve.tensor_tensor(strength[:], strength[:], mod[:], ALU.mult).then_inc(gate_dve, 1)
            dve.wait_ge(gate_dve, 3)
            dve.tensor_copy(pb[:, :, STRENGTH], strength[:])
            for j in range(J):
                dve.tensor_scalar(pb[:, :, GB2 + j], small(smalls, "gate"), small(smalls, "b2", j), None, ALU.mult)
            dve.tensor_copy(pb[:, :, GATE], small(smalls, "gate"))
            dve.tensor_scalar(pb[:, :, GATE_1], small(smalls, "gate"), -1.0, None, ALU.add).then_inc(gate_dve, 1)
            for n in range(2):
                dve.memset(stack[n][3 * DH:3 * DH + 2, 1::2, :].bitcast(F32), 1.0).then_inc(rows_made, 1)
            dve.wait_ge(gate_dve, 4)
            for k in range(2):
                dve.sem_inc(s_free[k], 1)

            def wo_low():
                for j in range(J):
                    dve.wait_ge(w_hi_set, j + 1)
                    dve.tensor_tensor(w_lo["wo"][:, j, :], wo_raw[:, j, :], w_hi["wo"][:, j, :].bitcast(F32),
                                      ALU.subtract).then_inc(w_lo_set, 1)

            def prepare_scalars(s, b):
                dve.tensor_copy(cur[s][:], pb[:, bass.ds(b, 1), :].rearrange("p b n -> p (b n)")).then_inc(cur_set, 1)

            def prepare_stats(ring, i, s, b, t):
                wait_freed(dve, "dve", ring, i, (s, "tin", t))
                dve.bn_stats(st[:, t, :], tok_at[s][:, t, :]).then_inc(stat_set, 1)
                wait_apart(dve, stat_set, T * b + t + 1, waited["dve"])
                dve.bn_aggr(mv[:, t, :], st[:, t, :]).then_inc(mv_set, 1)

            def prepare_steer(ring, i, s, b, j):
                k = ring.bank((s, "resp", j))
                if j == 0:
                    wait_apart(dve, cur_set, b + 1, waited["dve"])
                wait_apart(dve, pj_full[k], ring.full((s, "resp", j), i), waited["dve"])
                dve.scalar_tensor_tensor(xb[s][:, j, :], pj(k), cur[s][:, STRENGTH:STRENGTH + 1], xb[s][:, j, :], ALU.mult,
                                         ALU.add).then_inc(pj_free[k], 1)

            def prepare_norm(s, b, t):
                if t == 0:
                    wait_apart(dve, rstd_set, b + 1, waited["dve"])
                dve.tensor_scalar(tok_at[s][:, t, :], tok_at[s][:, t, :], mv[:, t, 0:1], rstd[:, t:t + 1], ALU.subtract,
                                  ALU.mult).then_inc(normed, 1)

            def split(ring, i, s, b, j):
                wait_freed(dve, "dve", ring, i, (s, "tback", j))
                dve.tensor_copy(by_tile(xh[:, j, :]), scaled(s, j)).then_inc(xh_set, 1)
                dve.wait_ge(xh_set, J * b + j + 1)
                dve.tensor_tensor(by_tile(xl[:, j, :]), scaled(s, j), by_tile(xh[:, j, :].bitcast(F32)), ALU.subtract).then_inc(xl_set, 1)

            def qk_low(ring, i, s, b, g, n):
                k = ring.bank((s, "qk"[n], g))
                wait_apart(dve, qk_hi, 8 * b + 2 * g + n + 1, waited["dve"])
                dve.scalar_tensor_tensor(qk4[g % 2][:, 3 * n, :].bitcast(F32R), pj(k), bias[n][:, g:g + 1],
                                         qk4[g % 2][:, 1 + n, :], ALU.add, ALU.subtract).then_inc(pj_free[k], 1)

            def max_unit(g, u, b):
                h, tiles = u // len(U_TILES), U_TILES[u % len(U_TILES)]
                k = s_ring.bank((g, u))
                wait_apart(dve, s_full[k], s_ring.full((g, u), b), waited["dve"])
                at = 0
                for t in tiles:
                    width = P * (t + 1)
                    got = sc(k)[:, at:at + width]
                    last = dve.tensor_tensor_reduce(got, got, mask[:, S - width:S], 1.0, 2.0 * MASKED, ALU.add, ALU.max,
                                                    mx[g % 2][:, t, h:h + 1])
                    at += width
                last.then_inc(s_free[k], 1)

            def minus_max(g, b):
                for u in (UNITS - 2, UNITS - 1):
                    wait_apart(dve, s_free[s_ring.bank((g, u))], s_ring.full((g, u), b) + 1, waited["dve"])
                dve.tensor_scalar(nm[:, :, :, 0], mx[g % 2][:], -1.0, None, ALU.mult).then_inc(nm_hi, 1)
                dve.wait_ge(nm_hi, G * b + g + 1)
                dve.scalar_tensor_tensor(nm[:, :, :, 1], mx[g % 2][:], -1.0, nm[:, :, :, 0].bitcast(F32), ALU.mult,
                                         ALU.subtract).then_inc(nm_lo, 1)

            def over_sums(g, c, b):
                if c == 0:
                    dve.wait_ge(ctx_free, 1 + G * b + g + 1)
                part = sums[:, c * P:(c + 1) * P]
                dve.reciprocal(part, part).then_inc(rec_set, 1)
                if c == T - 1:
                    dve.wait_ge(rec_set, T * (G * b + g + 1))
                    dve.tensor_tensor(ctxs[:], ctxs[:], sums[:], ALU.mult).then_inc(ctxn_set, 1)

            def ctx_low(s, g, b):
                at = context_at(s, g)
                dve.wait_ge(ch_set, G * b + g + 1)
                dve.scalar_tensor_tensor(cl[:, at, :], ctxs[:], bias[2][:, g:g + 1], ch[:, at, :].bitcast(F32), ALU.add,
                                         ALU.subtract).then_inc(cl_set, 1)

            def front(ring, n, i, s, previous, ahead):
                b = 2 * i + s
                for m in range(2):
                    qk_low(ring, n, s, b, 2, m)
                for u in range(UNITS):
                    max_unit(0, u, b)
                    if previous and 2 <= u < 2 + T:
                        over_sums(G - 1, u - 2, b - 1)
                minus_max(0, b)
                if previous:
                    ctx_low(1 - s, G - 1, b - 1)
                if ahead:
                    prepare_scalars(1 - s, b + 1)
                for u in range(UNITS):
                    max_unit(1, u, b)
                    if u in (3, 5):
                        qk_low(ring, n, s, b, 3, (u - 3) // 2)
                    if ahead and u >= UNITS - J + 1:
                        prepare_steer(ring, n, 1 - s, b + 1, u - (UNITS - J + 1))
                minus_max(1, b)
                if ahead:
                    prepare_steer(ring, n, 1 - s, b + 1, J - 1)
                for u in range(UNITS):
                    max_unit(2, u, b)
                    if 6 <= u < 6 + T:
                        over_sums(0, u - 6, b)
                    if ahead and u >= 10:
                        prepare_stats(ring, n, 1 - s, b + 1, u - 10)
                minus_max(2, b)
                ctx_low(s, 0, b)
                for u in range(UNITS):
                    max_unit(3, u, b)
                    if ahead and u < 2:
                        prepare_stats(ring, n, 1 - s, b + 1, 2 + u)
                    if ahead and u in (4, 5):
                        for t in (2 * u - 8, 2 * u - 7):
                            prepare_norm(1 - s, b + 1, t)
                    if 6 <= u < 6 + T:
                        over_sums(1, u - 6, b)
                minus_max(3, b)
                ctx_low(s, 1, b)

            def back(ring, n, i, s, ahead):
                b = 2 * i + s
                if ahead:
                    for j in range(J):
                        split(ring, n, 1 - s, b + 1, j)
                else:
                    dve.wait_ge(keep["sample_ld"], 32)
                    for j in range(J):
                        dve.tensor_tensor(xb[AFTER][:, j, :], xb[AFTER][:, j, :], keep["samples"][:, 1, j, :],
                                          ALU.add).then_inc(mid_set, 1)
                    for t in range(T):
                        prepare_stats(ring, n, AFTER, B, t)
                for c in range(T):
                    over_sums(2, c, b)
                if not ahead:
                    for t in range(T):
                        prepare_norm(AFTER, B, t)
                if ahead:
                    for m in range(2):
                        qk_low(ring, n, 1 - s, b + 1, 0, m)
                ctx_low(s, 2, b)
                if ahead:
                    for m in range(2):
                        qk_low(ring, n, 1 - s, b + 1, 1, m)

            prepare_scalars(0, 0)
            for j in range(J):
                prepare_steer(prologue, 0, 0, 0, j)
            for t in range(T):
                prepare_stats(prologue, 0, 0, 0, t)
            for t in range(T):
                prepare_norm(0, 0, t)
            for j in range(J):
                split(prologue, 0, 0, 0, j)
            for g in range(2):
                for n in range(2):
                    qk_low(prologue, 0, 0, 0, g, n)
            wo_low()
            dve.wait_ge(mask_made, 2)
            front(prologue, 0, 0, 0, False, True)
            with dve.Fori(0, PAIRS - 1) as i:
                back(steady, i, i, 0, True)
                front(steady, i, i, 1, True, True)
                back(steady, i, i, 1, True)
                front(steady, i, i + 1, 0, True, True)
            last = PAIRS - 1
            back(final, last, last, 0, True)
            front(final, last, last, 1, True, False)
            back(final, last, last, 1, False)
            for j in range(J):
                split(final, last, AFTER, B, j)
            for c in range(T):
                over_sums(G - 1, c, B - 1)
            ctx_low(1, G - 1, B - 1)
            for n in range(J):
                dve.wait_ge(w_hi_set, J + n + 1)
                dve.tensor_tensor(w1_lo[n], w1_raw[n], w1_hi[n].bitcast(F32), ALU.subtract).then_inc(w_lo_set, 1)

        @block.scalar
        def _(act):
            act.activation(mod[:], small(smalls, "safety"), ACT.Sigmoid).then_inc(gate_act, 1)
            act.wait_ge(gate_full, 1)
            act.activation(gate_h[:], psum[:, 5, 0:B], ACT.Relu, bias=small(smalls, "gate_b1"), scale=1.0 / S).then_inc(gate_act, 1)
            act.wait_ge(gate_full, 2)
            act.activation(strength[:], psum[:, 6, 0:B], ACT.Sigmoid, bias=small(smalls, "gate_b2")).then_inc(gate_act, 1)
            for k in range(2):
                act.sem_inc(e_free[k], 1)
            act.sem_inc(ctx_free, 1)

            def wo_high():
                act.wait_ge(wo_ld, 16)
                for j in range(J):
                    act.activation(w_hi["wo"][:, j, :], wo_raw[:, j, :], ACT.Copy).then_inc(w_hi_set, 1)

            def prepare_p(ring, i, s):
                k = ring.bank((s, "p"))
                act.wait_ge(pj_full[k], ring.full((s, "p"), i))
                act.activation(psb[0:R, :], pj(k)[0:R, :], ACT.Copy).then_inc(pj_free[k], 1)

            def prepare_tokens(ring, i, s, t, stacked):
                k = ring.bank((s, "tin", t))
                if stacked and t == 0:
                    act.wait_ge(stack_ld[stacked[0]], stacked[1])
                act.wait_ge(pj_full[k], ring.full((s, "tin", t), i))
                act.activation(tok_at[s][:, t, :], pj(k), ACT.Copy).then_inc(pj_free[k], 1)

            def scale_shift(ring, i, s, j):
                gamma, beta = ("gamma1", "beta1") if s != AFTER else ("gamma2", "beta2")
                k = ring.bank((s, "tback", j))
                act.wait_ge(pj_full[k], ring.full((s, "tback", j), i))
                act.activation(scaled(s, j), by_tile(pj(k)), ACT.Identity, bias=small(smalls, beta, j),
                               scale=small(smalls, gamma, j)).then_inc(pj_free[k], 1)

            def qk_high(ring, i, s, g, n, stacked):
                name = (s, "qk"[n], g)
                k = ring.bank(name)
                if stacked:
                    act.wait_ge(stack_ld[stacked[0]], stacked[1])
                act.wait_ge(pj_full[k], ring.full(name, i))
                act.activation(qk4[g % 2][:, 1 + n, :].bitcast(F32R), pj(k), ACT.Identity, bias=bias[n][:, g:g + 1]).then_inc(qk_hi, 1)

            def exponentials(g, j, half, b):
                width = S - P * j
                if T * g + j >= 2 and half == 0:
                    act.wait_ge(pv_done, G * T * b + T * g + j - 1)
                for h in exp_heads(half):
                    k = e_ring.bank((g, j, h))
                    act.wait_ge(e_full[k], e_ring.full((g, j, h), b))
                    act.activation(pt[j % 2][:, h, 0:width], ex(k)[:, 0:width], ACT.Exp,
                                   scale=INV_SQRT_DH).then_inc(e_free[k], 1)

            def context(g, b):
                if g:
                    act.wait_ge(cl_set, G * b + g)
                act.wait_ge(pv_done, G * T * b + T * (g + 1))
                act.activation(sums[:], sum_bank, ACT.Copy)
                act.activation(ctxs[:], ctx_bank, ACT.Copy).then_inc(ctx_free, 1)

            def ctx_high(s, g, b):
                act.wait_ge(ctxn_set, G * b + g + 1)
                act.activation(ch[:, context_at(s, g), :], ctxs[:], ACT.Identity, bias=bias[2][:, g:g + 1]).then_inc(ch_set, 1)

            def max_rows(g, b):
                k = s_ring.bank((g, UNITS))
                if g >= 2:
                    for half in range(2):
                        act.wait_ge(mr_ld[2 * (g % 2) + half], 64 * b + 32)
                act.wait_ge(s_full[k], s_ring.full((g, UNITS), b))
                act.activation(mr[g % 2][:], sc(k)[0:2 * HG, :], ACT.Copy).then_inc(mr_set, 1)
                act.wait_ge(mr_set, G * b + g + 1)
                act.sem_inc(s_free[k], 1)

            def stacking(i, s, g):
                return STACK_AT[s, g][0], stack_count(i, s, g)

            def attention_result(ring, n, s, j):
                k = ring.bank((s, "wo", j))
                act.wait_ge(pj_full[k], ring.full((s, "wo", j), n))
                act.activation(xb[1 - s][:, j, :], pj(k), ACT.Identity, bias=small(smalls, "bo", j)).then_inc(pj_free[k], 1)

            def steps(g, u, b):
                if u == LAST_AT + 1 and g >= 2:
                    context(g - 2, b)
                if u == 2 and 1 <= g <= G:
                    max_rows(g - 1, b)
                if g >= 2 and u < EXP_AT + EXP_STEPS - UNITS:
                    exponentials(g - 2, T - 1, u, b)
                if 1 <= g <= G and u >= EXP_AT:
                    exponentials(g - 1, (u - EXP_AT) // 2, (u - EXP_AT) % 2, b)

            def front(ring, n, i, s, previous, ahead):
                b = 2 * i + s
                for u in range(LAST_AT + 2):
                    if previous:
                        steps(G + 1, u, b - 1)
                    if u in (2, 4):
                        qk_high(ring, n, s, 2, (u - 2) // 2, stacking(i, s, 0))
                for t in range(T):
                    values_out(ring, n, s, b, t)
                    if previous and t == 2:
                        ctx_high(1 - s, G - 1, b - 1)
                for u in range(UNITS):
                    steps(1, u, b)
                    if u in (2, 4):
                        qk_high(ring, n, s, 3, (u - 2) // 2, stacking(i, s, 1))
                    if ahead and u == 8:
                        prepare_p(ring, n, 1 - s)
                for u in range(UNITS):
                    if previous and u == 4:
                        act.wait_ge(x2_st[s], 16 * (i + 1))
                    if previous and u in (4, 8):
                        attention_result(ring, n, 1 - s, (u - 4) // 4)
                    steps(2, u, b)
                    if ahead and u >= 10:
                        prepare_tokens(ring, n, 1 - s, u - 10, stacking(i, s, 3))
                ctx_high(s, 0, b)
                for u in range(UNITS):
                    if ahead and u < 2:
                        prepare_tokens(ring, n, 1 - s, 2 + u, None)
                    steps(3, u, b)
                    if previous and u in (5, 9):
                        attention_result(ring, n, 1 - s, 2 + (u - 5) // 4)
                ctx_high(s, 1, b)

            def values_out(ring, n, s, b, t):
                k = ring.bank((s, "v", t))
                act.wait_ge(pj_full[k], ring.full((s, "v", t), n))
                act.activation(v[:, t, :], pj(k), ACT.Copy).then_inc(pj_free[k], 1)

            def back(ring, n, i, s, ahead):
                b = 2 * i + s
                for u in range(UNITS):
                    if ahead and 3 <= u < 3 + J:
                        scale_shift(ring, n, 1 - s, u - 3)
                    steps(4, u, b)
                    if not ahead and 2 <= u < 2 + T:
                        if u == 2:
                            act.wait_ge(d_st[1], 16 * (PAIRS + 1))
                        prepare_tokens(ring, n, AFTER, u - 2, None)
                    if ahead and u in (8, 9):
                        qk_high(ring, n, 1 - s, 0, u - 8, stacking(i, s, 2))
                    if ahead and u == 10:
                        qk_high(ring, n, 1 - s, 1, 0, None)
                ctx_high(s, 2, b)
                if ahead:
                    qk_high(ring, n, 1 - s, 1, 1, None)

            prepare_p(prologue, 0, 0)
            for t in range(T):
                prepare_tokens(prologue, 0, 0, t, None)
            for j in range(J):
                scale_shift(prologue, 0, 0, j)
            for g in range(2):
                for n in range(2):
                    qk_high(prologue, 0, 0, g, n, None)
            wo_high()
            front(prologue, 0, 0, 0, False, True)
            with act.Fori(0, PAIRS - 1) as i:
                back(steady, i, i, 0, True)
                front(steady, i, i, 1, True, True)
                back(steady, i, i, 1, True)
                front(steady, i, i + 1, 0, True, True)
            last = PAIRS - 1
            back(final, last, last, 0, True)
            front(final, last, last, 1, True, False)
            back(final, last, last, 1, False)
            for j in range(J):
                scale_shift(final, last, AFTER, j)
            for u in range(LAST_AT + 2):
                steps(G + 1, u, B - 1)
            for k in range(2):
                act.wait_ge(e_full[k], e_ring.full((1, T - 1, HG - 2 + k), B - 1))

            def w1_high(n):
                act.wait_ge(keep["w_ld"][n], 32 if n < 3 else 16)
                act.activation(w1_hi[n], w1_raw[n], ACT.Copy).then_inc(w_hi_set, 1)

            w1_high(0)
            w1_high(1)
            ctx_high(1, G - 1, B - 1)
            w1_high(2)
            w1_high(3)
            act.wait_ge(d_st[0], 16 * PAIRS)
            for j in range(J):
                attention_result(final, last, 1, j)

        @block.tensor
        def _(pe):
            def claim(ring, i, name):
                k = ring.bank(name)
                if ring is not prologue or ring.free(name):
                    wait_apart(pe, pj_free[k], ring.free(name, i), waited["pe"])
                return k

            def prepare_p(ring, n, i, s, j):
                if j == 0:
                    wait_apart(pe, x_ld[s], 16 * (i + 1), waited["pe"])
                    claim(ring, n, (s, "p"))
                k = ring.bank((s, "p"))
                last = pe.matmul(pj(k)[0:R, :], keep["uo"][:, j, :], xb[s][:, j, :], start=(j == 0), stop=(j == J - 1))
                if j == J - 1:
                    last.then_inc(pj_full[k], 1)

            def prepare_steer(ring, i, s, j):
                if j == 0:
                    wait_freed(pe, "pe", ring, i, (s, "p"))
                k = claim(ring, i, (s, "resp", j))
                pe.matmul(pj(k), keep["steer"][:, j, :], psb[:], start=True, stop=True).then_inc(pj_full[k], 1)

            def prepare_tokens(ring, i, s, t):
                if t == 0 and s == AFTER:
                    pe.wait_ge(mid_set, J)
                elif t == 0:
                    wait_before(pe, "pe", ring, i, (s, "tin", 1))
                k = claim(ring, i, (s, "tin", t))
                for j in range(J):
                    last = pe.transpose(pj(k)[:, j * P:(j + 1) * P], xb[s][:, j, t * P:(t + 1) * P], ident[:])
                last.then_inc(pj_full[k], 1)

            def prepare_back(ring, i, s, b, j):
                if j == 0:
                    wait_apart(pe, normed, T * (b + 1), waited["pe"])
                k = claim(ring, i, (s, "tback", j))
                for t in range(T):
                    last = pe.transpose(pj(k)[:, t * P:(t + 1) * P], tok_at[s][:, t, j * P:(j + 1) * P], ident[:])
                last.then_inc(pj_full[k], 1)

            def qk_piece(ring, i, s, b, g, n, j):
                name, w, at = (s, "qk"[n], g), ("wq", "wk")[n], slice(g * P, (g + 1) * P)
                if (g, n) == (0, 0):
                    wait_apart(pe, xl_set, J * b + j + 1, waited["pe"])
                k = claim(ring, i, name) if j == 0 else ring.bank(name)
                last = three_pass(pe, pj(k), [(w_hi[w][:, j, at], w_lo[w][:, j, at], xh[:, j, :], xl[:, j, :])],
                                  start=j == 0, stop=j == J - 1)
                if j == J - 1:
                    last.then_inc(pj_full[k], 1)

            def v_piece(ring, i, s, t, j):
                name, at = (s, "v", t), slice(t * P, (t + 1) * P)
                k = claim(ring, i, name) if j == 0 else ring.bank(name)
                last = three_pass(pe, pj(k), [(xh[:, j, at], xl[:, j, at], w_hi["wv"][:, j, :], w_lo["wv"][:, j, :])],
                                  start=j == 0, stop=j == J - 1)
                if j == J - 1:
                    last.then_inc(pj_full[k], 1)

            def max_unit(i, s, g, u, b):
                h, tiles = u // len(U_TILES), U_TILES[u % len(U_TILES)]
                place = STACK_AT[s, g][0]
                if u == 0:
                    wait_apart(pe, stack_ld[place], stack_count(i, s, g), waited["pe"])
                k = s_ring.bank((g, u))
                wait_apart(pe, s_free[k], s_ring.free((g, u), b) + 1, waited["pe"])
                at = 0
                for t in tiles:
                    width = P * (t + 1)
                    last = pe.matmul(sc(k)[:, at:at + width], stack[place][0:3 * DH, 2 * h, t * P:(t + 1) * P],
                                     stack[place][0:3 * DH, 2 * h + 1, 0:width], start=True, stop=True)
                    at += width
                last.then_inc(s_full[k], 1)

            def max_rows(g, b):
                k = s_ring.bank((g, UNITS))
                wait_apart(pe, nm_lo, G * b + g + 1, waited["pe"])
                wait_apart(pe, s_free[k], s_ring.free((g, UNITS), b) + 1, waited["pe"])
                for t in range(T):
                    last = pe.transpose(sc(k)[0:2 * HG, t * P:(t + 1) * P],
                                        nm[:, t, :, :].rearrange("p h n -> p (h n)").bitcast(F32), ident[:])
                last.then_inc(s_full[k], 1)

            def exp_scores(s, g, j, half, b):
                place = STACK_AT[s, g][0]
                if j == 0:
                    wait_apart(pe, mr_ld[2 * (g % 2) + half], 64 * b + 32 * (g // 2 + 1), waited["pe"])
                width = S - P * j
                for h in exp_heads(half):
                    k = e_ring.bank((g, j, h))
                    wait_apart(pe, e_free[k], e_ring.free((g, j, h), b) + 1, waited["pe"])
                    pe.matmul(ex(k)[:, 0:width], stack[place][0:3 * DH + 2, 2 * h + 1, j * P:(j + 1) * P],
                              stack[place][0:3 * DH + 2, 2 * h, j * P:S], start=True, stop=True).then_inc(e_full[k], 1)

            def values(g, j, b):
                if j == 0:
                    wait_apart(pe, ctx_free, G * b + g + 1, waited["pe"])
                wait_apart(pe, masked, G * T * b + T * g + j + 1, waited["pe"])
                width = S - P * j
                for bank, is_ctx in ((ctx_bank, True), (sum_bank, False)):
                    for h in range(HG):
                        at = slice(h * DH, (h + 1) * DH)
                        lhs = v[:, j, (HG * g + h) * DH:(HG * g + h + 1) * DH] if is_ctx else keep["ones"][:]
                        last = pe.matmul(bank[at, j * P:S], lhs, pt[j % 2][:, h, 0:width], start=(j == 0), stop=(j == T - 1),
                                         tile_position=(0, h * DH))
                last.then_inc(pv_done, 1)

            def wo_piece(ring, n, s, b, jo, g):
                name, at, slot = (s, "wo", jo), slice(jo * P, (jo + 1) * P), context_at(s, g)
                if jo == 0 and g in (0, G - 1):
                    wait_apart(pe, cl_set, G * b + (G - 1 if g == 0 else G), waited["pe"])
                k = claim(ring, n, name) if g == 0 else ring.bank(name)
                last = three_pass(pe, pj(k), [(w_hi["wo"][:, g, at], w_lo["wo"][:, g, at], ch[:, slot, :], cl[:, slot, :])],
                                  start=g == 0, stop=g == G - 1)
                if g == G - 1:
                    last.then_inc(pj_full[k], 1)

            def exp_step(s, g, q, b):
                j, half = q // 2, q % 2
                exp_scores(s, g, j, half, b)
                if half and j:
                    values(g, j - 1, b)

            def steps(s, g, u, b):
                if u == ROWS_AT and 1 <= g <= G:
                    max_rows(g - 1, b)
                if g >= 2 and u < EXP_AT + EXP_STEPS - UNITS:
                    exp_step(s, g - 2, UNITS - EXP_AT + u, b)
                if g >= 2 and u == LAST_AT:
                    values(g - 2, T - 1, b)
                if 1 <= g <= G and u >= EXP_AT:
                    exp_step(s, g - 1, u - EXP_AT, b)

            def front(ring, n, i, s, previous, ahead):
                b = 2 * i + s
                for u in range(LAST_AT + 1):
                    if previous:
                        steps(1 - s, G + 1, u, b - 1)
                    for part in (2 * u, 2 * u + 1):
                        qk_piece(ring, n, s, b, 2, part // J, part % J)
                for u in range(UNITS):
                    max_unit(i, s, 0, u, b)
                    for part in range(T * J * u // UNITS, T * J * (u + 1) // UNITS):
                        v_piece(ring, n, s, part // J, part % J)
                for u in range(UNITS):
                    max_unit(i, s, 1, u, b)
                    steps(s, 1, u, b)
                    if u < J:
                        for part in (2 * u, 2 * u + 1):
                            qk_piece(ring, n, s, b, 3, part // J, part % J)
                    if ahead and J <= u < 2 * J:
                        prepare_p(ring, n, i + s, 1 - s, u - J)
                    if ahead and u >= UNITS - J:
                        prepare_steer(ring, n, 1 - s, u - (UNITS - J))
                for u in range(UNITS):
                    max_unit(i, s, 2, u, b)
                    steps(s, 2, u, b)
                    if previous and u < 2 * G:
                        wo_piece(ring, n, 1 - s, b - 1, u // G, u % G)
                    if ahead and u >= UNITS - T:
                        prepare_tokens(ring, n, 1 - s, u - (UNITS - T))
                for u in range(UNITS):
                    max_unit(i, s, 3, u, b)
                    steps(s, 3, u, b)
                    if previous and u < 2 * G:
                        wo_piece(ring, n, 1 - s, b - 1, 2 + u // G, u % G)

            def back(ring, n, i, s, ahead):
                b = 2 * i + s
                for u in range(UNITS):
                    steps(s, 4, u, b)
                    if not ahead and 2 <= u < 2 + T:
                        prepare_tokens(ring, n, AFTER, u - 2)
                    if ahead and 2 <= u < 2 + J:
                        prepare_back(ring, n, 1 - s, b + 1, u - 2)
                    if ahead and u >= 6:
                        for part in range(3 * (u - 6), min(3 * (u - 5), 4 * J)):
                            qk_piece(ring, n, 1 - s, b + 1, part // (2 * J), part // J % 2, part % J)

            pe.wait_ge(u_set, 2)
            for j in range(J):
                pe.transpose(psum[0:R, 2, j * P:(j + 1) * P], keep["uo"][:, j, :], ident[:])
            for j in range(J):
                last = pe.matmul(psum[0:R, 3, 0:R], v_o[:, j, :], v_o[:, j, :], start=(j == 0), stop=(j == J - 1))
            last.then_inc(steer_full, 1)
            pe.wait_ge(steer_dve, 1)
            pe.matmul(psum[0:R, 4, 0:R], u_head, gram, start=True, stop=True).then_inc(steer_full, 1)
            pe.wait_ge(steer_dve, 2)
            pe.wait_ge(row_ld, 48)
            pe.matmul(psum[0:R, 7, :], mix, resp_w, start=True, stop=True).then_inc(steer_full, 1)
            pe.wait_ge(steer_dve, 3)
            pe.wait_ge(gw_ld, 16)
            for j in range(J):
                last = pe.matmul(psum[:, 5, 0:B], gate_w1[:, j, :], pooled[:, :, j], start=(j == 0), stop=(j == J - 1))
            last.then_inc(gate_full, 1)
            pe.wait_ge(gate_act, 2)
            pe.wait_ge(gate_dve, 1)
            pe.matmul(psum[:, 6, 0:B], gate_w2, gate_h[:], start=True, stop=True).then_inc(gate_full, 1)
            for j in range(J):
                prepare_p(prologue, 0, 0, 0, j)
            pe.wait_ge(rows_made, 1)
            for j in range(J):
                prepare_steer(prologue, 0, 0, j)
            for t in range(T):
                prepare_tokens(prologue, 0, 0, t)
            for j in range(J):
                prepare_back(prologue, 0, 0, 0, j)
            for g in range(2):
                for n in range(2):
                    for j in range(J):
                        qk_piece(prologue, 0, 0, 0, g, n, j)
            pe.wait_ge(rows_made, 3)
            front(prologue, 0, 0, 0, False, True)
            pe.wait_ge(w_lo_set, J)
            with pe.Fori(0, PAIRS - 1) as i:
                back(steady, i, i, 0, True)
                front(steady, i, i, 1, True, True)
                back(steady, i, i, 1, True)
                front(steady, i, i + 1, 0, True, True)
            last = PAIRS - 1
            back(final, last, last, 0, True)
            front(final, last, last, 1, True, False)
            back(final, last, last, 1, False)
            for j in range(J):
                prepare_back(final, last, AFTER, B, j)
            for u in range(LAST_AT + 1):
                steps(1, G + 1, u, B - 1)
            for j in (0, 1):
                for g in range(G - 1):
                    wo_piece(final, last, 1, B - 1, j, g)
            for j in (0, 1):
                wo_piece(final, last, 1, B - 1, j, G - 1)
            for j in (2, 3):
                for g in range(G):
                    wo_piece(final, last, 1, B - 1, j, g)


def feed_forward_phase(nc, io, keep, psum):
    smalls, ident, pb = keep["smalls"], keep["ident"], keep["pb"]
    MID_AT, TIN_AT, BACK_AT = 4, 5, 10
    with ExitStack() as ctx:
        def sb(name, shape, dt=F32):
            return ctx.enter_context(nc.sbuf_tensor("c_" + name, shape, dt))

        def sem(name):
            return ctx.enter_context(nc.semaphore("c_" + name))

        w_hi = [keep["stack"][n // 2][:, HG * (n % 2):HG * (n % 2 + 1), :].rearrange("p h t -> p (h t)") for n in range(J)] + [
            sb(f"w{n}_hi", [P, FF], F32R)[:] for n in range(J, 2 * J)]
        w_lo = [keep["weights"][:, n, :, :].rearrange("p j d -> p (j d)") for n in range(6)] + [
            sb(f"w{n}_lo", [P, FF], F32R)[:] for n in range(6, 2 * J)]
        x = keep["samples"][:, 0, :, :]
        d = keep["samples"][:, 1, :, :]
        tok = keep["tokens"]
        base = keep["result"]
        at = aligned(nc.sbuf_base)
        normed = [keep["normed"], sb("normed1", [P, 2 * J, S], F32R)]
        h_hi, h_lo = ([a[:, J * part:J * (part + 1), :] for a in normed] for part in range(2))
        h_raw = nc.alloc_sbuf_tensor_at("c_raw", [P, 2 * J, S], F32, offset=at)
        act_f = sb("act", [P, S])
        act_hi = [sb(f"act_hi{k}", [P, S], F32R) for k in range(2)]
        act_lo = [sb(f"act_lo{k}", [P, S], F32R) for k in range(2)]
        st = sb("st", [P, T, 6])
        mv = sb("mv", [P, T, 2])
        var = sb("var", [P, T])
        rstd = sb("rstd", [P, T])
        cur = [sb(f"cur{s}", [P, N_PB]) for s in range(2)]

        raw_ld = [(keep["w_ld"][n], 16) for n in range(J, 6)] + [(sem(f"raw_ld{n}"), 16) for n in range(6, 2 * J)]
        w_hi_set, w_lo_set = sem("w_hi_set"), sem("w_lo_set")
        x_ld, d_ld, out_st = sem("x_ld"), sem("d_ld"), sem("out_st")
        mid_set, base_set = sem("mid_set"), sem("base_set")
        cur_set = sem("cur_set")
        tin_full, tok_set, stat_set, mv_set = sem("tin_full"), sem("tok_set"), sem("stat_set"), sem("mv_set")
        var_set, rstd_set, normed, tback_full = sem("var_set"), sem("rstd_set"), sem("normed"), sem("tback_full")
        h_set = sem("h_set")
        h_hi_set, h_lo_set = sem("h_hi_set"), sem("h_lo_set")
        hidden_full, gelu_set, act_hi_set, act_lo_set = sem("hidden_full"), sem("gelu_set"), sem("act_hi_set"), sem("act_lo_set")
        added = sem("added")
        gated, out_set = sem("gated"), sem("out_set")
        waited = {e: sem("waited_" + e) for e in ("dve", "act", "pool", "pe", "sp")}

        hidden = lambda n: psum[:, n % 2, :]
        total = lambda j: psum[:, 2 + j, :]
        turn = lambda n: psum[:, 6 + n % 2, :]
        w_raw = [keep["raw"][:, n, :, :].rearrange("p j d -> p (j d)") for n in range(6)] + [
            h_raw[:, J * n:J * (n + 1), :].rearrange("p j t -> p (j t)") for n in range(2)]

        scaled = lambda j: tok[:, :, j * P:(j + 1) * P]
        by_tile = lambda a: a.rearrange("p (t k) -> p t k", t=T)

        def w2_tile(w, m, jo):
            at = m % (M // J) * D + jo * P
            return w[J + m // (M // J)][:, at:at + P]

        block = ctx.enter_context(nc.Block())

        @block.sync
        def _(sp):
            for n in range(6, 2 * J):
                src = io["w2"][:, (n - J) * (M // J):(n - J + 1) * (M // J), :].rearrange("p m d -> p (m d)")
                sp.dma_start(w_raw[n], src).then_inc(raw_ld[n - J][0], 16)
            for s in range(2):
                sp.wait_ge(keep["d_st"][s], 16 * (PAIRS + 1))
            sp.sem_inc(out_st, 16)

            def load(b):
                sp.dma_start(x, sample_at(io["x2"], b)).then_inc(x_ld, 16)
                sp.dma_start(d, sample_at(io["d"], b)).then_inc(d_ld, 16)

            def sample(b, ahead):
                if ahead:
                    wait_apart(sp, base_set, J * (b + 1), waited["sp"])
                    load(b + 1)
                wait_apart(sp, out_set, J * (b + 1), waited["sp"])
                sp.dma_start(sample_at(io["out"], b), base[:]).then_inc(out_st, 16)

            sp.sem_inc(x_ld, 16)
            sp.sem_inc(d_ld, 16)
            with sp.Fori(0, B - 1) as b:
                sample(b, True)
            sample(B - 1, False)
            sp.wait_ge(out_st, 16 * (B + 1))

        @block.gpsimd
        def _(pool):
            def norm(b):
                wait_apart(pool, mv_set, T * (b + 1), waited["pool"])
                pool.tensor_scalar(var[:], mv[:, :, 1], LN_EPS, None, ALU.add).then_inc(var_set, 1)
                wait_apart(pool, var_set, b + 1, waited["pool"])
                pool.tensor_tensor(rstd[:], var[:], keep["minus_half"][:], ALU.pow).then_inc(rstd_set, 1)

            def sample(i, s, ahead):
                b = 2 * i + s
                if ahead:
                    norm(b + 1)
                for j in range(J):
                    wait_apart(pool, gated, J * b + J + j + 1, waited["pool"])
                    pool.tensor_scalar(base[:, j, :], base[:, j, :], cur[s][:, GB2 + j:GB2 + j + 1], None,
                                       ALU.add).then_inc(out_set, 1)

            pool.sem_inc(var_set, 1)
            pool.sem_inc(rstd_set, 1)
            sample(0, 0, True)
            sample(0, 1, True)
            with pool.Fori(1, PAIRS - 1) as i:
                sample(i, 0, True)
                sample(i, 1, True)
            sample(PAIRS - 1, 0, True)
            sample(PAIRS - 1, 1, False)

        @block.vector
        def _(dve):
            def weight_low(n):
                dve.wait_ge(w_hi_set, n - J + 1)
                dve.tensor_tensor(w_lo[n], w_raw[n], w_hi[n].bitcast(F32), ALU.subtract).then_inc(w_lo_set, 1)

            dve.sem_inc(act_hi_set, 2)
            dve.sem_inc(act_lo_set, 2)
            dve.sem_inc(gated, J)

            def add_attention(b, j):
                if j == 0:
                    wait_apart(dve, x_ld, 16 * (b + 1), waited["dve"])
                    wait_apart(dve, d_ld, 16 * (b + 1), waited["dve"])
                dve.tensor_tensor(x[:, j, :], x[:, j, :], d[:, j, :], ALU.add).then_inc(mid_set, 1)

            def start_result(s, b, j):
                if j == 0:
                    wait_apart(dve, out_st, 16 * (b + 1), waited["dve"])
                    wait_apart(dve, cur_set, b + 1, waited["dve"])
                    wait_apart(dve, mid_set, J * (b + 1), waited["dve"])
                dve.scalar_tensor_tensor(base[:, j, :], d[:, j, :], cur[s][:, GATE_1:GATE_1 + 1], x[:, j, :], ALU.mult,
                                         ALU.add).then_inc(base_set, 1)

            def statistics(b, t):
                dve.wait_ge(tok_set, T * b + t + 1)
                dve.bn_stats(st[:, t, :], tok[:, t, :]).then_inc(stat_set, 1)
                wait_apart(dve, stat_set, T * b + t + 1, waited["dve"])
                dve.bn_aggr(mv[:, t, :], st[:, t, :]).then_inc(mv_set, 1)

            def normalise(b):
                dve.wait_ge(rstd_set, b + 1)
                for t in range(T):
                    dve.tensor_scalar(tok[:, t, :], tok[:, t, :], mv[:, t, 0:1], rstd[:, t:t + 1], ALU.subtract,
                                      ALU.mult).then_inc(normed, 1)

            def norm_low(s, b, j):
                dve.wait_ge(h_hi_set, J * b + j + 1)
                dve.tensor_tensor(by_tile(h_lo[s][:, j, :]), scaled(j), by_tile(h_hi[s][:, j, :].bitcast(F32)),
                                  ALU.subtract).then_inc(h_lo_set, 1)

            def split(b, m):
                n, k = M * b + m, m % 2
                wait_apart(dve, gelu_set, n + 3, waited["dve"])
                wait_apart(dve, added, n + 1, waited["dve"])
                dve.tensor_copy(act_hi[k][:], act_f[:]).then_inc(act_hi_set, 1)
                dve.wait_ge(act_hi_set, n + 3)
                dve.tensor_tensor(act_lo[k][:], act_f[:], act_hi[k][:].bitcast(F32), ALU.subtract).then_inc(act_lo_set, 1)

            def sample(i, s, ahead):
                b = 2 * i + s
                dve.tensor_copy(cur[s][:], pb[:, bass.ds(b, 1), :].rearrange("p b n -> p (b n)")).then_inc(cur_set, 1)
                for m in range(M):
                    if m < M - 1:
                        split(b, m + 1)
                    elif ahead:
                        split(b + 1, 0)
                    if isinstance(b, int) and b == 0 and m < J - 1:
                        weight_low(J + 1 + m)
                    if m == 2:
                        for j in range(J):
                            start_result(s, b, j)
                    if ahead and m == MID_AT:
                        for j in range(J):
                            add_attention(b + 1, j)
                    if ahead and TIN_AT <= m < TIN_AT + T:
                        statistics(b + 1, m - TIN_AT)
                    if ahead and m == TIN_AT + T:
                        normalise(b + 1)
                    if ahead and BACK_AT <= m < BACK_AT + J:
                        norm_low(1 - s, b + 1, m - BACK_AT)
                wait_apart(dve, base_set, J * (b + 1), waited["dve"])
                wait_apart(dve, added, M * (b + 1) + 2, waited["dve"])
                for j in range(J):
                    dve.scalar_tensor_tensor(base[:, j, :], total(j), cur[s][:, GATE:GATE + 1], base[:, j, :], ALU.mult,
                                             ALU.add).then_inc(gated, 1)

            for made in (mid_set, stat_set, mv_set, normed, h_lo_set):
                dve.sem_inc(made, J)
            weight_low(J)
            split(0, 0)
            sample(0, 0, True)
            sample(0, 1, True)
            with dve.Fori(1, PAIRS - 1) as i:
                sample(i, 0, True)
                sample(i, 1, True)
            sample(PAIRS - 1, 0, True)
            sample(PAIRS - 1, 1, False)

        @block.scalar
        def _(act):
            def weight_high(n):
                act.wait_ge(*raw_ld[n - J])
                act.activation(w_hi[n], w_raw[n], ACT.Copy).then_inc(w_hi_set, 1)

            act.sem_inc(gelu_set, 2)

            def tokens(b, t):
                act.wait_ge(tin_full, T * b + t + 1)
                act.activation(tok[:, t, :], turn(t), ACT.Copy).then_inc(tok_set, 1)

            def norm_high(s, b, j):
                act.wait_ge(tback_full, J * b + j + 1)
                act.activation(scaled(j), by_tile(turn(j)), ACT.Identity, bias=small(smalls, "beta2", j),
                               scale=small(smalls, "gamma2", j)).then_inc(h_set, 1)
                act.wait_ge(h_set, J * b + j + 1)
                act.activation(by_tile(h_hi[s][:, j, :]), scaled(j), ACT.Copy).then_inc(h_hi_set, 1)

            def gelu(b, m):
                n = M * b + m
                wait_apart(act, act_lo_set, n + 2, waited["act"])
                act.wait_ge(hidden_full, n + 1)
                act.activation(act_f[:], hidden(m), ACT.Gelu, bias=small(smalls, "b1", m)).then_inc(gelu_set, 1)

            def sample(i, s, ahead):
                b = 2 * i + s
                for m in range(M):
                    if m < M - 1:
                        gelu(b, m + 1)
                    elif ahead:
                        gelu(b + 1, 0)
                    if isinstance(b, int) and b == 0 and m < J - 1:
                        weight_high(J + 1 + m)
                    if ahead and TIN_AT <= m < TIN_AT + T:
                        tokens(b + 1, m - TIN_AT)
                    if ahead and BACK_AT <= m < BACK_AT + J:
                        norm_high(1 - s, b + 1, m - BACK_AT)

            for made in (tok_set, h_set, h_hi_set):
                act.sem_inc(made, J)
            weight_high(J)
            gelu(0, 0)
            sample(0, 0, True)
            sample(0, 1, True)
            with act.Fori(1, PAIRS - 1) as i:
                sample(i, 0, True)
                sample(i, 1, True)
            sample(PAIRS - 1, 0, True)
            sample(PAIRS - 1, 1, False)

        @block.tensor
        def _(pe):
            pe.sem_inc(added, 2)

            def tokens(b, t):
                if t == 0:
                    wait_apart(pe, mid_set, J * (b + 1), waited["pe"])
                if t >= 2:
                    wait_apart(pe, tok_set, T * b + t - 1, waited["pe"])
                for j in range(J):
                    last = pe.transpose(turn(t)[:, j * P:(j + 1) * P], x[:, j, t * P:(t + 1) * P], ident[:])
                last.then_inc(tin_full, 1)

            def back(b, j):
                if j == 0:
                    wait_apart(pe, normed, T * (b + 1), waited["pe"])
                if j >= 2:
                    wait_apart(pe, h_set, J * b + j - 1, waited["pe"])
                for t in range(T):
                    last = pe.transpose(turn(j)[:, t * P:(t + 1) * P], tok[:, t, j * P:(j + 1) * P], ident[:])
                last.then_inc(tback_full, 1)

            def first_product(s, b, m):
                n, at = M * b + m, slice(m * P, (m + 1) * P)
                if m == 0:
                    wait_apart(pe, h_lo_set, J * (b + 1), waited["pe"])
                wait_apart(pe, gelu_set, n + 1, waited["pe"])
                three_pass(pe, hidden(m), [(w_hi[j][:, at], w_lo[j][:, at], h_hi[s][:, j, :], h_lo[s][:, j, :])
                                           for j in range(J)]).then_inc(hidden_full, 1)

            def second_product(b, m):
                n, k = M * b + m, m % 2
                if isinstance(b, int) and b == 0 and m % (M // J) == 0:
                    pe.wait_ge(w_lo_set, m // (M // J) + 1)
                wait_apart(pe, act_lo_set, n + 3, waited["pe"])
                for j in range(J):
                    if m == 0:
                        wait_apart(pe, gated, J * b + j + 1, waited["pe"])
                    last = three_pass(pe, total(j), [(w2_tile(w_hi, m, j), w2_tile(w_lo, m, j), act_hi[k][:], act_lo[k][:])],
                                      start=m == 0, stop=m == M - 1)
                last.then_inc(added, 1)

            def sample(i, s, ahead):
                b = 2 * i + s
                for m in range(M):
                    if m < M - 1:
                        first_product(s, b, m + 1)
                    elif ahead:
                        first_product(1 - s, b + 1, 0)
                    second_product(b, m)
                    if ahead and TIN_AT <= m < TIN_AT + T:
                        tokens(b + 1, m - TIN_AT)
                    if ahead and BACK_AT <= m < BACK_AT + J:
                        back(b + 1, m - BACK_AT)

            pe.sem_inc(tin_full, T)
            pe.sem_inc(tback_full, J)
            first_product(0, 0, 0)
            sample(0, 0, True)
            sample(0, 1, True)
            with pe.Fori(1, PAIRS - 1) as i:
                sample(i, 0, True)
                sample(i, 1, True)
            sample(PAIRS - 1, 0, True)
            sample(PAIRS - 1, 1, False)


def host_arrays(x, condB_theta, condB_phi, condB_t, condB_safetyscore, condB_gatescore, **w):
    def rows_of(a):
        return a.reshape(P, J, *a.shape[1:])

    def cols_of(a):
        return np.moveaxis(a.reshape(*a.shape[:-1], P, J), -1, -2)

    def every(a):
        return np.broadcast_to(a.reshape(1, -1), (P, a.size))

    half = P // 2
    freq = np.exp(np.arange(half, dtype=np.float32) * np.float32(-np.log(10000.0) / (half - 1)))
    shift = np.zeros((P, 5 * B), np.float32)
    shift[half:, 0:B] = shift[:, 2 * B:3 * B] = shift[:, 4 * B:5 * B] = 0.25
    l1, l2, l3 = (lambda n, k=k: w[f"L{k}_cond_{n}"] for k in (1, 2, 3))
    vectors = {
        "t": every(condB_t), "theta": every(condB_theta), "phi": every(condB_phi),
        "safety": every(condB_safetyscore), "gate": every(condB_gatescore),
        "freq": np.concatenate([freq, freq])[:, None], "quarter": shift,
        "half_pi": (shift * np.float32(TWO_PI)).astype(np.float32),
        "t_b1": rows_of(l1("b1")), "t_b2": rows_of(l1("b2")), "b_sc": rows_of(l1("bsc")), "b_sh": rows_of(l1("bsh")),
        "b_in": rows_of(l1("b_in")), "b_out": rows_of(l1("b_out")), "gate_b1": l2("gate_b1")[:, None],
        "gate_w2": l2("gate_w2").T, "gate_b2": every(l2("gate_b2")), "safety_bias": rows_of(l2("safety_bias")),
        "resp_b": rows_of(l2("resp_b")), "bq": l3("bq").reshape(G, P).T, "bk": l3("bk").reshape(G, P).T,
        "bv": l3("bv").reshape(G, P).T, "bo": rows_of(l3("bo")), "b1": l3("b1").reshape(M, P).T, "b2": rows_of(l3("b2")),
        "gamma1": rows_of(l3("gamma1")), "beta1": rows_of(l3("beta1")), "gamma2": rows_of(l3("gamma2")),
        "beta2": rows_of(l3("beta2")),
    }
    arrays = {
        "x": x.reshape(B, S, P, J).transpose(0, 2, 3, 1),
        "smalls": np.concatenate([vectors[n] for n, _ in SMALLS], axis=1),
        "uv": np.stack([rows_of(l2("U")), rows_of(l2("V"))], axis=1),
        "t_w1": cols_of(l1("W1")), "t_w2": rows_of(cols_of(l1("W2"))), "w_sc": rows_of(cols_of(l1("Wsc"))),
        "w_sh": rows_of(cols_of(l1("Wsh"))),
        "w_in": rows_of(l1("W_in").reshape(D, P, J).transpose(0, 2, 1).reshape(D, D)),
        "w_out": rows_of(l1("W_out").reshape(D, P, J).transpose(0, 2, 1).reshape(D, D)),
        "gamma_t": rows_of(l1("gamma").T), "beta_t": rows_of(l1("beta").T),
        "safety_bias_row": cols_of(l2("safety_bias"))[None], "resp_b_row": cols_of(l2("resp_b")).reshape(1, D),
        "resp_w": cols_of(l2("resp_w").T).reshape(R, D), "gate_w1": rows_of(l2("gate_w1").T),
        "wq": rows_of(l3("Wq")), "wk": rows_of(l3("Wk")), "wv": rows_of(l3("Wv")),
        "wo": cols_of(l3("Wo")).reshape(G, P, D).transpose(1, 0, 2),
        "w1": rows_of(l3("W1")), "w2": cols_of(l3("W2")).reshape(M, P, D).transpose(1, 0, 2),
    }
    return {n: np.ascontiguousarray(a) for n, a in arrays.items()}


def build(nc, io):
    with ExitStack() as ctx:
        def sb(name, shape, dt=F32):
            return ctx.enter_context(nc.sbuf_tensor("k_" + name, shape, dt))

        psum = ctx.enter_context(nc.psum_tensor("psum", [P, 8, 512], F32))
        at = aligned(nc.sbuf_base)
        weights = sb("weights", [P, 6, J, D], F32R)
        raw = nc.alloc_sbuf_tensor_at("k_raw", [P, 6, J, D], F32, offset=at)
        keep = {
            "smalls": sb("smalls", [P, N_SMALLS]), "ident": sb("ident", [P, P]), "ones": sb("ones", [P, DH]),
            "minus_half": sb("minus_half", [P, T]), "pb": sb("pb", [P, B, N_PB]),
            "samples": sb("samples", [P, 2, J, S]), "weights": weights, "raw": raw,
            "normed": sb("normed", [P, 2 * J, S], F32R), "tokens": sb("tokens", [P, J, S]), "result": sb("result", [P, J, S]),
            "stack": [sb(f"stack{n}", [P, 2 * HG, S], F32R) for n in range(2)],
            "d_st": [ctx.enter_context(nc.semaphore(f"d_st{n}")) for n in range(2)],
            "ahead": {n: ctx.enter_context(nc.semaphore("ahead_" + n)) for n in ("x0", "x1", "gamma_beta", "uv", "w_out")},
            "sample_ld": ctx.enter_context(nc.semaphore("sample_ld")),
            "w_ld": [ctx.enter_context(nc.semaphore(f"w_ld{n}")) for n in range(6)],
        }
        with ExitStack() as middle:
            for n, shape in (("pa", [P, B, N_PA]), ("pooled", [P, B, J]), ("uo", [P, J, R]), ("steer", [R + 1, J, P]),
                             ("gs_x", [P, 2, J, R]), ("gs_q", [P, 2, J, R]), ("gs_norm", [P, 2, R])):
                keep[n] = middle.enter_context(nc.sbuf_tensor("k_" + n, shape, F32))
            with ExitStack() as first:
                for k, part in enumerate(("hi", "lo")):
                    keep[f"w_in_{part}"] = keep["stack"][1][:, J * k:J * (k + 1), :].rearrange("p j (a k) -> p j a k", a=J)
                    keep[f"w_out_{part}"] = first.enter_context(nc.sbuf_tensor(f"k_w_out_{part}", [P, J, J, P], F32R))
                for n in ("gamma_t", "beta_t"):
                    keep[n] = first.enter_context(nc.sbuf_tensor("k_" + n, [P, J, S], F32))
                setup_phase(nc, io, keep, psum)
                first_phase(nc, io, keep, psum)
            attention_phase(nc, io, keep, psum)
        feed_forward_phase(nc, io, keep, psum)


def kernel(**inputs):
    import concourse.bacc as bacc
    from concourse.bass_utils import run_bass_kernel_spmd

    nc = bacc.Bacc("TRN2", target_bir_lowering=False, num_devices=1)
    arrays = host_arrays(**{n: np.asarray(a) for n, a in inputs.items()})
    io = {n: nc.dram_tensor("in_" + n, a.shape, mybir.dt.from_np(a.dtype), kind="ExternalInput").ap()
          for n, a in arrays.items()}
    shape = (B, P, J, S)
    for n in ("x1", "x2", "d"):
        io[n] = nc.dram_tensor(n, shape, F32, kind="Internal").ap()
    io["out"] = nc.dram_tensor("out", shape, F32, kind="ExternalOutput").ap()
    build(nc, io)
    r = run_bass_kernel_spmd(nc, [{"in_" + n: a for n, a in arrays.items()}], core_ids=[0])
    return r.results[0]["out"].transpose(0, 3, 1, 2).reshape(B, S, D)
```
